# Optimizing a Trainium2 kernel written in Bass

```python
import numpy as np
import jax
import jax.numpy as jnp

def _softmax(x, axis=-1):
    return jax.nn.softmax(x, axis=axis)

def _gelu(x):
    return jax.nn.gelu(x, approximate=True)

def _silu(x):
    return jax.nn.silu(x)

def _sigmoid(x):
    return jax.nn.sigmoid(x)

def _layernorm(x, axis=-1, eps=1e-05):
    m = jnp.mean(x, axis=axis, keepdims=True)
    v = jnp.var(x, axis=axis, keepdims=True)
    return (x - m) / jnp.sqrt(v + eps)

def _scatter_add(tgt, idx, src, axis=0):
    return tgt.at[idx].add(src)

def _segment_sum(src, seg, n):
    return jax.ops.segment_sum(src, seg, n)
kernel_name = 'mk_decoder_preln_d1_seqx_r4_ced4f0'

def setup_inputs(seed: int=0):
    np.random.seed(seed)
    _w = jnp.asarray

    def _rec_inputs():
        import jax
        import jax.numpy as jnp
        _rk = jax.random.key(seed)
        x = 7.22e-05 + 1 * jax.random.normal(jax.random.fold_in(_rk, 1), (4, 512, 512), jnp.float32)
        _lenS = 512 - jax.random.randint(jax.random.fold_in(_rk, 7), (4,), 0, max(1, 512 // 4) + 1, jnp.int32)
        _lenS2 = 512 - jax.random.randint(jax.random.fold_in(_rk, 8), (4,), 0, max(1, 512 // 4) + 1, jnp.int32)
        _ctx_1024P = jax.random.normal(jax.random.fold_in(_rk, 11), (4, 16, 256), jnp.float32)
        _ctx_1024c = jax.random.dirichlet(jax.random.fold_in(_rk, 511), 0.3 * jnp.ones((16,), jnp.float32), (4, 512))
        _ctx_1024t = jnp.einsum('bsk,bkd->bsd', _ctx_1024c, _ctx_1024P)
        _ctx_1024t = _ctx_1024t * jax.lax.rsqrt(jnp.mean(jnp.square(_ctx_1024t)) + 1e-12) * 0.953939
        ctx_1024 = -1.39393e-06 + 0.999914 * (_ctx_1024t + 0.3 * jax.random.normal(jax.random.fold_in(_rk, 611), (4, 512, 256), jnp.float32))
        fside_BxSx2_0 = jax.random.uniform(jax.random.fold_in(_rk, 12), (4, 512, 2), jnp.float32, 0.0, 0.999707)
        return (x, ctx_1024, fside_BxSx2_0)
    x, ctx_1024, fside_BxSx2_0 = _rec_inputs()

    def _L0_attn_setup():
        import jax, jax.numpy as jnp
        import numpy as np
        HIDDEN = 512
        HEADS = 16
        HEAD_DIM = HIDDEN // HEADS
        NEG = -10000000000.0
        key = jax.random.key(seed)
        k1, k2, k3 = jax.random.split(key, 3)
        x = jax.random.normal(k1, (2, 512, HIDDEN), dtype=jnp.float32)
        w_qkv = jax.random.normal(k2, (HIDDEN, 3 * HIDDEN), dtype=jnp.float32) / np.sqrt(HIDDEN)
        w_out = jax.random.normal(k3, (HIDDEN, HIDDEN), dtype=jnp.float32) / np.sqrt(HIDDEN)
        return {'x': x, 'w_qkv': w_qkv, 'w_out': w_out}
    _L0_attn_all = _L0_attn_setup()
    _L0_attn_in = {k: v for k, v in _L0_attn_all.items() if k in ('w_qkv', 'w_out')}
    del _L0_attn_all

    def _L0_xattn_setup():
        import jax, jax.numpy as jnp
        import numpy as np
        DIM = 512
        CTX_DIM = 256
        N_HEADS = 32
        HEAD_DIM = DIM // N_HEADS
        POS_DIM = 2
        B, N, CTXN = (2, 512, 512)
        ROPE_BASE = 10000.0

        def apply_axial_rope(x, pos):
            b, n, h, d = x.shape
            p = pos.shape[-1]
            dpa = d // p
            half = dpa // 2
            freqs = ROPE_BASE ** (-jnp.arange(half, dtype=x.dtype) / half)
            ang = pos[..., :, None] * freqs
            cos = jnp.cos(ang)[:, :, None, :, :]
            sin = jnp.sin(ang)[:, :, None, :, :]
            xr = x.reshape(b, n, h, p, half, 2)
            x1, x2 = (xr[..., 0], xr[..., 1])
            out = jnp.stack([x1 * cos - x2 * sin, x1 * sin + x2 * cos], axis=-1)
            return out.reshape(b, n, h, d)
        key = jax.random.key(seed)
        ks = jax.random.split(key, 8)
        x = jax.random.normal(ks[0], (B, N, DIM), jnp.float32)
        ctx = jax.random.normal(ks[1], (B, CTXN, CTX_DIM), jnp.float32)
        pos_map = jax.random.uniform(ks[2], (B, N, POS_DIM), jnp.float32)
        ctx_pos_map = jax.random.uniform(ks[3], (B, CTXN, POS_DIM), jnp.float32)
        Wq = jax.random.normal(ks[4], (DIM, DIM), jnp.float32) / np.sqrt(DIM)
        Wkv = jax.random.normal(ks[5], (CTX_DIM, 2 * DIM), jnp.float32) / np.sqrt(CTX_DIM)
        Wout = jax.random.normal(ks[6], (DIM, DIM), jnp.float32) / np.sqrt(DIM)
        bout = jnp.zeros((DIM,), jnp.float32)
        return {'x': x, 'ctx': ctx, 'pos_map': pos_map, 'ctx_pos_map': ctx_pos_map, 'Wq': Wq, 'Wkv': Wkv, 'Wout': Wout, 'bout': bout}
    _L0_xattn_all = _L0_xattn_setup()
    _L0_xattn_in = {k: v for k, v in _L0_xattn_all.items() if k in ('Wq', 'Wkv', 'Wout', 'bout')}
    del _L0_xattn_all

    def _L0_ffn_setup():
        import jax, jax.numpy as jnp
        import numpy as np
        HID = 512
        N_HEADS = 16
        N_KV = 16
        HEAD_DIM = HID // N_HEADS
        N_EXP = 8
        TOP_K = 2
        MOE_I = 352
        SH_I = 1408
        EPS = 1e-06
        ROPE_THETA = 1000000.0

        def _rms(x, w):
            v = jnp.mean(jnp.square(x), axis=-1, keepdims=True)
            return x * jax.lax.rsqrt(v + EPS) * w

        def _rope(q, k):
            S, D = (q.shape[1], q.shape[-1])
            inv = 1.0 / ROPE_THETA ** (jnp.arange(0, D, 2, dtype=jnp.float32) / D)
            freqs = jnp.arange(S, dtype=jnp.float32)[:, None] * inv[None, :]
            emb = jnp.concatenate([freqs, freqs], axis=-1)
            cos = jnp.cos(emb)[None, :, None, :]
            sin = jnp.sin(emb)[None, :, None, :]

            def rot(t):
                t1, t2 = (t[..., :D // 2], t[..., D // 2:])
                return jnp.concatenate([-t2, t1], axis=-1)
            return (q * cos + rot(q) * sin, k * cos + rot(k) * sin)
        key = jax.random.key(seed)
        ks = jax.random.split(key, 20)
        s = 0.02
        d = {'x': jax.random.normal(ks[0], (2, 256, HID), jnp.float32), 'w_ln1': jnp.ones((HID,), jnp.float32), 'wq': jax.random.normal(ks[1], (HID, N_HEADS * HEAD_DIM), jnp.float32) * s, 'bq': jnp.zeros((N_HEADS * HEAD_DIM,), jnp.float32), 'wk': jax.random.normal(ks[2], (HID, N_KV * HEAD_DIM), jnp.float32) * s, 'bk': jnp.zeros((N_KV * HEAD_DIM,), jnp.float32), 'wv': jax.random.normal(ks[3], (HID, N_KV * HEAD_DIM), jnp.float32) * s, 'bv': jnp.zeros((N_KV * HEAD_DIM,), jnp.float32), 'wo': jax.random.normal(ks[4], (N_HEADS * HEAD_DIM, HID), jnp.float32) * s, 'w_ln2': jnp.ones((HID,), jnp.float32), 'w_router': jax.random.normal(ks[5], (HID, N_EXP), jnp.float32) * s, 'w_gate_e': jax.random.normal(ks[6], (N_EXP, HID, MOE_I), jnp.float32) * s, 'w_up_e': jax.random.normal(ks[7], (N_EXP, HID, MOE_I), jnp.float32) * s, 'w_down_e': jax.random.normal(ks[8], (N_EXP, MOE_I, HID), jnp.float32) * s, 'w_sh_gate': jax.random.normal(ks[9], (HID, SH_I), jnp.float32) * s, 'w_sh_up': jax.random.normal(ks[10], (HID, SH_I), jnp.float32) * s, 'w_sh_down': jax.random.normal(ks[11], (SH_I, HID), jnp.float32) * s, 'w_sh_eg': jax.random.normal(ks[12], (HID, 1), jnp.float32) * s}
        return d
    _L0_ffn_all = _L0_ffn_setup()
    _L0_ffn_in = {k: v for k, v in _L0_ffn_all.items() if k in ('w_ln1', 'wq', 'bq', 'wk', 'bk', 'wv', 'bv', 'wo', 'w_ln2', 'w_router', 'w_gate_e', 'w_up_e', 'w_down_e', 'w_sh_gate', 'w_sh_up', 'w_sh_down', 'w_sh_eg')}
    del _L0_ffn_all
    return {'x': x, 'ctx_1024': ctx_1024, 'fside_BxSx2_0': fside_BxSx2_0, 'L0_attn_w_qkv': _L0_attn_in['w_qkv'], 'L0_attn_w_out': _L0_attn_in['w_out'], 'L0_xattn_Wq': _L0_xattn_in['Wq'], 'L0_xattn_Wkv': _L0_xattn_in['Wkv'], 'L0_xattn_Wout': _L0_xattn_in['Wout'], 'L0_xattn_bout': _L0_xattn_in['bout'], 'L0_ffn_w_ln1': _L0_ffn_in['w_ln1'], 'L0_ffn_wq': _L0_ffn_in['wq'], 'L0_ffn_bq': _L0_ffn_in['bq'], 'L0_ffn_wk': _L0_ffn_in['wk'], 'L0_ffn_bk': _L0_ffn_in['bk'], 'L0_ffn_wv': _L0_ffn_in['wv'], 'L0_ffn_bv': _L0_ffn_in['bv'], 'L0_ffn_wo': _L0_ffn_in['wo'], 'L0_ffn_w_ln2': _L0_ffn_in['w_ln2'], 'L0_ffn_w_router': _L0_ffn_in['w_router'], 'L0_ffn_w_gate_e': _L0_ffn_in['w_gate_e'], 'L0_ffn_w_up_e': _L0_ffn_in['w_up_e'], 'L0_ffn_w_down_e': _L0_ffn_in['w_down_e'], 'L0_ffn_w_sh_gate': _L0_ffn_in['w_sh_gate'], 'L0_ffn_w_sh_up': _L0_ffn_in['w_sh_up'], 'L0_ffn_w_sh_down': _L0_ffn_in['w_sh_down'], 'L0_ffn_w_sh_eg': _L0_ffn_in['w_sh_eg']}

def reference(x, ctx_1024, fside_BxSx2_0, L0_attn_w_qkv, L0_attn_w_out, L0_xattn_Wq, L0_xattn_Wkv, L0_xattn_Wout, L0_xattn_bout, L0_ffn_w_ln1, L0_ffn_wq, L0_ffn_bq, L0_ffn_wk, L0_ffn_bk, L0_ffn_wv, L0_ffn_bv, L0_ffn_wo, L0_ffn_w_ln2, L0_ffn_w_router, L0_ffn_w_gate_e, L0_ffn_w_up_e, L0_ffn_w_down_e, L0_ffn_w_sh_gate, L0_ffn_w_sh_up, L0_ffn_w_sh_down, L0_ffn_w_sh_eg):
    import jax
    import jax.numpy as jnp

    def _L0_attn_ref(x, w_qkv, w_out):
        import jax, jax.numpy as jnp
        import numpy as np
        HIDDEN = 512
        HEADS = 16
        HEAD_DIM = HIDDEN // HEADS
        NEG = -10000000000.0
        b, s, _ = x.shape
        qkv = x @ w_qkv
        qkv = qkv.reshape(b, s, 3, HEADS, HEAD_DIM)
        q, k, v = (qkv[:, :, 0], qkv[:, :, 1], qkv[:, :, 2])
        scale = jnp.sqrt(jnp.float32(HEAD_DIM)).astype(x.dtype)
        q = q / scale
        scores = jnp.einsum('bqhd,bkhd->bhqk', q, k)
        causal_mask = jnp.arange(s)[:, None] >= jnp.arange(s)[None, :]
        scores = jnp.where(causal_mask[None, None], scores, NEG)
        attn = jax.nn.softmax(scores, axis=-1)
        out = jnp.einsum('bhqk,bkhd->bqhd', attn, v).reshape(b, s, HIDDEN)
        return out @ w_out

    def _L0_xattn_ref(x, ctx, pos_map, ctx_pos_map, Wq, Wkv, Wout, bout):
        import jax, jax.numpy as jnp
        import numpy as np
        DIM = 512
        CTX_DIM = 256
        N_HEADS = 32
        HEAD_DIM = DIM // N_HEADS
        POS_DIM = 2
        B, N, CTXN = (2, 512, 512)
        ROPE_BASE = 10000.0

        def apply_axial_rope(x, pos):
            b, n, h, d = x.shape
            p = pos.shape[-1]
            dpa = d // p
            half = dpa // 2
            freqs = ROPE_BASE ** (-jnp.arange(half, dtype=x.dtype) / half)
            ang = pos[..., :, None] * freqs
            cos = jnp.cos(ang)[:, :, None, :, :]
            sin = jnp.sin(ang)[:, :, None, :, :]
            xr = x.reshape(b, n, h, p, half, 2)
            x1, x2 = (xr[..., 0], xr[..., 1])
            out = jnp.stack([x1 * cos - x2 * sin, x1 * sin + x2 * cos], axis=-1)
            return out.reshape(b, n, h, d)
        b, n, _ = x.shape
        ctx_n = ctx.shape[1]
        q = (x @ Wq).reshape(b, n, N_HEADS, HEAD_DIM)
        k, v = jnp.split(ctx @ Wkv, 2, axis=-1)
        k = k.reshape(b, ctx_n, N_HEADS, HEAD_DIM)
        v = v.reshape(b, ctx_n, N_HEADS, HEAD_DIM)
        q = apply_axial_rope(q, pos_map)
        k = apply_axial_rope(k, ctx_pos_map)
        scale = 1.0 / np.sqrt(HEAD_DIM).astype(np.float32)
        logits = jnp.einsum('bqhd,bkhd->bhqk', q, k) * scale
        w = jax.nn.softmax(logits, axis=-1)
        attn = jnp.einsum('bhqk,bkhd->bqhd', w, v)
        attn = attn.reshape(b, n, N_HEADS * HEAD_DIM)
        return attn @ Wout + bout

    def _L0_ffn_ref(x, w_ln1, wq, bq, wk, bk, wv, bv, wo, w_ln2, w_router, w_gate_e, w_up_e, w_down_e, w_sh_gate, w_sh_up, w_sh_down, w_sh_eg):
        import jax, jax.numpy as jnp
        import numpy as np
        HID = 512
        N_HEADS = 16
        N_KV = 16
        HEAD_DIM = HID // N_HEADS
        N_EXP = 8
        TOP_K = 2
        MOE_I = 352
        SH_I = 1408
        EPS = 1e-06
        ROPE_THETA = 1000000.0

        def _rms(x, w):
            v = jnp.mean(jnp.square(x), axis=-1, keepdims=True)
            return x * jax.lax.rsqrt(v + EPS) * w

        def _rope(q, k):
            S, D = (q.shape[1], q.shape[-1])
            inv = 1.0 / ROPE_THETA ** (jnp.arange(0, D, 2, dtype=jnp.float32) / D)
            freqs = jnp.arange(S, dtype=jnp.float32)[:, None] * inv[None, :]
            emb = jnp.concatenate([freqs, freqs], axis=-1)
            cos = jnp.cos(emb)[None, :, None, :]
            sin = jnp.sin(emb)[None, :, None, :]

            def rot(t):
                t1, t2 = (t[..., :D // 2], t[..., D // 2:])
                return jnp.concatenate([-t2, t1], axis=-1)
            return (q * cos + rot(q) * sin, k * cos + rot(k) * sin)
        B, S, H = x.shape
        h = _rms(x, w_ln1)
        q = (h @ wq + bq).reshape(B, S, N_HEADS, HEAD_DIM)
        k = (h @ wk + bk).reshape(B, S, N_KV, HEAD_DIM)
        v = (h @ wv + bv).reshape(B, S, N_KV, HEAD_DIM)
        q, k = _rope(q, k)
        rep = N_HEADS // N_KV
        if rep > 1:
            k = jnp.repeat(k, rep, axis=2)
            v = jnp.repeat(v, rep, axis=2)
        scores = jnp.einsum('bqhd,bkhd->bhqk', q, k) * HEAD_DIM ** (-0.5)
        causal = jnp.tril(jnp.ones((S, S), bool))
        scores = jnp.where(causal[None, None], scores, jnp.finfo(scores.dtype).min)
        attn = jax.nn.softmax(scores, axis=-1)
        ctx = jnp.einsum('bhqk,bkhd->bqhd', attn, v).reshape(B, S, N_HEADS * HEAD_DIM)
        x = x + ctx @ wo
        h = _rms(x, w_ln2).reshape(B * S, H)
        logits = h @ w_router
        probs = jax.nn.softmax(logits, axis=-1)
        top_w, top_i = jax.lax.top_k(probs, TOP_K)
        combine = jnp.sum(jax.nn.one_hot(top_i, N_EXP, dtype=h.dtype) * top_w[..., None], axis=1)
        g = jnp.einsum('th,ehi->eti', h, w_gate_e)
        u = jnp.einsum('th,ehi->eti', h, w_up_e)
        y = jnp.einsum('eti,eih->eth', jax.nn.silu(g) * u, w_down_e)
        routed = jnp.einsum('eth,te->th', y, combine)
        sh = jax.nn.silu(h @ w_sh_gate) * (h @ w_sh_up) @ w_sh_down
        sh = sh * jax.nn.sigmoid(h @ w_sh_eg)
        x = x + (routed + sh).reshape(B, S, H)
        return x
    x = x + _L0_attn_ref(_layernorm(x, axis=-1), L0_attn_w_qkv, L0_attn_w_out)
    x = x + _L0_xattn_ref(_layernorm(x, axis=-1), ctx_1024, fside_BxSx2_0, fside_BxSx2_0, L0_xattn_Wq, L0_xattn_Wkv, L0_xattn_Wout, L0_xattn_bout)
    x = x + _L0_ffn_ref(_layernorm(x, axis=-1), L0_ffn_w_ln1, L0_ffn_wq, L0_ffn_bq, L0_ffn_wk, L0_ffn_bk, L0_ffn_wv, L0_ffn_bv, L0_ffn_wo, L0_ffn_w_ln2, L0_ffn_w_router, L0_ffn_w_gate_e, L0_ffn_w_up_e, L0_ffn_w_down_e, L0_ffn_w_sh_gate, L0_ffn_w_sh_up, L0_ffn_w_sh_down, L0_ffn_w_sh_eg)
    return x

_drawn_inputs = setup_inputs


def setup_inputs(seed=0):
    import zlib

    import numpy as np

    out = dict(_drawn_inputs(seed))
    spreads = {'L0_xattn_bout': (0.0, 0.1),
     'L0_ffn_w_ln1': (1.0, 0.6),
     'L0_ffn_bq': (0.0, 0.8),
     'L0_ffn_bk': (0.0, 0.8),
     'L0_ffn_bv': (0.0, 0.38),
     'L0_ffn_w_ln2': (1.0, 0.6)}
    factors = {'L0_ffn_wq': 8.0,
     'L0_ffn_wk': 8.0,
     'L0_ffn_w_router': 8.0,
     'L0_ffn_w_gate_e': 8.0,
     'L0_ffn_w_up_e': 8.0,
     'L0_ffn_w_down_e': 8.0,
     'L0_ffn_w_sh_gate': 2.763,
     'L0_ffn_w_sh_up': 2.681,
     'L0_ffn_w_sh_down': 2.695,
     'L0_ffn_w_sh_eg': 8.0}
    for name, (base, spread) in spreads.items():
        noise = np.random.default_rng([zlib.crc32(name.encode()), seed]).standard_normal(out[name].shape)
        drawn = base * np.exp(spread * noise) if base else spread * noise
        out[name] = jnp.asarray(drawn.astype(out[name].dtype))
    for name, factor in factors.items():
        out[name] = (out[name] * factor).astype(out[name].dtype)
    return out
```

```python
from contextlib import ExitStack

import numpy as np

import concourse.bass as bass
import concourse.mybir as mybir

F32 = mybir.dt.float32
F32R = mybir.dt.float32r
BF16 = mybir.dt.bfloat16
I32 = mybir.dt.int32
U32 = mybir.dt.uint32
ACT = mybir.ActivationFunctionType
ALU = mybir.AluOpType
AX_X = mybir.AxisListType.X

P = 128
B, S, D = 4, 512, 512
TT = S // P
KD = D // P
CTX = 256
MASKED = -1.0e30
HEADS_AT_ONCE = 4
STACK_SLOTS = 3
PROB_SLOTS = 8
MAX_ROW = 96
STACK_ROWS = MAX_ROW + 2 * HEADS_AT_ONCE


def hi_lo_passes(n_k):
    return [(k, a, b) for k in range(n_k) for a, b in ((0, 0), (0, 1), (1, 0))]


class Args:

    def __init__(self, **items):
        self.items = items

    def __getattr__(self, name):
        return self.items[name]


class Signals:

    def __init__(self, nc, names):
        self.nc = nc
        self.of = {n: nc.alloc_semaphore(n) for n in names}
        nums = sorted(s.num for s in self.of.values())
        assert nums == list(range(nums[0], nums[-1] + 1))
        self.range = range(nums[0], nums[-1] + 1)

    def __getattr__(self, name):
        return self.of[name]

    def clear(self):
        self.nc.all_engine_barrier(sems_to_clear=self.range)


SIGNALS = [
    "raw_loaded0", "raw_loaded1", "hi_made", "lo_made", "table_loaded", "table_made",
    "x_loaded", "ctx_loaded", "ln_step", "var_ready", "std_ready", "norm_ready", "rms_ready", "rms_std",
    "transposed", "hT_hi", "hT_lo", "proj_done", "v_stored", "raw_made", "shuffled", "cos_made",
    "sin_made", "rotated", "proj_hi", "proj_lo", "qk_stored0", "qk_stored1", "stack_loaded0", "stack_loaded1", "stack_loaded2",
    "scores_ready", "max_done", "max_transposed", "max_hi", "max_lo", "max_loaded", "scoresT_ready",
    "exp_done", "pv_done", "recip_made", "sums_moved", "attn_out", "attn_hi", "attn_lo", "attn_packed0", "attn_packed1",
    "out_proj", "out_made", "out_stored0", "out_stored1", "ang_step", "angles", "trig_made", "pos_loaded", "pos_t", "pos_sb",
    "residual_made", "const_made",
]


def make_constants(nc, s, c):
    with (
        nc.sbuf_tensor("maskq", [P, P], F32) as maskq,
        nc.sbuf_tensor("maskk", [P, P], F32) as maskk,
        nc.Block() as block,
    ):

        @block.gpsimd
        def _(pool):
            pool.memset(c.ident[:], 0.0).then_inc(s.const_made, 1)
            pool.memset(maskq[:], 0.0).then_inc(s.const_made, 1)
            pool.memset(maskk[:], 0.0).then_inc(s.const_made, 1)
            pool.memset(c.pick[:], 0.0).then_inc(s.const_made, 1)
            pool.wait_ge(s.const_made, 4)
            diag = dict(base=0, pattern=[[-1, P]], channel_multiplier=1)
            pool.affine_select(out=c.ident[:], in_=c.ident[:], compare_op=ALU.not_equal, fill=1.0,
                               **diag).then_inc(s.const_made, 1)
            pool.affine_select(out=maskq[:], in_=maskq[:], compare_op=ALU.is_ge, fill=MASKED,
                               **diag).then_inc(s.const_made, 1)
            pool.affine_select(out=maskk[:], in_=maskk[:], compare_op=ALU.is_ge, fill=MASKED,
                               base=0, pattern=[[1, P]], channel_multiplier=-1).then_inc(s.const_made, 1)
            for n, base in enumerate((0, -HEADS_AT_ONCE)):
                pool.wait_ge(s.const_made, 7 + n)
                pool.affine_select(out=c.pick[MAX_ROW:STACK_ROWS, :], in_=c.pick[MAX_ROW:STACK_ROWS, :],
                                   compare_op=ALU.not_equal, fill=1.0, base=base,
                                   pattern=[[-1, HEADS_AT_ONCE]], channel_multiplier=1).then_inc(s.const_made, 1)

        @block.vector
        def _(dve):
            nc.vector.memset(c.ones[:], 1.0).then_inc(s.table_made, 1)
            dve.wait_ge(s.const_made, 9)
            nc.vector.tensor_copy(c.identb[:], c.ident[:]).then_inc(s.table_made, 1)
            nc.vector.tensor_copy(c.maskqb[:], maskq[:]).then_inc(s.table_made, 1)
            nc.vector.tensor_copy(c.maskkb[:], maskk[:]).then_inc(s.table_made, 1)

    s.clear()


def split_weights(nc, s, jobs, raw):

    def staged(n, j):
        k, m = j[0].shape[1], j[0].shape[2]
        return raw[:, n % 2, 0 : k * m].rearrange("p (k n) -> p k n", k=k)

    with nc.Block() as block:

        @block.sync
        def _(sp):
            for n, j in enumerate(jobs):
                if n >= 2:
                    sp.wait_ge(s.hi_made, n - 1)
                    sp.wait_ge(s.lo_made, n - 1)
                sp.dma_start(staged(n, j), j[0], allow_slow_non_contiguous=True).then_inc((s.raw_loaded0, s.raw_loaded1)[n % 2], 16)

        @block.scalar
        def _(act):
            for n, j in enumerate(jobs):
                act.wait_ge((s.raw_loaded0, s.raw_loaded1)[n % 2], 16 * (n // 2 + 1))
                nc.scalar.activation(j[1], staged(n, j), ACT.Copy).then_inc(s.hi_made, 1)

        @block.vector
        def _(dve):
            for n, j in enumerate(jobs):
                dve.wait_ge(s.hi_made, n + 1)
                nc.vector.tensor_tensor(j[2], staged(n, j), j[1].bitcast(F32), ALU.subtract).then_inc(s.lo_made, 1)

    s.clear()


def attention_phase(nc, s, c, psum, a):
    cross, rotary = a.kind == "cross", a.kind == "rotary"
    causal, rope = not cross, a.kind != "first"
    dh = 16 if cross else 32
    heads = D // dh
    groups = heads // HEADS_AT_ONCE
    tiles_qk = KD
    groups_of_tile = groups // tiles_qk
    scale = float(dh) ** -0.5
    nkv = (CTX if cross else D) // P
    v_width = 2 * D if cross else D
    n_in = KD + (nkv if cross else 0)


    ctx = ExitStack()
    with ctx:
        sb = lambda name, shape, dt=F32: ctx.enter_context(nc.sbuf_tensor(f"{a.kind}_{name}", shape, dt))
        w_hi, w_lo = sb("w_hi", [P, 2 * KD + 2 * nkv, D], F32R), sb("w_lo", [P, 2 * KD + 2 * nkv, D], F32R)
        wq, wk, wv, wo = 0, KD, KD + nkv, KD + 2 * nkv
        xt = sb("xt", [P, TT, D])
        h1 = sb("h1", [P, TT, D]) if rotary else None
        prob = sb("prob", [P, PROB_SLOTS, S])
        raw = prob[:].rearrange("p (a b) n -> p a (b n)", a=2)
        hn = prob[:, 0:TT, :]
        hT = [sb("hT_hi", [P, n_in, S], F32R), sb("hT_lo", [P, n_in, S], F32R)]
        ctx_t = prob[:, TT : TT + 2, :].rearrange("p a (b n) -> p (a b) n", b=2)
        v = sb("v", [P, TT, v_width])
        q_stack = sb("q_stack", [P, STACK_SLOTS, HEADS_AT_ONCE, S], F32R)
        k_stack = sb("k_stack", [P, STACK_SLOTS, HEADS_AT_ONCE, S], F32R)
        part_hi, part_lo = sb("part_hi", [P, 2, S], F32R), sb("part_lo", [P, 2, S], F32R)
        if rope:
            rawqk, shuf, cosp = sb("rawqk", [P, 2, S]), sb("shuf", [P, S]), sb("cosp", [P, 2, S])
            cos_t, sin_t = sb("cos_t", [P, S]), sb("sin_t", [P, S])
        neg_max = sb("neg_max", [P, 2, TT, HEADS_AT_ONCE])
        max_hi, max_lo = sb("max_hi", [HEADS_AT_ONCE, 2, S], F32R), sb("max_lo", [HEADS_AT_ONCE, 2, S], F32R)
        recip = sb("recip", [P, S])
        attn = sb("attn", [P, S])
        attn_part = [sb("attn_hi", [P, 2, S], F32R), sb("attn_lo", [P, 2, S], F32R)] if cross else None
        out_t = prob[:, 0:2, :]
        stats, mv = sb("stats", [P, TT, 6]), sb("mv", [P, TT, 2])
        std, rstd = sb("std", [P, TT]), sb("rstd", [P, TT])
        ssq, rms = sb("ssq", [P, TT]), sb("rms", [P, TT])
        if rotary:
            w_ln, bias_raw, bias_q = sb("w_ln", [P, KD]), sb("bias_raw", [P, 2, KD]), sb("bias_q", [P, KD])
            bv_row = sb("bv_row", [P, D])
        if cross:
            bo_row = sb("bo_row", [P, D])
            freq = sb("freq", [2, P])
            sign = sb("sign", [P, 1])
            pos = sb("pos", [P, TT, 2])
            ang, turns, posT = [recip, attn], prob[:, 6, :], prob[0:2, 7, :]

        cols = lambda w, n: w.rearrange("(k p) n -> p k n", p=P)[:, :, n * D : (n + 1) * D]
        jobs = []
        for at, n_k, src in ((wq, KD, cols(*a.wq)), (wk, nkv, cols(*a.wk)), (wv, nkv, cols(*a.wv)), (wo, KD, cols(*a.wo))):
            jobs.append((src, w_hi[:, at : at + n_k, :], w_lo[:, at : at + n_k, :]))
        split_weights(nc, s, jobs, raw)

        with nc.Block() as block:

            @block.sync
            def _(sp):
                n = 0
                if rotary:
                    for dst, src in ((cos_t[:], a.cos), (sin_t[:], a.sin),
                                     (w_ln[:], a.w_ln.rearrange("(k p) -> p k", p=P)),
                                     (bias_raw[:, 0, :], a.bq.rearrange("(k p) -> p k", p=P)),
                                     (bias_raw[:, 1, :], a.bk.rearrange("(k p) -> p k", p=P)),
                                     (bv_row[:], a.bv.partition_broadcast(P))):
                        sp.dma_start(dst, src, allow_slow_non_contiguous=True).then_inc(s.table_loaded, 16)
                        n += 16
                if cross:
                    for dst, src in ((freq[:], a.freq), (sign[:], a.sign), (bo_row[:], a.bo.partition_broadcast(P))):
                        sp.dma_start(dst, src).then_inc(s.table_loaded, 16)
                        n += 16
                if n:
                    sp.wait_ge(s.table_loaded, n)

            @block.vector
            def _(dve):
                if rotary:
                    dve.wait_ge(s.table_loaded, 6 * 16)
                    nc.vector.tensor_scalar(bias_q[:], bias_raw[:, 0, :], scale, None, ALU.mult).then_inc(s.table_made, 1)
                zero = s.table_made
                for slot in range(STACK_SLOTS):
                    for stack in (q_stack, k_stack):
                        if cross:
                            for r0 in (32, 64):
                                nc.vector.memset(stack[r0 : r0 + 32, slot].bitcast(F32), 0.0).then_inc(zero, 1)
                    nc.vector.tensor_copy(
                        k_stack[MAX_ROW:STACK_ROWS, slot],
                        c.pick[MAX_ROW:STACK_ROWS, :].unsqueeze(2).to_broadcast([2 * HEADS_AT_ONCE, HEADS_AT_ONCE, S]),
                    ).then_inc(zero, 1)

            @block.gpsimd
            def _(pool):
                if cross:
                    vv = v[:].rearrange("p t (h two d) -> p t h two d", two=2, d=dh)
                    for t in range(TT):
                        pool.memset(vv[:, t, :, 1, :], 1.0).then_inc(s.const_made, 1)

        s.clear()

        N16 = TT * HEADS_AT_ONCE
        stack_loaded = (s.stack_loaded0, s.stack_loaded1, s.stack_loaded2)
        attn_packed = (s.attn_packed0, s.attn_packed1)
        out_stored = (s.out_stored0, s.out_stored1)

        def first_step(i):
            return (i * a.lead) // N16

        NORM_STEP = 6
        MAX_STEP = a.lead
        width_q = lambda t: (t + 1) * P if causal else S
        start_k = lambda t: t * P if causal else 0
        bank_score, bank_max, bank_scoreT = (0, 1), 2, (3, 4)
        bank_o = (5, 6) if cross else (5, 5)
        bank_sum = 6
        bank_proj = (6, 7)

        proj = [("v", t, n) for t in range(TT) for n in range(1)]
        proj += [(w, m, 0) for m in range(tiles_qk) for w in "qk"]
        n_v = TT
        n_qk = 2 * tiles_qk

        with nc.Fori(0, B) as b:
            x_dram = a.x[bass.ds(b * S, S), :].rearrange("(t p) d -> p t d", p=P)
            out_dram = a.out[bass.ds(b * S, S), :].rearrange("(t p) d -> t p d", p=P)
            with nc.Block() as block:

                def pack(sp, g):
                    sp.wait_ge(s.attn_hi, g + 1)
                    sp.wait_ge(s.attn_lo, g + 1)
                    for part in range(2):
                        for j in range(HEADS_AT_ONCE):
                            r = (g % 2) * 64 + 16 * j
                            sp.dma_start(hT[part][r : r + 16, g // 2].bitcast(F32),
                                         attn_part[part][32 * j : 32 * j + 16, g % 2].bitcast(F32)).then_inc(attn_packed[g % 2], 16)

                def angle_steps(dve):
                    two_pi = 2.0 * np.pi
                    big = float(np.float32(6.28125))
                    small = float(np.float32(two_pi - 6.28125))
                    dve.wait_ge(s.angles, 1)
                    n = 0
                    nc.vector.tensor_copy(ang[0][:], psum[7][:]).then_inc(s.ang_step, 1)
                    nc.vector.tensor_scalar(ang[1][:], psum[7][:], float(np.pi / 2), None, ALU.add).then_inc(s.ang_step, 1)
                    n = 2
                    for x in ang:
                        dve.wait_ge(s.ang_step, n)
                        nc.vector.tensor_scalar(turns, x[:], 1.0 / two_pi, 12582912.0, ALU.mult, ALU.add).then_inc(s.ang_step, 1)
                        dve.wait_ge(s.ang_step, n + 1)
                        nc.vector.tensor_scalar(turns, turns, 12582912.0, None, ALU.subtract).then_inc(s.ang_step, 1)
                        dve.wait_ge(s.ang_step, n + 2)
                        nc.vector.scalar_tensor_tensor(x[:], turns, -big, x[:], ALU.mult, ALU.add).then_inc(s.ang_step, 1)
                        dve.wait_ge(s.ang_step, n + 3)
                        nc.vector.scalar_tensor_tensor(x[:], turns, -small, x[:], ALU.mult, ALU.add).then_inc(s.ang_step, 1)
                        dve.wait_ge(s.ang_step, n + 4)
                        nc.vector.tensor_scalar(x[:], x[:], 3.1415925, -3.1415925, ALU.min, ALU.max).then_inc(s.ang_step, 1)
                        n += 5

                @block.sync
                def _(sp):
                    sp.dma_start(xt[:], x_dram).then_inc(s.x_loaded, 16)
                    if cross:
                        sp.dma_start(ctx_t, a.ctx[bass.ds(b * S, S), :].rearrange("(t p) d -> p t d", p=P)).then_inc(s.ctx_loaded, 16)
                        sp.dma_start(pos[:], a.pos[bass.ds(b * S, S), :].rearrange("(t p) d -> p t d", p=P)).then_inc(s.pos_loaded, 16)

                    def load_stack(g):
                        m = g // groups_of_tile
                        rows = slice(g * HEADS_AT_ONCE * dh, (g + 1) * HEADS_AT_ONCE * dh)
                        sp.wait_ge(s.qk_stored0, 32 * (m + 1))
                        sp.wait_ge(s.qk_stored1, 32 * (m + 1))
                        if g >= STACK_SLOTS:
                            sp.wait_ge(s.scoresT_ready, N16 * (g - STACK_SLOTS + 1))
                        for stack, w, parts in ((q_stack, 0, (0, 1, 0)), (k_stack, 1, (0, 0, 1))):
                            for i, part in enumerate(parts):
                                sp.dma_start(stack[i * dh : (i + 1) * dh, g % STACK_SLOTS].bitcast(F32),
                                             a.scratch[w, part, rows, :].rearrange("(h p) n -> p h n", p=dh)
                                             ).then_inc(stack_loaded[g % STACK_SLOTS], 16)

                    loaded = 0
                    for n in range(n_qk):
                        sp.wait_ge(s.proj_hi, n + 1)
                        sp.wait_ge(s.proj_lo, n + 1)
                        dst = a.scratch[n % 2, :, (n // 2) * P : (n // 2 + 1) * P, :]
                        stored = (s.qk_stored0, s.qk_stored1)[n % 2]
                        sp.dma_start(dst[0], part_hi[:, n % 2].bitcast(F32)).then_inc(stored, 16)
                        sp.dma_start(dst[1], part_lo[:, n % 2].bitcast(F32)).then_inc(stored, 16)
                        if n >= 3 and n % 2 == 1 and loaded < STACK_SLOTS:
                            for _g in range(groups_of_tile):
                                if loaded < STACK_SLOTS:
                                    load_stack(loaded)
                                    loaded += 1
                    while loaded < min(STACK_SLOTS, groups):
                        load_stack(loaded)
                        loaded += 1

                    for g in range(groups):
                        sp.wait_ge(s.max_hi, g + 1)
                        sp.wait_ge(s.max_lo, g + 1)
                        for i, src in enumerate((max_hi, max_lo)):
                            r0 = MAX_ROW + i * HEADS_AT_ONCE
                            sp.dma_start(q_stack[r0 : r0 + HEADS_AT_ONCE, g % STACK_SLOTS].bitcast(F32),
                                         src[:, g % 2].bitcast(F32).unsqueeze(1).to_broadcast([HEADS_AT_ONCE, HEADS_AT_ONCE, S])
                                         ).then_inc(s.max_loaded, 16)
                        if g >= 1 and g + 2 < groups:
                            load_stack(g + 2)
                        if cross and g >= 3:
                            pack(sp, g - 3)
                    if cross:
                        for g in range(groups - 3, groups):
                            pack(sp, g)
                    for t in range(TT):
                        sp.wait_ge(s.out_made, t + 1)
                        sp.dma_start(out_dram[t], out_t[:, t % 2]).then_inc(out_stored[t % 2], 16)
                    for stored in out_stored:
                        sp.wait_ge(stored, 16 * (TT // 2))

                @block.tensor
                def _(pe):
                    for t in range(TT):
                        pe.wait_ge(s.norm_ready, t + 1)
                        for k in range(KD):
                            last = nc.tensor.transpose(psum[k][:, t * P : (t + 1) * P], hn[:, t, k * P : (k + 1) * P], c.ident[:])
                    last.then_inc(s.transposed, 1)
                    if cross:
                        pe.wait_ge(s.ctx_loaded, 16)
                        for k in range(nkv):
                            for t in range(TT):
                                last = nc.tensor.transpose(psum[KD + k][:, t * P : (t + 1) * P], ctx_t[:, t, k * P : (k + 1) * P], c.ident[:])
                        last.then_inc(s.transposed, 1)
                        pe.wait_ge(s.pos_loaded, 16)
                        for t in range(TT):
                            last = nc.tensor.transpose(psum[6][0:2, t * P : (t + 1) * P], pos[:, t, :], c.ident[:])
                        last.then_inc(s.pos_t, 1)
                        pe.wait_ge(s.pos_sb, 1)
                        nc.tensor.matmul(psum[7][:], freq[:], posT, start=True, stop=True).then_inc(s.angles, 1)
                        pe.wait_ge(s.ang_step, 2)
                    for n, (what, m, _c) in enumerate(proj):
                        if n == 0:
                            pe.wait_ge(s.hT_hi, n_in)
                            pe.wait_ge(s.hT_lo, n_in)
                        if n >= 2:
                            if n - 2 < n_v:
                                pe.wait_ge(s.v_stored, n - 1)
                            elif rope:
                                pe.wait_ge(s.raw_made, n - 1 - n_v)
                            else:
                                pe.wait_ge(s.proj_hi, n - 1 - n_v)
                                pe.wait_ge(s.proj_lo, n - 1 - n_v)
                        nk = nkv if what in "kv" else KD
                        first = KD if cross and what in "kv" else 0
                        w0 = {"q": wq, "k": wk, "v": wv}[what]
                        steps = hi_lo_passes(nk)
                        for i, (k, pa, pb) in enumerate(steps):
                            w = (w_hi, w_lo)
                            if what == "v":
                                lhs, rhs = hT[pa][:, first + k, m * P : (m + 1) * P], w[pb][:, w0 + k, :]
                            else:
                                lhs, rhs = w[pa][:, w0 + k, m * P : (m + 1) * P], hT[pb][:, first + k, :]
                            last = nc.tensor.matmul(psum[bank_proj[n % 2]][:], lhs, rhs, start=i == 0, stop=i == len(steps) - 1)
                        last.then_inc(s.proj_done, 1)

                    def scores(g, i):
                        t, j = divmod(i, HEADS_AT_ONCE)
                        n = g * N16 + i
                        bank = psum[bank_score[n % 2]]
                        if i == 0:
                            pe.wait_ge(stack_loaded[g % STACK_SLOTS], 96 * (g // STACK_SLOTS + 1))
                        if n >= 2:
                            pe.wait_ge(s.max_done, n - 1)
                        elif n == 0:
                            pe.wait_ge(s.hT_lo, n_in)
                        last = nc.tensor.matmul(bank[:, 0 : width_q(t)], q_stack[0:MAX_ROW, g % STACK_SLOTS, j, t * P : (t + 1) * P],
                                                k_stack[0:MAX_ROW, g % STACK_SLOTS, j, 0 : width_q(t)], start=True, stop=not causal)
                        if causal:
                            last = nc.tensor.matmul(bank[:, t * P : (t + 1) * P], c.identb[:], c.maskqb[:], start=False, stop=True)
                        last.then_inc(s.scores_ready, 1)

                    def max_transpose(g):
                        pe.wait_ge(s.max_done, N16 * (g + 1))
                        if g >= 1:
                            pe.wait_ge(s.max_lo, g)
                            pe.wait_ge(s.max_hi, g)
                        for t in range(TT):
                            last = nc.tensor.transpose(psum[bank_max][0:HEADS_AT_ONCE, t * P : (t + 1) * P], neg_max[:, g % 2, t, :], c.ident[:])
                        last.then_inc(s.max_transposed, 1)

                    def scoresT(g, i):
                        t, j = divmod(i, HEADS_AT_ONCE)
                        n = g * N16 + i
                        bank, q0 = psum[bank_scoreT[n % 2]], start_k(t)
                        if i == 0:
                            pe.wait_ge(s.max_loaded, 32 * (g + 1))
                        if n >= 2:
                            pe.wait_ge(s.exp_done, n - 1)
                        last = nc.tensor.matmul(bank[:, 0 : S - q0], k_stack[0:STACK_ROWS, g % STACK_SLOTS, j, t * P : (t + 1) * P],
                                                q_stack[0:STACK_ROWS, g % STACK_SLOTS, j, q0:S], start=True, stop=not causal)
                        if causal:
                            last = nc.tensor.matmul(bank[:, 0:P], c.identb[:], c.maskkb[:], start=False, stop=True)
                        last.then_inc(s.scoresT_ready, 1)

                    def weighted(g, t):
                        q0 = start_k(t)
                        pe.wait_ge(s.exp_done, g * N16 + (t + 1) * HEADS_AT_ONCE)
                        back = 2 if cross else 1
                        if t == 0 and g >= back:
                            pe.wait_ge(s.attn_out, g - back + 1)
                        for bank in (bank_o[g % 2],) if cross else (bank_o[0], bank_sum):
                            for j in range(HEADS_AT_ONCE):
                                pr = prob[:, (g * N16 + t * HEADS_AT_ONCE + j) % PROB_SLOTS, 0 : S - q0]
                                h = g * HEADS_AT_ONCE + j
                                val = v[:, t, 32 * h : 32 * h + 32] if bank != bank_sum or cross else c.ones[:]
                                last = nc.tensor.matmul(psum[bank][32 * j : 32 * j + 32, q0:S], val, pr, start=t == 0, stop=t == TT - 1)
                        last.then_inc(s.pv_done, 1)

                    for i in range(N16):
                        scores(0, i)
                    max_transpose(0)
                    for g in range(groups):
                        i = 0
                        for step in range(N16):
                            while g + 1 < groups and i < N16 and first_step(i) <= step:
                                scores(g + 1, i)
                                i += 1
                            scoresT(g, step)
                            if step == MAX_STEP and g + 1 < groups:
                                max_transpose(g + 1)
                            if step % HEADS_AT_ONCE == HEADS_AT_ONCE - 1:
                                t = step // HEADS_AT_ONCE
                                if t:
                                    weighted(g, t - 1)
                                elif g:
                                    weighted(g - 1, TT - 1)
                    weighted(groups - 1, TT - 1)

                    if cross:
                        for packed in attn_packed:
                            pe.wait_ge(packed, 16 * 8 * (groups // 2))
                    else:
                        pe.wait_ge(s.attn_hi, groups)
                        pe.wait_ge(s.attn_lo, groups)
                    for t in range(TT):
                        if t >= 2:
                            pe.wait_ge(s.out_made, t - 1)
                        steps = hi_lo_passes(KD)
                        for i, (k, pa, pb) in enumerate(steps):
                            last = nc.tensor.matmul(psum[t % 2][:], hT[pa][:, k, t * P : (t + 1) * P], (w_hi, w_lo)[pb][:, wo + k, :],
                                                    start=i == 0, stop=i == len(steps) - 1)
                        last.then_inc(s.out_proj, 1)

                @block.scalar
                def _(act):
                    act.wait_ge(s.var_ready, 1)
                    nc.scalar.activation(std[:], mv[:, :, 1], ACT.Sqrt).then_inc(s.std_ready, 1)
                    if rotary:
                        act.wait_ge(s.rms_ready, 1)
                        nc.scalar.activation(rms[:], ssq[:], ACT.Sqrt).then_inc(s.rms_std, 1)
                    for k in range(n_in):
                        act.wait_ge(s.transposed, 1 if k < KD else 2)
                        if rotary:
                            nc.scalar.activation(hT[0][:, k, :], psum[k][:], ACT.Copy, scale=w_ln[:, k : k + 1]).then_inc(s.hT_hi, 1)
                        else:
                            nc.scalar.activation(hT[0][:, k, :], psum[k][:], ACT.Copy).then_inc(s.hT_hi, 1)
                    if cross:
                        act.wait_ge(s.pos_t, 1)
                        nc.scalar.activation(posT, psum[6][0:2, :], ACT.Copy).then_inc(s.pos_sb, 1)
                        act.wait_ge(s.ang_step, 12)
                        nc.scalar.activation(sin_t[:], ang[0][:], ACT.Sin, scale=sign[:, 0:1]).then_inc(s.trig_made, 1)
                        nc.scalar.activation(cos_t[:], ang[1][:], ACT.Sin).then_inc(s.trig_made, 1)

                    def qk_hi(n):
                        act.wait_ge(s.rotated, n + 1)
                        if n >= 2:
                            act.wait_ge((s.qk_stored0, s.qk_stored1)[n % 2], 32 * (n // 2))
                        nc.scalar.activation(part_hi[:, n % 2], cosp[:, n % 2], ACT.Copy).then_inc(s.proj_hi, 1)

                    for n, (what, m, _c) in enumerate(proj):
                        act.wait_ge(s.proj_done, n + 1)
                        bank = psum[bank_proj[n % 2]]
                        if what == "v":
                            if rotary:
                                continue
                            if cross:
                                dst = v[:, m, :].rearrange("p (h two d) -> p h two d", two=2, d=dh)[:, :, 0, :]
                                src = bank[:].rearrange("p (h d) -> p h d", d=dh)
                            else:
                                dst, src = v[:, m, :], bank[:]
                            nc.scalar.activation(dst, src, ACT.Copy).then_inc(s.v_stored, 1)
                            continue
                        i = n - n_v
                        if rope:
                            if i >= 2:
                                act.wait_ge(s.shuffled, i - 1)
                                act.wait_ge(s.cos_made, i - 1)
                            if rotary:
                                bias = bias_q[:, m : m + 1] if what == "q" else bias_raw[:, 1, m : m + 1]
                                nc.scalar.activation(rawqk[:, i % 2], bank[:], ACT.Identity, bias=bias,
                                                     scale=scale if what == "q" else 1.0).then_inc(s.raw_made, 1)
                            else:
                                nc.scalar.activation(rawqk[:, i % 2], bank[:], ACT.Copy,
                                                     scale=scale if what == "q" else 1.0).then_inc(s.raw_made, 1)
                            if i >= 1:
                                qk_hi(i - 1)
                        else:
                            if i >= 2:
                                act.wait_ge((s.qk_stored0, s.qk_stored1)[i % 2], 32 * (i // 2))
                            nc.scalar.activation(part_hi[:, i % 2], bank[:], ACT.Copy,
                                                 scale=scale if what == "q" else 1.0).then_inc(s.proj_hi, 1)
                    if rope:
                        qk_hi(n_qk - 1)

                    def split_max(g):
                        act.wait_ge(s.max_transposed, g + 1)
                        if g >= 2:
                            act.wait_ge(s.max_loaded, 32 * (g - 1))
                        nc.scalar.activation(max_hi[:, g % 2], psum[bank_max][0:HEADS_AT_ONCE, :], ACT.Copy).then_inc(s.max_hi, 1)

                    def attn_high(g):
                        act.wait_ge(s.attn_out, g + 1)
                        if cross:
                            if g >= 2:
                                act.wait_ge(attn_packed[g % 2], 16 * 8 * (g // 2))
                            dst = attn_part[0][:, g % 2]
                        else:
                            dst = hT[0][:, g, :]
                        nc.scalar.activation(dst, attn[:], ACT.Copy).then_inc(s.attn_hi, 1)

                    split_max(0)
                    for g in range(groups):
                        for step in range(N16):
                            n = g * N16 + step
                            q0 = start_k(step // HEADS_AT_ONCE)
                            act.wait_ge(s.scoresT_ready, n + 1)
                            if n >= PROB_SLOTS:
                                act.wait_ge(s.pv_done, (n - PROB_SLOTS) // HEADS_AT_ONCE + 1)
                            nc.scalar.activation(prob[:, n % PROB_SLOTS, 0 : S - q0], psum[bank_scoreT[n % 2]][:, 0 : S - q0],
                                                 ACT.Exp).then_inc(s.exp_done, 1)
                            if step == MAX_STEP and g + 1 < groups:
                                split_max(g + 1)
                            if step == NORM_STEP and g >= 1:
                                attn_high(g - 1)
                    attn_high(groups - 1)

                @block.vector
                def _(dve):
                    dve.wait_ge(s.x_loaded, 16)
                    steps = 0
                    for t in range(TT):
                        nc.vector.bn_stats(stats[:, t, :], xt[:, t, :]).then_inc(s.ln_step, 1)
                    for t in range(TT):
                        dve.wait_ge(s.ln_step, t + 1)
                        nc.vector.bn_aggr(mv[:, t, :], stats[:, t, :]).then_inc(s.ln_step, 1)
                    dve.wait_ge(s.ln_step, 2 * TT)
                    nc.vector.tensor_scalar(mv[:, :, 1], mv[:, :, 1], 1e-5, None, ALU.add).then_inc(s.var_ready, 1)
                    dve.wait_ge(s.std_ready, 1)
                    nc.vector.reciprocal(rstd[:], std[:]).then_inc(s.ln_step, 1)
                    dve.wait_ge(s.ln_step, 2 * TT + 1)
                    norm = h1 if rotary else hn
                    for t in range(TT):
                        nc.vector.tensor_scalar(norm[:, t, :], xt[:, t, :], mv[:, t, 0:1], rstd[:, t : t + 1], ALU.subtract, ALU.mult
                                                ).then_inc(s.ln_step if rotary else s.norm_ready, 1)
                    if rotary:
                        for t in range(TT):
                            dve.wait_ge(s.ln_step, 2 * TT + 2 + t)
                            nc.vector.tensor_tensor_reduce(out=xt[:, t, :], in0=h1[:, t, :], in1=h1[:, t, :], scale=1.0, scalar=0.0,
                                                           op0=ALU.mult, op1=ALU.add, accum_out=ssq[:, t : t + 1]).then_inc(s.ln_step, 1)
                        dve.wait_ge(s.ln_step, 4 * TT + 1)
                        nc.vector.tensor_scalar(ssq[:], ssq[:], 1.0 / D, 1e-6, ALU.mult, ALU.add).then_inc(s.rms_ready, 1)
                        dve.wait_ge(s.rms_std, 1)
                        nc.vector.reciprocal(rstd[:], rms[:]).then_inc(s.ln_step, 1)
                        dve.wait_ge(s.ln_step, 4 * TT + 2)
                        for t in range(TT):
                            nc.vector.tensor_scalar(hn[:, t, :], h1[:, t, :], rstd[:, t : t + 1], None, ALU.mult).then_inc(s.norm_ready, 1)
                    for k in range(n_in):
                        dve.wait_ge(s.hT_hi, k + 1)
                        if rotary:
                            nc.vector.scalar_tensor_tensor(hT[1][:, k, :], psum[k][:], w_ln[:, k : k + 1], hT[0][:, k, :].bitcast(F32),
                                                           ALU.mult, ALU.subtract).then_inc(s.hT_lo, 1)
                        else:
                            nc.vector.tensor_tensor(hT[1][:, k, :], psum[k][:], hT[0][:, k, :].bitcast(F32), ALU.subtract).then_inc(s.hT_lo, 1)
                    if cross:
                        angle_steps(dve)

                    def qk_lo(n):
                        dve.wait_ge(s.proj_hi, n + 1)
                        if rope:
                            nc.vector.tensor_tensor(part_lo[:, n % 2], cosp[:, n % 2], part_hi[:, n % 2].bitcast(F32), ALU.subtract).then_inc(s.proj_lo, 1)
                        else:
                            nc.vector.scalar_tensor_tensor(part_lo[:, n % 2], psum[bank_proj[(n + n_v) % 2]][:], scale if n % 2 == 0 else 1.0,
                                                           part_hi[:, n % 2].bitcast(F32), ALU.mult, ALU.subtract).then_inc(s.proj_lo, 1)

                    for n, (what, m, _c) in enumerate(proj):
                        if what == "v":
                            if rotary:
                                dve.wait_ge(s.proj_done, n + 1)
                                nc.vector.tensor_tensor(v[:, m, :], psum[bank_proj[n % 2]][:], bv_row[:], ALU.add).then_inc(s.v_stored, 1)
                            continue
                        i = n - n_v
                        if rope:
                            dve.wait_ge(s.raw_made, i + 1)
                            if i == 0 and cross:
                                dve.wait_ge(s.trig_made, 2)
                            if i >= 1:
                                dve.wait_ge(s.rotated, i)
                            swap = [r ^ 1 for r in range(32)] if cross else [(r + 16) % 32 for r in range(32)]
                            nc.vector.stream_shuffle(shuf[:], rawqk[:, i % 2], swap).then_inc(s.shuffled, 1)
                            dve.wait_ge(s.shuffled, i + 1)
                            nc.vector.tensor_tensor(shuf[:], shuf[:], sin_t[:], ALU.mult).then_inc(s.sin_made, 1)
                            dve.wait_ge(s.sin_made, i + 1)
                            dve.wait_ge(s.cos_made, i + 1)
                            nc.vector.tensor_tensor(cosp[:, i % 2], cosp[:, i % 2], shuf[:], ALU.add).then_inc(s.rotated, 1)
                        qk_lo(i)

                    def tile_max(g, i):
                        t, j = divmod(i, HEADS_AT_ONCE)
                        n = g * N16 + i
                        dve.wait_ge(s.scores_ready, n + 1)
                        if i == 0 and g >= 2:
                            dve.wait_ge(s.max_transposed, g - 1)
                        nc.vector.tensor_reduce(neg_max[:, g % 2, t, j : j + 1], psum[bank_score[n % 2]][:, 0 : width_q(t)], AX_X, ALU.max,
                                                negate=True).then_inc(s.max_done, 1)

                    def split_max(g):
                        dve.wait_ge(s.max_hi, g + 1)
                        nc.vector.tensor_tensor(max_lo[:, g % 2], psum[bank_max][0:HEADS_AT_ONCE, :], max_hi[:, g % 2].bitcast(F32),
                                                ALU.subtract).then_inc(s.max_lo, 1)

                    def normalise(g):
                        dve.wait_ge(s.pv_done, TT * (g + 1))
                        if g >= 1:
                            dve.wait_ge(s.attn_out, g)
                        if cross:
                            nc.vector.stream_shuffle(recip[:], psum[bank_o[g % 2]][:], [16 + r % 16 for r in range(32)]).then_inc(s.sums_moved, 1)
                            dve.wait_ge(s.sums_moved, g + 1)
                            nc.vector.reciprocal(recip[:], recip[:]).then_inc(s.recip_made, 1)
                        else:
                            nc.vector.reciprocal(recip[:], psum[bank_sum][:]).then_inc(s.recip_made, 1)
                        dve.wait_ge(s.recip_made, g + 1)
                        if g >= 1:
                            dve.wait_ge(s.attn_hi, g)
                            dve.wait_ge(s.attn_lo, g)
                        nc.vector.tensor_tensor(attn[:], psum[bank_o[g % 2]][:], recip[:], ALU.mult).then_inc(s.attn_out, 1)

                    def attn_low(g):
                        dve.wait_ge(s.attn_hi, g + 1)
                        if cross:
                            if g >= 2:
                                dve.wait_ge(attn_packed[g % 2], 16 * 8 * (g // 2))
                            dst, high = attn_part[1][:, g % 2], attn_part[0][:, g % 2]
                        else:
                            dst, high = hT[1][:, g, :], hT[0][:, g, :]
                        nc.vector.tensor_tensor(dst, attn[:], high.bitcast(F32), ALU.subtract).then_inc(s.attn_lo, 1)

                    for i in range(N16):
                        tile_max(0, i)
                    split_max(0)
                    for g in range(groups):
                        i = 0
                        for step in range(N16):
                            while g + 1 < groups and i < N16 and first_step(i) <= step:
                                tile_max(g + 1, i)
                                i += 1
                            if step == NORM_STEP - 2 and g >= 1:
                                normalise(g - 1)
                            if step == NORM_STEP + 1 and g >= 1:
                                attn_low(g - 1)
                            if step == MAX_STEP and g + 1 < groups:
                                split_max(g + 1)
                    normalise(groups - 1)
                    attn_low(groups - 1)
                    if cross:
                        dve.wait_ge(s.residual_made, 1)
                    for t in range(TT):
                        dve.wait_ge(s.out_proj, t + 1)
                        if t >= 2:
                            dve.wait_ge(out_stored[t % 2], 16 * (t // 2))
                        nc.vector.tensor_tensor(out_t[:, t % 2], psum[t % 2][:], (h1 if rotary else xt)[:, t, :], ALU.add).then_inc(s.out_made, 1)

                @block.gpsimd
                def _(pool):
                    if rope:
                        for i in range(n_qk):
                            pool.wait_ge(s.raw_made, i + 1)
                            if i == 0 and cross:
                                pool.wait_ge(s.trig_made, 2)
                            if i >= 2:
                                pool.wait_ge(s.proj_lo, i - 1)
                            nc.gpsimd.tensor_tensor(cosp[:, i % 2], rawqk[:, i % 2], cos_t[:], ALU.mult).then_inc(s.cos_made, 1)
                    if cross:
                        pool.wait_ge(s.norm_ready, TT)
                        for t in range(TT):
                            last = nc.gpsimd.tensor_tensor(xt[:, t, :], xt[:, t, :], bo_row[:], ALU.add)
                        last.then_inc(s.residual_made, 1)

            s.clear()


EXPERTS, TOP, FE, FS = 8, 2, 352, 1408
N_TILES = B * TT
SLOT_TILES = (B * S * TOP + EXPERTS * (P - 1)) // P
SLOTS = SLOT_TILES * P
CHUNK = 2
KF = FS // P
FE_K = [(0, P), (P, P), (2 * P, FE - 2 * P)]

MOE_SIGNALS = [
    "m_loaded", "m_x2_loaded", "m_sq", "m_var", "m_std", "m_rstd", "m_norm", "m_t", "m_hi", "m_lo", "m_rt", "m_rt_sb",
    "m_logits", "m_step", "m_exp", "m_egexp", "m_gate_up", "m_silu", "m_act", "m_ahi", "m_alo", "m_down", "m_resid",
    "m_out", "m_stored", "m_rows", "m_tab", "m_ld0", "m_ld1", "g_got0", "g_got1", "g_row0", "g_row1", "g_row2", "g_row3", "g_sent0", "g_sent1", "g_sent2", "g_sent3", "m_wt", "m_zero",
    "e_ld0", "e_ld1", "e_t", "e_hT", "e_g", "e_s", "e_a", "e_at", "e_aT", "e_y", "e_ysb", "e_st0", "e_st1",
]


def shared_phase(nc, s, c, psum, a, keep):

    n_col = EXPERTS + 1
    W = CHUNK * P
    ctx = ExitStack()
    with ctx:
        sb = lambda name, shape, dt=F32: ctx.enter_context(nc.sbuf_tensor(f"shared_{name}", shape, dt))
        wg = [sb(f"wg{i}", [P, KD, FS], F32R) for i in range(2)]
        wu = [sb(f"wu{i}", [P, KD, FS], F32R) for i in range(2)]
        wd = [sb(f"wd{i}", [P, KF, D], F32R) for i in range(2)]
        wr = [sb(f"wr{i}", [P, KD, n_col], F32R) for i in range(2)]
        raw = sb("raw", [P, 2, 4 * D])
        xt, x2 = raw[:, 0, :].rearrange("p (t d) -> p t d", d=D), raw[:, 1, :].rearrange("p (t d) -> p t d", d=D)
        xt, hn = xt[:, 0:2], xt[:, 2:4]
        x2, out_t = x2[:, 0:2], x2[:, 2:4]
        hT = [sb(f"hT{i}", [P, KD, W], F32R) for i in range(2)]
        act_p = [sb(f"act{i}", [P, KF, W], F32R) for i in range(2)]
        silu, prod = sb("silu", [P, 2, W]), sb("prod", [P, 2, W])
        w_ln = sb("w_ln", [P, KD])
        rt = sb("rt", [n_col, W])
        ssq, std, rstd = sb("ssq", [P, CHUNK]), sb("std", [P, CHUNK]), sb("rstd", [P, CHUNK])
        logit, nmax, ex = sb("logit", [P, CHUNK, n_col]), sb("nmax", [P, CHUNK]), sb("ex", [P, CHUNK, EXPERTS])
        total, best = sb("total", [P, CHUNK]), sb("best", [P, CHUNK, 8])
        where = sb("where", [P, CHUNK, 8], U32)
        wheref = sb("wheref", [P, CHUNK, 8])
        gate = sb("gate", [P, CHUNK])
        rows8 = sb("rows8", [P, EXPERTS])

        jobs = []
        for src, dst in ((a.w_gate, wg), (a.w_up, wu)):
            for k in range(KD):
                jobs.append((src[k * P : (k + 1) * P, :].rearrange("(k p) n -> p k n", p=P), dst[0][:, k : k + 1], dst[1][:, k : k + 1]))
        for k0 in range(0, KF, 4):
            k1 = min(KF, k0 + 4)
            jobs.append((a.w_down[k0 * P : k1 * P, :].rearrange("(k p) n -> p k n", p=P), wd[0][:, k0:k1], wd[1][:, k0:k1]))
        jobs.append((a.w_router.rearrange("(k p) n -> p k n", p=P), wr[0][:, :, 0:EXPERTS], wr[1][:, :, 0:EXPERTS]))
        jobs.append((a.w_eg.rearrange("(k p) n -> p k n", p=P), wr[0][:, :, EXPERTS:n_col], wr[1][:, :, EXPERTS:n_col]))
        split_weights(nc, s, jobs, raw)

        with nc.Block() as block:

            @block.sync
            def _(sp):
                sp.dma_start(w_ln[:], a.w_ln.rearrange("(k p) -> p k", p=P), allow_slow_non_contiguous=True).then_inc(s.m_tab, 16)
                sp.dma_start(rows8[:], a.count8.partition_broadcast(P)).then_inc(s.m_tab, 16)
                sp.wait_ge(s.m_tab, 32)

        s.clear()

        with nc.Fori(0, N_TILES // CHUNK) as i:
            at = lambda t: t[bass.ds(i * W, W), :].rearrange("(t p) d -> p t d", p=P)
            with nc.Block() as block:

                @block.sync
                def _(sp):
                    sp.dma_start(xt, at(a.x3)).then_inc(s.m_loaded, 16)
                    sp.dma_start(x2, at(a.x2)).then_inc(s.m_x2_loaded, 16)
                    sp.wait_ge(s.m_norm, CHUNK)
                    sp.dma_start(at(a.rows), hn).then_inc(s.m_rows, 16)
                    sp.wait_ge(s.m_out, CHUNK)
                    sp.dma_start(at(a.base), out_t).then_inc(s.m_stored, 16)
                    sp.wait_ge(s.m_rows, 16)
                    sp.wait_ge(s.m_stored, 16)

                @block.tensor
                def _(pe):
                    for t in range(CHUNK):
                        pe.wait_ge(s.m_norm, t + 1)
                        for k in range(KD):
                            last = nc.tensor.transpose(psum[k][:, t * P : (t + 1) * P], hn[:, t, k * P : (k + 1) * P], c.ident[:])
                    last.then_inc(s.m_t, 1)
                    pe.wait_ge(s.m_hi, KD)
                    pe.wait_ge(s.m_lo, KD)
                    steps = hi_lo_passes(KD)
                    for n, (k, pa, pb) in enumerate(steps):
                        last = nc.tensor.matmul(psum[2][0:n_col, 0:W], wr[pa][:, k, :], hT[pb][:, k, :], start=n == 0, stop=n == len(steps) - 1)
                    last.then_inc(s.m_rt, 1)
                    for f in range(KF):
                        if f == 1:
                            pe.wait_ge(s.m_rt_sb, 1)
                            for t in range(CHUNK):
                                last = nc.tensor.transpose(psum[3][:, t * 16 : t * 16 + n_col], rt[:, t * P : (t + 1) * P], c.ident[0:n_col, 0:n_col])
                            last.then_inc(s.m_logits, 1)
                        if f >= 2:
                            pe.wait_ge(s.m_act, f - 1)
                        for half, w in enumerate((wg, wu)):
                            for n, (k, pa, pb) in enumerate(steps):
                                last = nc.tensor.matmul(psum[4 + f % 2][:, half * W : (half + 1) * W], w[pa][:, k, f * P : (f + 1) * P], hT[pb][:, k, :],
                                                        start=n == 0, stop=n == len(steps) - 1)
                        last.then_inc(s.m_gate_up, 1)
                    down = hi_lo_passes(KF)
                    for t in range(CHUNK):
                        for n, (k, pa, pb) in enumerate(down):
                            if t == 0 and (pa, pb) == (0, 0):
                                pe.wait_ge(s.m_ahi, k + 1)
                                pe.wait_ge(s.m_alo, k + 1)
                            last = nc.tensor.matmul(psum[6 + t][:], act_p[pa][:, k, t * P : (t + 1) * P], wd[pb][:, k, :], start=n == 0, stop=n == len(down) - 1)
                        last.then_inc(s.m_down, 1)

                @block.scalar
                def _(act):
                    act.wait_ge(s.m_var, 1)
                    nc.scalar.activation(std[:], ssq[:], ACT.Sqrt).then_inc(s.m_std, 1)
                    act.wait_ge(s.m_t, 1)
                    for k in range(KD):
                        nc.scalar.activation(hT[0][:, k, :], psum[k][:, 0:W], ACT.Copy, scale=w_ln[:, k : k + 1]).then_inc(s.m_hi, 1)
                    act.wait_ge(s.m_rt, 1)
                    nc.scalar.activation(rt[:], psum[2][0:n_col, 0:W], ACT.Copy).then_inc(s.m_rt_sb, 1)
                    act.wait_ge(s.m_step, 1 + CHUNK)
                    for t in range(CHUNK):
                        nc.scalar.activation(ex[:, t, :], logit[:, t, 0:EXPERTS], ACT.Exp, bias=nmax[:, t : t + 1], accum_out=total[:, t : t + 1]).then_inc(s.m_exp, 1)
                    nc.scalar.activation(gate[:], logit[:, :, EXPERTS], ACT.Exp, scale=-1.0).then_inc(s.m_exp, 1)

                    def high(f):
                        act.wait_ge(s.m_act, f + 1)
                        nc.scalar.activation(act_p[0][:, f, :], prod[:, f % 2, :], ACT.Copy).then_inc(s.m_ahi, 1)

                    for f in range(KF):
                        act.wait_ge(s.m_gate_up, f + 1)
                        if f >= 2:
                            act.wait_ge(s.m_act, f - 1)
                        nc.scalar.activation(silu[:, f % 2, :], psum[4 + f % 2][:, 0:W], ACT.Silu).then_inc(s.m_silu, 1)
                        if f:
                            high(f - 1)
                    high(KF - 1)

                @block.vector
                def _(dve):
                    dve.wait_ge(s.m_loaded, 16)
                    for t in range(CHUNK):
                        nc.vector.tensor_tensor_reduce(out=hn[:, t, :], in0=xt[:, t, :], in1=xt[:, t, :], scale=1.0, scalar=0.0,
                                                       op0=ALU.mult, op1=ALU.add, accum_out=ssq[:, t : t + 1]).then_inc(s.m_sq, 1)
                    dve.wait_ge(s.m_sq, CHUNK)
                    nc.vector.tensor_scalar(ssq[:], ssq[:], 1.0 / D, 1e-6, ALU.mult, ALU.add).then_inc(s.m_var, 1)
                    dve.wait_ge(s.m_std, 1)
                    nc.vector.reciprocal(rstd[:], std[:]).then_inc(s.m_rstd, 1)
                    dve.wait_ge(s.m_rstd, 1)
                    for t in range(CHUNK):
                        nc.vector.tensor_scalar(hn[:, t, :], xt[:, t, :], rstd[:, t : t + 1], None, ALU.mult).then_inc(s.m_norm, 1)
                    for k in range(KD):
                        dve.wait_ge(s.m_hi, k + 1)
                        nc.vector.scalar_tensor_tensor(hT[1][:, k, :], psum[k][:, 0:W], w_ln[:, k : k + 1],
                                                       hT[0][:, k, :].bitcast(F32), ALU.mult, ALU.subtract).then_inc(s.m_lo, 1)
                    dve.wait_ge(s.m_logits, 1)
                    nc.vector.tensor_copy(logit[:], psum[3][:, 0 : 16 * CHUNK].rearrange("p (t e) -> p t e", e=16)[:, :, 0:n_col]).then_inc(s.m_step, 1)
                    dve.wait_ge(s.m_step, 1)
                    for t in range(CHUNK):
                        nc.vector.tensor_reduce(nmax[:, t : t + 1], logit[:, t, 0:EXPERTS], AX_X, ALU.max, negate=True).then_inc(s.m_step, 1)
                    dve.wait_ge(s.m_exp, CHUNK + 1)
                    nc.vector.reciprocal(total[:], total[:]).then_inc(s.m_step, 1)
                    nc.vector.tensor_scalar(gate[:], gate[:], 1.0, None, ALU.add).then_inc(s.m_step, 1)
                    n = CHUNK + 3
                    dve.wait_ge(s.m_step, n)
                    nc.vector.reciprocal(gate[:], gate[:]).then_inc(s.m_step, 1)
                    for t in range(CHUNK):
                        nc.vector.tensor_scalar(ex[:, t, :], ex[:, t, :], total[:, t : t + 1], None, ALU.mult).then_inc(s.m_step, 1)
                    n += 1 + CHUNK
                    dve.wait_ge(s.m_step, n)
                    for t in range(CHUNK):
                        nc.vector.max(best[:, t, :], ex[:, t, :]).then_inc(s.m_step, 1)
                    n += CHUNK
                    dve.wait_ge(s.m_step, n)
                    for t in range(CHUNK):
                        nc.vector.max_index(where[:, t, :], best[:, t, :], ex[:, t, :]).then_inc(s.m_step, 1)
                    n += CHUNK
                    dve.wait_ge(s.m_step, n)
                    nc.vector.tensor_copy(wheref[:], where[:]).then_inc(s.m_step, 1)
                    nc.vector.tensor_copy(keep.weight[:, bass.ds(i * CHUNK, CHUNK), :], best[:, :, 0:TOP]).then_inc(s.m_step, 1)
                    n += 2
                    dve.wait_ge(s.m_step, n)
                    for t in range(CHUNK):
                        for j in range(TOP):
                            nc.vector.tensor_scalar(keep.hot[:, j, bass.ds(i * CHUNK + t, 1), :].rearrange("p a e -> p (a e)"), rows8[:],
                                                    wheref[:, t, j : j + 1], None, ALU.is_equal).then_inc(s.m_step, 1)

                    def low(f):
                        dve.wait_ge(s.m_ahi, f + 1)
                        nc.vector.tensor_tensor(act_p[1][:, f, :], prod[:, f % 2, :], act_p[0][:, f, :].bitcast(F32), ALU.subtract).then_inc(s.m_alo, 1)

                    for f in range(KF):
                        dve.wait_ge(s.m_silu, f + 1)
                        if f >= 2:
                            dve.wait_ge(s.m_alo, f - 1)
                        nc.vector.tensor_tensor(prod[:, f % 2, :], silu[:, f % 2, :], psum[4 + f % 2][:, W : 2 * W], ALU.mult).then_inc(s.m_act, 1)
                        if f:
                            low(f - 1)
                    low(KF - 1)
                    dve.wait_ge(s.m_resid, CHUNK)
                    for t in range(CHUNK):
                        dve.wait_ge(s.m_down, t + 1)
                        nc.vector.scalar_tensor_tensor(out_t[:, t, :], psum[6 + t][:], gate[:, t : t + 1], x2[:, t, :], ALU.mult, ALU.add).then_inc(s.m_out, 1)

                @block.gpsimd
                def _(pool):
                    pool.wait_ge(s.m_loaded, 16)
                    pool.wait_ge(s.m_x2_loaded, 16)
                    for t in range(CHUNK):
                        nc.gpsimd.tensor_tensor(x2[:, t, :], x2[:, t, :], xt[:, t, :], ALU.add).then_inc(s.m_resid, 1)

            s.clear()


def routed_phase(nc, s, c, psum, a, keep):

    NT, E = N_TILES, EXPERTS
    ctx = ExitStack()
    with ctx:
        sb = lambda name, shape, dt=F32: ctx.enter_context(nc.sbuf_tensor(f"routed_{name}", shape, dt))
        w_gu = sb("w_gu", [P, E, KD, 2 * FE])
        w_dn = sb("w_dn", [P, E, len(FE_K), D])
        w_ln = sb("w_ln", [P, KD])
        row = sb("row", [P, 4, D])
        below = sb("below", [P, P])
        allones = sb("allones", [P, P])
        hot = sb("hot", [P, NT, E])
        pre, tot, carry = sb("pre", [P, NT, E]), sb("tot", [P, NT, E]), sb("carry", [P, NT + 1, E])
        tiles_i, tiles_f = sb("tiles_i", [P, E], I32), sb("tiles_f", [P, E])
        begin = sb("begin", [P, E + 1])
        pick = sb("pick", [P, TOP, NT, E])
        slot_f, slot = sb("slot_f", [P, TOP, NT]), sb("slot", [P, TOP, NT], U32)
        count_t = sb("count_t", [P, SLOT_TILES])
        passed = sb("passed", [P, SLOT_TILES, E])
        owner_f, owner = sb("owner_f", [P, SLOT_TILES]), sb("owner", [P, SLOT_TILES], I32)
        hT = sb("hT", [P, 2, KD, P])
        silu, inner = sb("silu", [P, 2, FE]), sb("inner", [P, 2, FE])
        innerT = sb("innerT", [P, 2, len(FE_K), P])
        y = sb("y", [P, 2, D])

        row_here = (s.g_row0, s.g_row1, s.g_row2, s.g_row3)
        row_sent = (s.g_sent0, s.g_sent1, s.g_sent2, s.g_sent3)
        SLOT_STEPS = 4 + NT + 4 + E + 3 + 2 * TOP + 1

        def send(pool, i):
            pool.wait_ge(row_here[i % 4], 16 * (i // 4 + 1))
            if i == 0:
                pool.wait_ge(s.m_step, SLOT_STEPS)
            for j in range(TOP):
                pool.indirect_dma_start(a.slots, bass.IndirectOffsetOnAxis(ap=slot[:, j, i : i + 1], axis=0), row[:, i % 4, :], None
                                        ).then_inc(row_sent[i % 4], 16)

        with nc.Block() as block:

            @block.sync
            def _(sp):
                sp.dma_start(w_ln[:], a.w_ln.rearrange("(k p) -> p k", p=P), allow_slow_non_contiguous=True).then_inc(s.m_tab, 16)
                sp.dma_start(count_t[:], a.count_t.partition_broadcast(P)).then_inc(s.m_tab, 16)
                n = 0
                for e in range(E):
                    for dst, src in ((w_gu[:, e, :, 0:FE], a.w_gate[e]), (w_gu[:, e, :, FE : 2 * FE], a.w_up[e])):
                        sp.dma_start(dst, src.rearrange("(k p) n -> p k n", p=P)).then_inc(s.m_wt, 16)
                        n += 16
                    sp.dma_start(w_dn[:, e, 0:2, :], a.w_down[e][0 : 2 * P, :].rearrange("(k p) n -> p k n", p=P)).then_inc(s.m_wt, 16)
                    sp.dma_start(w_dn[0 : FE - 2 * P, e, 2, :], a.w_down[e][2 * P : FE, :]).then_inc(s.m_wt, 16)
                    n += 32
                sp.wait_ge(s.m_tab, 32)
                sp.wait_ge(s.m_wt, n)

            @block.gpsimd
            def _(pool):
                pool.memset(below[:], 1.0).then_inc(s.m_zero, 1)
                pool.memset(allones[:], 1.0).then_inc(s.m_zero, 1)
                pool.wait_ge(s.m_zero, 2)
                pool.affine_select(out=below[:], in_=below[:], compare_op=ALU.is_gt, fill=0.0, base=0,
                                   pattern=[[1, P]], channel_multiplier=-1).then_inc(s.m_zero, 1)
                for i in range(NT):
                    if i >= 4:
                        pool.wait_ge(row_sent[i % 4], 32 * (i // 4))
                    pool.dma_start(row[:, i % 4, :], a.rows[i * P : (i + 1) * P, :]).then_inc(row_here[i % 4], 16)
                    if i >= 2:
                        send(pool, i - 2)
                send(pool, NT - 2)
                send(pool, NT - 1)
                for m in range(4):
                    pool.wait_ge(row_sent[m], 32 * (NT // 4))

            @block.tensor
            def _(pe):
                pe.wait_ge(s.m_zero, 3)
                pe.wait_ge(s.m_step, 1)
                flat = hot[:].rearrange("p t e -> p (t e)")
                nc.tensor.matmul(psum[0][:, 0 : NT * E], below[:], flat, start=True, stop=True).then_inc(s.m_t, 1)
                nc.tensor.matmul(psum[1][:, 0 : NT * E], allones[:], flat, start=True, stop=True).then_inc(s.m_t, 1)

            @block.vector
            def _(dve):
                done = [0]

                def step(ins):
                    done[0] += 1
                    ins.then_inc(s.m_step, 1)
                    dve.wait_ge(s.m_step, done[0])

                step(nc.vector.tensor_tensor(hot[:], keep.hot[:, 0], keep.hot[:, 1], ALU.add))
                dve.wait_ge(s.m_t, 2)
                step(nc.vector.tensor_copy(pre[:].rearrange("p t e -> p (t e)"), psum[0][:, 0 : NT * E]))
                step(nc.vector.tensor_copy(tot[:].rearrange("p t e -> p (t e)"), psum[1][:, 0 : NT * E]))
                step(nc.vector.memset(carry[:, 0, :], 0.0))
                for t in range(NT):
                    step(nc.vector.tensor_tensor(carry[:, t + 1, :], carry[:, t, :], tot[:, t, :], ALU.add))
                step(nc.vector.tensor_scalar(tiles_i[:], carry[:, NT, :], float(P - 1), None, ALU.add))
                step(nc.vector.tensor_scalar(tiles_i[:], tiles_i[:], P.bit_length() - 1, None, ALU.arith_shift_right))
                step(nc.vector.tensor_copy(tiles_f[:], tiles_i[:]))
                step(nc.vector.memset(begin[:, 0:1], 0.0))
                for e in range(E):
                    step(nc.vector.tensor_tensor(begin[:, e + 1 : e + 2], begin[:, e : e + 1], tiles_f[:, e : e + 1], ALU.add))
                step(nc.vector.tensor_tensor(pre[:], pre[:], carry[:, 0:NT, :], ALU.add))
                step(nc.vector.tensor_scalar(tiles_f[:], begin[:, 0:E], float(P), None, ALU.mult))
                step(nc.vector.tensor_tensor(pre[:], pre[:], tiles_f[:].unsqueeze(1).to_broadcast([P, NT, E]), ALU.add))
                for j in range(TOP):
                    step(nc.vector.tensor_tensor(pick[:, j], keep.hot[:, j], pre[:], ALU.mult))
                    step(nc.vector.tensor_reduce(slot_f[:, j, :], pick[:, j], AX_X, ALU.add))
                done[0] += 1
                nc.vector.tensor_copy(slot[:], slot_f[:]).then_inc(s.m_step, 1)
                dve.wait_ge(s.m_step, done[0])
                assert done[0] == SLOT_STEPS
                dve.wait_ge(s.m_tab, 32)
                step(nc.vector.tensor_tensor(passed[:], count_t[:].unsqueeze(2).to_broadcast([P, SLOT_TILES, E]),
                                             begin[:, 1 : E + 1].unsqueeze(1).to_broadcast([P, SLOT_TILES, E]), ALU.is_ge))
                step(nc.vector.tensor_reduce(owner_f[:], passed[:], AX_X, ALU.add))
                step(nc.vector.tensor_scalar(owner[:], owner_f[:], float(E - 1), None, ALU.min))

        s.clear()

        def store(sp, t):
            sp.wait_ge(s.e_ysb, t + 1)
            sp.dma_start(a.results[bass.ds((i * PER + t) * P, P), :], y[:, t % 2, :]).then_inc((s.e_st0, s.e_st1)[t % 2], 16)

        def result(act, t):
            act.wait_ge(s.e_y, t + 1)
            if t >= 2:
                act.wait_ge((s.e_st0, s.e_st1)[t % 2], 16 * (t // 2))
            nc.scalar.activation(y[:, t % 2, :], psum[6 + t % 2][:], ACT.Copy).then_inc(s.e_ysb, 1)

        def put(sp, t):
            sp.wait_ge(s.m_out, t + 1)
            sp.dma_start(a.out[t * P : (t + 1) * P, :], y[:, t % 2, :]).then_inc((s.e_st0, s.e_st1)[t % 2], 16)

        PER = 13
        with nc.Fori(0, SLOT_TILES // PER) as i:
            with nc.Block() as block:

                @block.sync
                def _(sp):
                    for t in range(PER):
                        if t >= 4:
                            sp.wait_ge(s.e_t, t - 3)
                        sp.dma_start(row[:, t % 4, :], a.slots[bass.ds((i * PER + t) * P, P), :]).then_inc((s.e_ld0, s.e_ld1, s.m_ld0, s.m_ld1)[t % 4], 16)
                        if t >= 2:
                            store(sp, t - 2)
                    store(sp, PER - 2)
                    store(sp, PER - 1)
                    for m, st in enumerate((s.e_st0, s.e_st1)):
                        sp.wait_ge(st, 16 * len(range(m, PER, 2)))

                @block.tensor
                def _(pe):
                    experts = {}

                    def front(t):
                        pe.wait_ge((s.e_ld0, s.e_ld1, s.m_ld0, s.m_ld1)[t % 4], 16 * (t // 4 + 1))
                        if t >= 1:
                            pe.wait_ge(s.e_hT, t)
                        for k in range(KD):
                            last = nc.tensor.transpose(psum[0][:, k * P : (k + 1) * P], row[:, t % 4, k * P : (k + 1) * P], c.ident[:])
                        last.then_inc(s.e_t, 1)

                    def gate_up(t):
                        e = pe.value_load(owner[0:1, bass.ds(i * PER + t, 1)], min_val=0, max_val=E - 1)
                        experts[t % 2] = e
                        pe.wait_ge(s.e_hT, t + 1)
                        if t >= 2:
                            pe.wait_ge(s.e_a, t - 1)
                        for half in range(2):
                            for k in range(KD):
                                rhs = w_gu[:, bass.ds(e, 1), k, half * FE : (half + 1) * FE].rearrange("p a n -> p (a n)")
                                last = nc.tensor.matmul(psum[1 + 2 * (t % 2) + half][:, 0:FE], hT[:, t % 2, k, :], rhs, start=k == 0, stop=k == KD - 1)
                        last.then_inc(s.e_g, 1)

                    def turn(t):
                        pe.wait_ge(s.e_a, t + 1)
                        if t >= 1:
                            pe.wait_ge(s.e_aT, t)
                        for n, (k0, kn) in enumerate(FE_K):
                            last = nc.tensor.transpose(psum[5][0:kn, n * P : (n + 1) * P], inner[:, t % 2, k0 : k0 + kn], c.ident[:])
                        last.then_inc(s.e_at, 1)

                    def down(t):
                        pe.wait_ge(s.e_aT, t + 1)
                        if t >= 2:
                            pe.wait_ge(s.e_ysb, t - 1)
                        for n, (k0, kn) in enumerate(FE_K):
                            rhs = w_dn[0:kn, bass.ds(experts[t % 2], 1), n, :].rearrange("p a n -> p (a n)")
                            last = nc.tensor.matmul(psum[6 + t % 2][:], innerT[0:kn, t % 2, n, :], rhs, start=n == 0, stop=n == len(FE_K) - 1)
                        last.then_inc(s.e_y, 1)

                    front(0)
                    for t in range(PER):
                        if t + 1 < PER:
                            front(t + 1)
                        if t:
                            turn(t - 1)
                            down_e = experts[(t - 1) % 2]
                        gate_up(t)
                        if t:
                            experts[(t - 1) % 2] = down_e
                            down(t - 1)
                    turn(PER - 1)
                    down(PER - 1)

                @block.scalar
                def _(act):
                    for t in range(PER):
                        act.wait_ge(s.e_g, t + 1)
                        if t >= 2:
                            act.wait_ge(s.e_a, t - 1)
                        nc.scalar.activation(silu[:, t % 2], psum[1 + 2 * (t % 2)][:, 0:FE], ACT.Silu).then_inc(s.e_s, 1)
                        if t:
                            result(act, t - 1)
                    result(act, PER - 1)

                @block.vector
                def _(dve):
                    def columns(t):
                        dve.wait_ge(s.e_t, t + 1)
                        if t >= 2:
                            dve.wait_ge(s.e_g, t - 1)
                        nc.vector.tensor_tensor(hT[:, t % 2], psum[0][:].rearrange("p (k n) -> p k n", k=KD),
                                                w_ln[:].unsqueeze(2).to_broadcast([P, KD, P]), ALU.mult).then_inc(s.e_hT, 1)

                    columns(0)
                    for t in range(PER):
                        if t + 1 < PER:
                            columns(t + 1)
                        dve.wait_ge(s.e_s, t + 1)
                        if t >= 2:
                            dve.wait_ge(s.e_at, t - 1)
                        nc.vector.tensor_tensor(inner[:, t % 2], silu[:, t % 2], psum[2 + 2 * (t % 2)][:, 0:FE], ALU.mult).then_inc(s.e_a, 1)
                        dve.wait_ge(s.e_at, t + 1)
                        if t >= 2:
                            dve.wait_ge(s.e_y, t - 1)
                        nc.vector.tensor_copy(innerT[:, t % 2, 0:2], psum[5][:, 0 : 2 * P].rearrange("p (k n) -> p k n", k=2)).then_inc(s.m_step, 1)
                        kn = FE_K[2][1]
                        nc.vector.tensor_copy(innerT[0:kn, t % 2, 2], psum[5][0:kn, 2 * P : 3 * P]).then_inc(s.e_aT, 1)

            s.clear()

        with nc.Block() as block:
            NB = 2
            got = row[:].rearrange("p (n j) d -> p n j d", n=NB)
            baset, res = y, innerT[:].rearrange("p a b n -> p (a b n)")[:, 0:D]

            @block.gpsimd
            def _(pool):
                for t in range(NT):
                    if t >= NB:
                        pool.wait_ge(s.m_out, t - NB + 1)
                    for j in range(TOP):
                        pool.indirect_dma_start(got[:, t % NB, j, :], None, a.results, bass.IndirectOffsetOnAxis(ap=slot[:, j, t : t + 1], axis=0)
                                                ).then_inc((s.g_got0, s.g_got1)[t % NB], 16)

            @block.sync
            def _(sp):
                for t in range(NT):
                    if t >= NB:
                        sp.wait_ge((s.e_st0, s.e_st1)[t % 2], 16 * (t // 2))
                    sp.dma_start(baset[:, t % 2, :], a.base[t * P : (t + 1) * P, :]).then_inc((s.m_ld0, s.m_ld1)[t % 2], 16)
                    if t >= 1:
                        put(sp, t - 1)
                put(sp, NT - 1)
                for st in (s.e_st0, s.e_st1):
                    sp.wait_ge(st, 16 * (NT // 2))

            @block.vector
            def _(dve):
                for t in range(NT):
                    dve.wait_ge((s.m_ld0, s.m_ld1)[t % 2], 16 * (t // 2 + 1))
                    dve.wait_ge((s.g_got0, s.g_got1)[t % NB], 32 * (t // NB + 1))
                    if t >= 1:
                        dve.wait_ge(s.m_out, t)
                    nc.vector.scalar_tensor_tensor(res, got[:, t % NB, 0, :], keep.weight[:, t, 0:1], baset[:, t % 2, :], ALU.mult, ALU.add).then_inc(s.m_act, 1)
                    dve.wait_ge(s.m_act, t + 1)
                    nc.vector.scalar_tensor_tensor(baset[:, t % 2, :], got[:, t % NB, 1, :], keep.weight[:, t, 1:2], res, ALU.mult, ALU.add).then_inc(s.m_out, 1)

        s.clear()


def zero_slots(nc, s, slots):
    with nc.sbuf_tensor("zeros", [P, D], F32) as zeros, nc.Block() as block:

        @block.vector
        def _(dve):
            nc.vector.memset(zeros[:], 0.0).then_inc(s.m_zero, 1)

        @block.sync
        def _(sp):
            sp.wait_ge(s.m_zero, 1)
            for t in range(SLOT_TILES):
                sp.dma_start(slots[t * P : (t + 1) * P, :], zeros[:]).then_inc(s.m_stored, 16)
            sp.wait_ge(s.m_stored, 16 * SLOT_TILES)

    s.clear()


ROPE_HEAD, ROPE_THETA = 32, 1.0e6
AXIAL_HEAD, AXIAL_BASE = 16, 10000.0


def shape_constants():
    inv = (np.float32(1.0) / np.float32(ROPE_THETA) ** (np.arange(0, ROPE_HEAD, 2, dtype=np.float32) / ROPE_HEAD)).astype(np.float32)
    angle = (inv[:, None] * np.arange(S, dtype=np.float32)[None, :]).astype(np.float32)
    cos, sin = np.cos(angle), np.sin(angle)
    half = AXIAL_HEAD // 4
    base = (np.float32(AXIAL_BASE) ** (-np.arange(half, dtype=np.float32) / half)).astype(np.float32)
    freq, sign = np.zeros((2, P), np.float32), np.zeros((P, 1), np.float32)
    for r in range(P):
        axis, rest = divmod(r % AXIAL_HEAD, AXIAL_HEAD // 2)
        freq[axis, r] = base[rest // 2]
        sign[r, 0] = -1.0 if r % 2 == 0 else 1.0
    return {
        "rope_cos": np.tile(cos, (2 * P // ROPE_HEAD, 1)),
        "rope_sin": np.tile(np.concatenate([-sin, sin]), (P // ROPE_HEAD, 1)),
        "axial_freq": freq,
        "axial_sign": sign,
        "expert_number": np.arange(EXPERTS, dtype=np.float32),
        "tile_number": np.arange(SLOT_TILES, dtype=np.float32),
    }


def build(nc, i, out):

    rows = lambda t: t.rearrange("b s d -> (b s) d")
    dram = lambda name, shape: nc.dram_tensor(name, shape, F32, kind="Internal").ap()
    x1, x2, x3 = (dram(n, (B * S, D)) for n in ("x1", "x2", "x3"))
    scratch = dram("qk_parts", (2, 2, D, S))
    normed, base = dram("normed", (B * S, D)), dram("base", (B * S, D))
    slots, results = dram("slots", (SLOTS, D)), dram("results", (SLOTS, D))
    ctx = ExitStack()
    with ctx:
        sb = lambda name, shape, dt=F32: ctx.enter_context(nc.sbuf_tensor(name, shape, dt))
        c = Args(ident=sb("ident", [P, P]), pick=sb("pick", [P, HEADS_AT_ONCE]),
                 ones=sb("ones", [P, 32]), identb=sb("identb", [P, P], BF16), maskqb=sb("maskqb", [P, P], BF16), maskkb=sb("maskkb", [P, P], BF16))
        psum = [ctx.enter_context(nc.psum_tensor(f"bank{n}", [P, D], F32)) for n in range(8)]
        s = Signals(nc, SIGNALS + MOE_SIGNALS)
        make_constants(nc, s, c)
        zero_slots(nc, s, slots)
        qkv = i["L0_attn_w_qkv"]
        attention_phase(nc, s, c, psum, Args(
            kind="first", lead=10, x=rows(i["x"]), out=x1, scratch=scratch,
            wq=(qkv, 0), wk=(qkv, 1), wv=(qkv, 2), wo=(i["L0_attn_w_out"], 0)))
        wkv = i["L0_xattn_Wkv"]
        attention_phase(nc, s, c, psum, Args(
            kind="cross", lead=10, x=x1, out=x2, scratch=scratch, ctx=rows(i["ctx_1024"]), pos=rows(i["fside_BxSx2_0"]),
            wq=(i["L0_xattn_Wq"], 0), wk=(wkv, 0), wv=(wkv, 1), wo=(i["L0_xattn_Wout"], 0), bo=i["L0_xattn_bout"],
            freq=i["axial_freq"], sign=i["axial_sign"]))
        attention_phase(nc, s, c, psum, Args(
            kind="rotary", lead=10, x=x2, out=x3, scratch=scratch,
            wq=(i["L0_ffn_wq"], 0), wk=(i["L0_ffn_wk"], 0), wv=(i["L0_ffn_wv"], 0), wo=(i["L0_ffn_wo"], 0),
            bq=i["L0_ffn_bq"], bk=i["L0_ffn_bk"], bv=i["L0_ffn_bv"], w_ln=i["L0_ffn_w_ln1"],
            cos=i["rope_cos"], sin=i["rope_sin"]))
        keep = Args(weight=sb("top_weight", [P, N_TILES, TOP]), hot=sb("top_hot", [P, TOP, N_TILES, EXPERTS]))
        shared_phase(nc, s, c, psum, Args(
            x3=x3, x2=x2, rows=normed, base=base, w_ln=i["L0_ffn_w_ln2"], w_gate=i["L0_ffn_w_sh_gate"], w_up=i["L0_ffn_w_sh_up"],
            w_down=i["L0_ffn_w_sh_down"], w_router=i["L0_ffn_w_router"], w_eg=i["L0_ffn_w_sh_eg"], count8=i["expert_number"]), keep)
        routed_phase(nc, s, c, psum, Args(
            rows=normed, base=base, slots=slots, results=results, w_ln=i["L0_ffn_w_ln2"], w_gate=i["L0_ffn_w_gate_e"],
            w_up=i["L0_ffn_w_up_e"], w_down=i["L0_ffn_w_down_e"], count_t=i["tile_number"], out=rows(out)), keep)


def kernel(**inputs):
    import concourse.bacc as bacc
    from concourse.bass_utils import run_bass_kernel_spmd

    nc = bacc.Bacc("TRN2", target_bir_lowering=False, num_devices=1)
    arrays, args = {}, {}
    for name, value in [*inputs.items(), *shape_constants().items()]:
        array = np.ascontiguousarray(value)
        arrays[f"in_{name}"] = array
        args[name] = nc.dram_tensor(f"in_{name}", array.shape, mybir.dt.from_np(array.dtype), kind="ExternalInput").ap()
    out = nc.dram_tensor("out_x", (B, S, D), F32, kind="ExternalOutput").ap()
    build(nc, args, out)
    result = run_bass_kernel_spmd(nc, [arrays], core_ids=[0])
    return result.results[0]["out_x"]
```

```python
from contextlib import ExitStack

import numpy as np

import concourse.bass as bass
import concourse.mybir as mybir

F32 = mybir.dt.float32
F32R = mybir.dt.float32r
BF16 = mybir.dt.bfloat16
I32 = mybir.dt.int32
U32 = mybir.dt.uint32
ACT = mybir.ActivationFunctionType
ALU = mybir.AluOpType
AX_X = mybir.AxisListType.X

P = 128
B, S, D = 4, 512, 512
TT = S // P
KD = D // P
CTX = 256
MASKED = -1.0e30
HEADS_AT_ONCE = 4
STACK_SLOTS = 4
PROB_SLOTS = 8
MAX_ROW = 96
STACK_ROWS = MAX_ROW + 2 * HEADS_AT_ONCE


def hi_lo_passes(n_k):
    return [(k, a, b) for k in range(n_k) for a, b in ((0, 0), (0, 1), (1, 0))]


class Args:

    def __init__(self, **items):
        self.items = items

    def __getattr__(self, name):
        return self.items[name]


class Signals:

    def __init__(self, nc, names):
        self.nc = nc
        self.of = {n: nc.alloc_semaphore(n) for n in names}
        nums = sorted(s.num for s in self.of.values())
        assert nums == list(range(nums[0], nums[-1] + 1))
        self.range = range(nums[0], nums[-1] + 1)

    def __getattr__(self, name):
        return self.of[name]

    def clear(self):
        self.nc.all_engine_barrier(sems_to_clear=self.range)


SIGNALS = [
    "raw_loaded0", "raw_loaded1", "hi_made", "lo_made", "table_loaded", "table_made", "const_made",
    "x_loaded0", "x_loaded1", "ctx_loaded", "pos_loaded", "ln_step", "var_ready", "std_ready", "norm_ready", "rms_ready",
    "rms_std", "transposed", "hT_hi", "hT_lo", "proj_done", "v_made", "v_stored0", "v_stored1", "h1_stored",
    "straight_made", "swap_made", "cos_made", "sin_made", "rotated", "parts_hi", "parts_lo", "qk_stored0", "qk_stored1",
    "pos_t", "pos_sb", "angles", "ang_step", "trig_made",
    "stack_loaded0", "stack_loaded1", "stack_loaded2", "stack_loaded3", "v_loaded0", "v_loaded1", "scores_ready", "max_done",
    "max_split", "max_transposed", "max_rows", "max_loaded", "scoresT_ready", "exp_done", "pv_done", "flip",
    "recip_made", "scaled", "attn_out", "attn_hi", "attn_lo", "attn_packed0", "attn_packed1", "out_proj", "out_made",
    "out_stored0", "out_stored1", "residual_made",
]


def make_constants(nc, s, c):
    with (
        nc.sbuf_tensor("maskq", [P, P], F32) as maskq,
        nc.sbuf_tensor("maskk", [P, P], F32) as maskk,
        nc.Block() as block,
    ):

        @block.gpsimd
        def _(pool):
            pool.memset(c.ident[:], 0.0).then_inc(s.const_made, 1)
            pool.memset(maskq[:], 0.0).then_inc(s.const_made, 1)
            pool.memset(maskk[:], 0.0).then_inc(s.const_made, 1)
            pool.memset(c.pick[:], 0.0).then_inc(s.const_made, 1)
            pool.wait_ge(s.const_made, 4)
            diag = dict(base=0, pattern=[[-1, P]], channel_multiplier=1)
            pool.affine_select(out=c.ident[:], in_=c.ident[:], compare_op=ALU.not_equal, fill=1.0,
                               **diag).then_inc(s.const_made, 1)
            pool.affine_select(out=maskq[:], in_=maskq[:], compare_op=ALU.is_ge, fill=MASKED,
                               **diag).then_inc(s.const_made, 1)
            pool.affine_select(out=maskk[:], in_=maskk[:], compare_op=ALU.is_ge, fill=MASKED,
                               base=0, pattern=[[1, P]], channel_multiplier=-1).then_inc(s.const_made, 1)
            for n, base in enumerate((0, -HEADS_AT_ONCE)):
                pool.wait_ge(s.const_made, 7 + n)
                pool.affine_select(out=c.pick[MAX_ROW:STACK_ROWS, :], in_=c.pick[MAX_ROW:STACK_ROWS, :],
                                   compare_op=ALU.not_equal, fill=1.0, base=base,
                                   pattern=[[-1, HEADS_AT_ONCE]], channel_multiplier=1).then_inc(s.const_made, 1)

        @block.vector
        def _(dve):
            nc.vector.memset(c.ones[:], 1.0).then_inc(s.table_made, 1)
            dve.wait_ge(s.const_made, 9)
            nc.vector.tensor_copy(c.identb[:], c.ident[:]).then_inc(s.table_made, 1)
            nc.vector.tensor_copy(c.maskqb[:], maskq[:]).then_inc(s.table_made, 1)
            nc.vector.tensor_copy(c.maskkb[:], maskk[:]).then_inc(s.table_made, 1)

    s.clear()


def split_weights(nc, s, jobs, raw):

    def staged(n, j):
        k, m = j[0].shape[1], j[0].shape[2]
        return raw[:, n % 2, 0 : k * m].rearrange("p (k n) -> p k n", k=k)

    with nc.Block() as block:

        @block.sync
        def _(sp):
            for n, j in enumerate(jobs):
                if n >= 2:
                    sp.wait_ge(s.hi_made, n - 1)
                    sp.wait_ge(s.lo_made, n - 1)
                sp.dma_start(staged(n, j), j[0], allow_slow_non_contiguous=True).then_inc((s.raw_loaded0, s.raw_loaded1)[n % 2], 16)

        @block.scalar
        def _(act):
            for n, j in enumerate(jobs):
                act.wait_ge((s.raw_loaded0, s.raw_loaded1)[n % 2], 16 * (n // 2 + 1))
                nc.scalar.activation(j[1], staged(n, j), ACT.Copy).then_inc(s.hi_made, 1)

        @block.vector
        def _(dve):
            for n, j in enumerate(jobs):
                dve.wait_ge(s.hi_made, n + 1)
                nc.vector.tensor_tensor(j[2], staged(n, j), j[1].bitcast(F32), ALU.subtract).then_inc(s.lo_made, 1)

    s.clear()


class Attention:

    def __init__(self, kind):
        self.kind = kind
        self.cross, self.rotary = kind == "cross", kind == "rotary"
        self.causal, self.rope = not self.cross, kind != "first"
        self.dh = 16 if self.cross else 32
        self.heads = D // self.dh
        self.groups = self.heads // HEADS_AT_ONCE
        self.scale = float(self.dh) ** -0.5
        self.n_kv = (CTX if self.cross else D) // P
        self.v_width = 2 * D if self.cross else D
        self.n_in = KD + (self.n_kv if self.cross else 0)


def projection_phase(nc, s, c, psum, a):
    t = Attention(a.kind)
    cross, rotary, rope = t.cross, t.rotary, t.rope
    BODY = a.body
    ctx = ExitStack()
    with ctx:
        sb = lambda name, shape, dt=F32: ctx.enter_context(nc.sbuf_tensor(f"{a.kind}_p_{name}", shape, dt))
        n_w = KD + 2 * t.n_kv
        w = [sb("w_hi", [P, n_w, D], F32R), sb("w_lo", [P, n_w, D], F32R)]
        at_w = {"q": 0, "k": KD, "v": KD + t.n_kv}
        raw = sb("raw", [P, 2, KD * D])
        xt = sb("xt", [P, 2, TT, D])
        h1 = sb("h1", [P, TT, D]) if rotary else None
        hn = sb("hn", [P, TT, D])
        hT = [sb("hT_hi", [P, 1 if cross else 2, t.n_in, S], F32R), sb("hT_lo", [P, 1 if cross else 2, t.n_in, S], F32R)]
        IN_SLOTS = 1 if cross else 2
        v = sb("v", [P, 2, t.v_width])
        parts = sb("parts", [P, 2, 2, S], F32R)
        if rope:
            straight, swapped, turned = sb("straight", [P, 2, S]), sb("swapped", [P, S]), sb("turned", [P, 2, S])
            cos_t, sin_t = sb("cos_t", [P, S]), sb("sin_t", [P, S])
        stats, mv = sb("stats", [P, TT, 6]), sb("mv", [P, TT, 2])
        std, rstd = sb("std", [P, TT]), sb("rstd", [P, TT])
        ssq, rms = sb("ssq", [P, TT]), sb("rms", [P, TT])
        if rotary:
            w_ln, bias_raw, bias_q = sb("w_ln", [P, KD]), sb("bias_raw", [P, 2, KD]), sb("bias_q", [P, KD])
            bv_row = sb("bv_row", [P, D])
        if cross:
            freq, sign = sb("freq", [2, P]), sb("sign", [P, 1])
            ctx_t, pos = sb("ctx_t", [P, TT, CTX]), sb("pos", [P, TT, 2])
            posT, turns = sb("posT", [2, S]), sb("turns", [P, S])
            ang = [sb("ang0", [P, S]), sb("ang1", [P, S])]

        cols = lambda m, n: m.rearrange("(k p) n -> p k n", p=P)[:, :, n * D : (n + 1) * D]
        jobs = []
        for what, src in (("v", a.wv), ("q", a.wq), ("k", a.wk)):
            n_k = KD if what == "q" else t.n_kv
            jobs.append((cols(*src), *(x[:, at_w[what] : at_w[what] + n_k, :] for x in w)))
        split_weights(nc, s, jobs, raw)

        with nc.Block() as block:

            @block.sync
            def _(sp):
                tables = []
                if rotary:
                    tables = [(cos_t[:], a.cos), (sin_t[:], a.sin), (w_ln[:], a.w_ln.rearrange("(k p) -> p k", p=P)),
                              (bias_raw[:, 0, :], a.bq.rearrange("(k p) -> p k", p=P)),
                              (bias_raw[:, 1, :], a.bk.rearrange("(k p) -> p k", p=P)), (bv_row[:], a.bv.partition_broadcast(P))]
                if cross:
                    tables = [(freq[:], a.freq), (sign[:], a.sign)]
                for dst, src in tables:
                    sp.dma_start(dst, src, allow_slow_non_contiguous=True).then_inc(s.table_loaded, 16)
                if tables:
                    sp.wait_ge(s.table_loaded, 16 * len(tables))

            @block.vector
            def _(dve):
                if rotary:
                    dve.wait_ge(s.table_loaded, 6 * 16)
                    nc.vector.tensor_scalar(bias_q[:], bias_raw[:, 0, :], t.scale, None, ALU.mult).then_inc(s.table_made, 1)

            @block.gpsimd
            def _(pool):
                if cross:
                    for slot in range(2):
                        pool.memset(v[:, slot].rearrange("p (h two d) -> p h two d", two=2, d=t.dh)[:, :, 1, :], 1.0).then_inc(s.const_made, 1)

        s.clear()

        order = ([("pos", 0), ("angle", 0)] if cross else []) + [("v", m) for m in range(TT)]
        order += [(what, m) for m in range(KD) for what in "qk"]
        ring = [(bi, what, m) for bi in range(BODY) for what, m in order]
        n_v, n_qk = TT, 2 * KD
        freed, count = [], {}
        for bi, what, m in ring:
            name = {"pos": "pos_sb", "angle": "ang_step", "v": "v_made"}.get(what, "straight_made" if rope else "parts_lo")
            count[name] = count.get(name, 0) + 1
            freed.append(("ang_step", 12 * bi + 1) if what == "angle" else (name, count[name]))
        qk_stored, v_stored = (s.qk_stored0, s.qk_stored1), (s.v_stored0, s.v_stored1)
        x_loaded = (s.x_loaded0, s.x_loaded1)

        with nc.Fori(0, B // BODY) as loop:
            rows = lambda m, bi: m[bass.ds((loop * BODY + bi) * S, S), :].rearrange("(t p) d -> p t d", p=P)
            with nc.Block() as block:

                @block.sync
                def _(sp):
                    def load(bi):
                        if bi >= 2:
                            sp.wait_ge(s.norm_ready, TT * (bi - 1))
                        sp.dma_start(xt[:, bi % 2], rows(a.x, bi)).then_inc(x_loaded[bi % 2], 16)
                        if cross:
                            if bi >= 1:
                                sp.wait_ge(s.transposed, 2 * bi)
                                sp.wait_ge(s.pos_t, bi)
                            sp.dma_start(ctx_t[:], rows(a.ctx, bi)).then_inc(s.ctx_loaded, 16)
                            sp.dma_start(pos[:], rows(a.pos, bi)).then_inc(s.pos_loaded, 16)

                    load(0)
                    for bi in range(BODY):
                        if bi + 1 < BODY:
                            load(bi + 1)
                        for m in range(TT):
                            n = bi * TT + m
                            sp.wait_ge(s.v_made, n + 1)
                            sp.dma_start(a.v[bass.ds((loop * BODY + bi) * S + m * P, P), :], v[:, n % 2]).then_inc(v_stored[n % 2], 16)
                            if m == 0 and rotary:
                                sp.dma_start(rows(a.h1, bi), h1[:]).then_inc(s.h1_stored, 16)
                        for i in range(n_qk):
                            n = bi * n_qk + i
                            sp.wait_ge(s.parts_hi, n + 1)
                            sp.wait_ge(s.parts_lo, n + 1)
                            dst = a.scratch[bass.ds(loop * BODY + bi, 1), i % 2, (i // 2) * P : (i // 2 + 1) * P]
                            sp.dma_start(dst.rearrange("a p x n -> p (a x) n"), parts[:, n % 2].bitcast(F32)).then_inc(qk_stored[n % 2], 16)
                    for st in v_stored:
                        sp.wait_ge(st, 16 * (BODY * TT // 2))
                    for st in qk_stored:
                        sp.wait_ge(st, 16 * (BODY * n_qk // 2))
                    if rotary:
                        sp.wait_ge(s.h1_stored, 16 * BODY)

                @block.tensor
                def _(pe):
                    def turn_in(bi):
                        if bi:
                            pe.wait_ge(s.hT_lo, t.n_in * bi)
                        for m in range(TT):
                            pe.wait_ge(s.norm_ready, bi * TT + m + 1)
                            for k in range(KD):
                                last = nc.tensor.transpose(psum[k][:, m * P : (m + 1) * P], hn[:, m, k * P : (k + 1) * P], c.ident[:])
                        last.then_inc(s.transposed, 1)
                        if cross:
                            pe.wait_ge(s.ctx_loaded, 16 * (bi + 1))
                            for k in range(t.n_kv):
                                for m in range(TT):
                                    last = nc.tensor.transpose(psum[KD + k][:, m * P : (m + 1) * P], ctx_t[:, m, k * P : (k + 1) * P], c.ident[:])
                            last.then_inc(s.transposed, 1)

                    turn_in(0)
                    for n, (bi, what, m) in enumerate(ring):
                        bank = psum[6 + n % 2]
                        if n >= 2:
                            name, value = freed[n - 2]
                            pe.wait_ge(s.of[name], value)
                        slot = bi % IN_SLOTS
                        if what == "pos":
                            pe.wait_ge(s.pos_loaded, 16 * (bi + 1))
                            for m_ in range(TT):
                                last = nc.tensor.transpose(bank[0:2, m_ * P : (m_ + 1) * P], pos[:, m_, :], c.ident[:])
                            last.then_inc(s.pos_t, 1)
                            continue
                        if what == "angle":
                            pe.wait_ge(s.pos_sb, bi + 1)
                            nc.tensor.matmul(bank[:], freq[:], posT[:], start=True, stop=True).then_inc(s.angles, 1)
                            continue
                        if (what, m) == ("v", 0):
                            pe.wait_ge(s.hT_hi, t.n_in * (bi + 1))
                            pe.wait_ge(s.hT_lo, t.n_in * (bi + 1))
                        nk, first = (t.n_kv if what in "kv" else KD), (KD if cross and what in "kv" else 0)
                        steps = hi_lo_passes(nk)
                        for i, (k, pa, pb) in enumerate(steps):
                            if what == "v":
                                lhs, rhs = hT[pa][:, slot, first + k, m * P : (m + 1) * P], w[pb][:, at_w[what] + k, :]
                            else:
                                lhs, rhs = w[pa][:, at_w[what] + k, m * P : (m + 1) * P], hT[pb][:, slot, first + k, :]
                            last = nc.tensor.matmul(bank[:], lhs, rhs, start=i == 0, stop=i == len(steps) - 1)
                        last.then_inc(s.proj_done, 1)
                        if not cross and (what, m) == ("v", TT - 1) and bi + 1 < BODY:
                            turn_in(bi + 1)
                        if cross and (what, m) == ("k", KD - 1) and bi + 1 < BODY:
                            turn_in(bi + 1)

                def hT_high(act, bi):
                    if bi >= IN_SLOTS:
                        act.wait_ge(s.proj_done, (n_v + n_qk) * (bi - IN_SLOTS + 1))
                    for k in range(t.n_in):
                        act.wait_ge(s.transposed, (2 * bi + (1 if k < KD else 2)) if cross else bi + 1)
                        dst, src = hT[0][:, bi % IN_SLOTS, k, :], psum[k][:]
                        if rotary:
                            nc.scalar.activation(dst, src, ACT.Copy, scale=w_ln[:, k : k + 1]).then_inc(s.hT_hi, 1)
                        else:
                            nc.scalar.activation(dst, src, ACT.Copy).then_inc(s.hT_hi, 1)

                def hT_low(dve, bi):
                    for k in range(t.n_in):
                        dve.wait_ge(s.hT_hi, t.n_in * bi + k + 1)
                        dst, src, high = hT[1][:, bi % IN_SLOTS, k, :], psum[k][:], hT[0][:, bi % IN_SLOTS, k, :].bitcast(F32)
                        if rotary:
                            nc.vector.scalar_tensor_tensor(dst, src, w_ln[:, k : k + 1], high, ALU.mult, ALU.subtract).then_inc(s.hT_lo, 1)
                        else:
                            nc.vector.tensor_tensor(dst, src, high, ALU.subtract).then_inc(s.hT_lo, 1)

                @block.scalar
                def _(act):
                    def roots(bi):
                        act.wait_ge(s.var_ready, bi + 1)
                        nc.scalar.activation(std[:], mv[:, :, 1], ACT.Sqrt).then_inc(s.std_ready, 1)
                        if rotary:
                            act.wait_ge(s.rms_ready, bi + 1)
                            nc.scalar.activation(rms[:], ssq[:], ACT.Sqrt).then_inc(s.rms_std, 1)

                    def high(n):
                        act.wait_ge(s.rotated, n + 1)
                        if n >= 2:
                            act.wait_ge(qk_stored[n % 2], 16 * (n // 2))
                        nc.scalar.activation(parts[:, n % 2, 0], turned[:, n % 2], ACT.Copy).then_inc(s.parts_hi, 1)

                    roots(0)
                    hT_high(act, 0)
                    done = 0
                    for n, (bi, what, m) in enumerate(ring):
                        bank = psum[6 + n % 2]
                        if what == "pos":
                            act.wait_ge(s.pos_t, bi + 1)
                            if bi:
                                act.wait_ge(s.angles, bi)
                            nc.scalar.activation(posT[:], bank[0:2, :], ACT.Copy).then_inc(s.pos_sb, 1)
                            continue
                        if what == "angle":
                            if bi + 1 < BODY:
                                roots(bi + 1)
                            act.wait_ge(s.ang_step, 12 * (bi + 1))
                            if bi:
                                act.wait_ge(s.rotated, n_qk * bi)
                            nc.scalar.activation(sin_t[:], ang[0][:], ACT.Sin, scale=sign[:, 0:1]).then_inc(s.trig_made, 1)
                            nc.scalar.activation(cos_t[:], ang[1][:], ACT.Sin).then_inc(s.trig_made, 1)
                            continue
                        done += 1
                        if what == "v":
                            i = bi * TT + m
                            if m == 0 and not cross and bi + 1 < BODY:
                                roots(bi + 1)
                            if not rotary:
                                act.wait_ge(s.proj_done, done)
                                if i >= 2:
                                    act.wait_ge(v_stored[i % 2], 16 * (i // 2))
                                dst, src = v[:, i % 2], bank[:]
                                if cross:
                                    dst = dst.rearrange("p (h two d) -> p h two d", two=2, d=t.dh)[:, :, 0, :]
                                    src = src.rearrange("p (h d) -> p h d", d=t.dh)
                                nc.scalar.activation(dst, src, ACT.Copy).then_inc(s.v_made, 1)
                            if m == TT - 1 and not cross and bi + 1 < BODY:
                                hT_high(act, bi + 1)
                            continue
                        i = bi * n_qk + 2 * m + (what == "k")
                        scale = t.scale if what == "q" else 1.0
                        act.wait_ge(s.proj_done, done)
                        if rope:
                            if i >= 2:
                                act.wait_ge(s.swap_made, i - 1)
                                act.wait_ge(s.cos_made, i - 1)
                            if rotary:
                                bias = bias_q[:, m : m + 1] if what == "q" else bias_raw[:, 1, m : m + 1]
                                nc.scalar.activation(straight[:, i % 2], bank[:], ACT.Identity, bias=bias, scale=scale).then_inc(s.straight_made, 1)
                            else:
                                nc.scalar.activation(straight[:, i % 2], bank[:], ACT.Copy, scale=scale).then_inc(s.straight_made, 1)
                            if i % n_qk:
                                high(i - 1)
                            if i % n_qk == n_qk - 1:
                                high(i)
                        else:
                            if i >= 2:
                                act.wait_ge(qk_stored[i % 2], 16 * (i // 2))
                            nc.scalar.activation(parts[:, i % 2, 0], bank[:], ACT.Copy, scale=scale).then_inc(s.parts_hi, 1)
                        if cross and (what, m) == ("k", KD - 1) and bi + 1 < BODY:
                            hT_high(act, bi + 1)

                @block.vector
                def _(dve):
                    count = [0]

                    def small(ins):
                        count[0] += 1
                        ins.then_inc(s.ln_step, 1)
                        dve.wait_ge(s.ln_step, count[0])

                    def norm(bi):
                        dve.wait_ge(x_loaded[bi % 2], 16 * (bi // 2 + 1))
                        if bi:
                            dve.wait_ge(s.transposed, 2 * bi - 1 if cross else bi)
                        x = xt[:, bi % 2]
                        for m in range(TT):
                            count[0] += 1
                            nc.vector.bn_stats(stats[:, m, :], x[:, m, :]).then_inc(s.ln_step, 1)
                        dve.wait_ge(s.ln_step, count[0])
                        for m in range(TT):
                            count[0] += 1
                            nc.vector.bn_aggr(mv[:, m, :], stats[:, m, :]).then_inc(s.ln_step, 1)
                        dve.wait_ge(s.ln_step, count[0])
                        nc.vector.tensor_scalar(mv[:, :, 1], mv[:, :, 1], 1e-5, None, ALU.add).then_inc(s.var_ready, 1)
                        dve.wait_ge(s.std_ready, bi + 1)
                        small(nc.vector.reciprocal(rstd[:], std[:]))
                        if not rotary:
                            for m in range(TT):
                                nc.vector.tensor_scalar(hn[:, m, :], x[:, m, :], mv[:, m, 0:1], rstd[:, m : m + 1],
                                                        ALU.subtract, ALU.mult).then_inc(s.norm_ready, 1)
                            return
                        if bi:
                            dve.wait_ge(s.h1_stored, 16 * bi)
                        for m in range(TT):
                            count[0] += 1
                            nc.vector.tensor_scalar(h1[:, m, :], x[:, m, :], mv[:, m, 0:1], rstd[:, m : m + 1],
                                                    ALU.subtract, ALU.mult).then_inc(s.ln_step, 1)
                        dve.wait_ge(s.ln_step, count[0])
                        for m in range(TT):
                            count[0] += 1
                            nc.vector.tensor_tensor_reduce(out=hn[:, m, :], in0=h1[:, m, :], in1=h1[:, m, :], scale=1.0, scalar=0.0,
                                                           op0=ALU.mult, op1=ALU.add, accum_out=ssq[:, m : m + 1]).then_inc(s.ln_step, 1)
                        dve.wait_ge(s.ln_step, count[0])
                        nc.vector.tensor_scalar(ssq[:], ssq[:], 1.0 / D, 1e-6, ALU.mult, ALU.add).then_inc(s.rms_ready, 1)
                        dve.wait_ge(s.rms_std, bi + 1)
                        small(nc.vector.reciprocal(rstd[:], rms[:]))
                        for m in range(TT):
                            nc.vector.tensor_scalar(hn[:, m, :], h1[:, m, :], rstd[:, m : m + 1], None, ALU.mult).then_inc(s.norm_ready, 1)

                    def angle_steps(bi, bank):
                        two_pi = 2.0 * np.pi
                        big = 6.28125
                        small_part = float(np.float32(two_pi - big))
                        n = 12 * bi
                        dve.wait_ge(s.angles, bi + 1)
                        if bi:
                            dve.wait_ge(s.trig_made, 2 * bi)
                        nc.vector.tensor_copy(ang[0][:], bank[:]).then_inc(s.ang_step, 1)
                        dve.wait_ge(s.ang_step, n + 1)
                        nc.vector.tensor_scalar(ang[1][:], ang[0][:], float(np.pi / 2), None, ALU.add).then_inc(s.ang_step, 1)
                        n += 2
                        for x in ang:
                            dve.wait_ge(s.ang_step, n)
                            nc.vector.tensor_scalar(turns[:], x[:], 1.0 / two_pi, 12582912.0, ALU.mult, ALU.add).then_inc(s.ang_step, 1)
                            dve.wait_ge(s.ang_step, n + 1)
                            nc.vector.tensor_scalar(turns[:], turns[:], 12582912.0, None, ALU.subtract).then_inc(s.ang_step, 1)
                            dve.wait_ge(s.ang_step, n + 2)
                            nc.vector.scalar_tensor_tensor(x[:], turns[:], -big, x[:], ALU.mult, ALU.add).then_inc(s.ang_step, 1)
                            dve.wait_ge(s.ang_step, n + 3)
                            nc.vector.scalar_tensor_tensor(x[:], turns[:], -small_part, x[:], ALU.mult, ALU.add).then_inc(s.ang_step, 1)
                            dve.wait_ge(s.ang_step, n + 4)
                            nc.vector.tensor_scalar(x[:], x[:], 3.1415925, -3.1415925, ALU.min, ALU.max).then_inc(s.ang_step, 1)
                            n += 5

                    norm(0)
                    hT_low(dve, 0)
                    done = 0
                    for n, (bi, what, m) in enumerate(ring):
                        bank = psum[6 + n % 2]
                        if what == "pos":
                            continue
                        if what == "angle":
                            angle_steps(bi, bank)
                            if bi + 1 < BODY:
                                norm(bi + 1)
                            continue
                        done += 1
                        if what == "v":
                            i = bi * TT + m
                            if m == 0 and not cross and bi + 1 < BODY and not rotary:
                                norm(bi + 1)
                            if rotary:
                                dve.wait_ge(s.proj_done, done)
                                if i >= 2:
                                    dve.wait_ge(v_stored[i % 2], 16 * (i // 2))
                                nc.vector.tensor_tensor(v[:, i % 2], bank[:], bv_row[:], ALU.add).then_inc(s.v_made, 1)
                                if m == 1 and bi + 1 < BODY:
                                    norm(bi + 1)
                            if m == TT - 1 and not cross and bi + 1 < BODY:
                                hT_low(dve, bi + 1)
                            continue
                        i = bi * n_qk + 2 * m + (what == "k")
                        if rope:
                            dve.wait_ge(s.straight_made, i + 1)
                            if i % n_qk == 0 and cross:
                                dve.wait_ge(s.trig_made, 2 * (bi + 1))
                            if i:
                                dve.wait_ge(s.rotated, i)
                            swap = [r ^ 1 for r in range(32)] if cross else [(r + 16) % 32 for r in range(32)]
                            nc.vector.stream_shuffle(swapped[:], straight[:, i % 2], swap).then_inc(s.swap_made, 1)
                            dve.wait_ge(s.swap_made, i + 1)
                            nc.vector.tensor_tensor(swapped[:], swapped[:], sin_t[:], ALU.mult).then_inc(s.sin_made, 1)
                            dve.wait_ge(s.sin_made, i + 1)
                            dve.wait_ge(s.cos_made, i + 1)
                            nc.vector.tensor_tensor(turned[:, i % 2], turned[:, i % 2], swapped[:], ALU.add).then_inc(s.rotated, 1)
                            dve.wait_ge(s.parts_hi, i + 1)
                            nc.vector.tensor_tensor(parts[:, i % 2, 1], turned[:, i % 2], parts[:, i % 2, 0].bitcast(F32), ALU.subtract).then_inc(s.parts_lo, 1)
                        else:
                            dve.wait_ge(s.parts_hi, i + 1)
                            nc.vector.scalar_tensor_tensor(parts[:, i % 2, 1], bank[:], t.scale if what == "q" else 1.0,
                                                           parts[:, i % 2, 0].bitcast(F32), ALU.mult, ALU.subtract).then_inc(s.parts_lo, 1)
                        if cross and (what, m) == ("k", KD - 1) and bi + 1 < BODY:
                            hT_low(dve, bi + 1)

                @block.gpsimd
                def _(pool):
                    if rope:
                        for i in range(BODY * n_qk):
                            pool.wait_ge(s.straight_made, i + 1)
                            if i % n_qk == 0 and cross:
                                pool.wait_ge(s.trig_made, 2 * (i // n_qk + 1))
                            if i >= 2:
                                pool.wait_ge(s.parts_lo, i - 1)
                            nc.gpsimd.tensor_tensor(turned[:, i % 2], straight[:, i % 2], cos_t[:], ALU.mult).then_inc(s.cos_made, 1)

            s.clear()


def core_phase(nc, s, c, psum, a):
    t = Attention(a.kind)
    cross, causal, dh, G = t.cross, t.causal, t.dh, t.groups
    BODY = a.body
    GROUPS = G * BODY
    N16 = TT * HEADS_AT_ONCE
    ctx = ExitStack()
    with ctx:
        sb = lambda name, shape, dt=F32: ctx.enter_context(nc.sbuf_tensor(f"{a.kind}_c_{name}", shape, dt))
        wo = [sb("wo_hi", [P, KD, D], F32R), sb("wo_lo", [P, KD, D], F32R)]
        v = sb("v", [P, 2, TT, t.v_width])
        xt = sb("xt", [P, TT, D])
        prob = sb("prob", [P, PROB_SLOTS, S])
        raw = prob[:].rearrange("p (a b) n -> p a (b n)", a=2)
        q_stack = sb("q_stack", [P, STACK_SLOTS, HEADS_AT_ONCE, S], F32R)
        k_stack = sb("k_stack", [P, STACK_SLOTS, HEADS_AT_ONCE, S], F32R)
        oT = sb("oT", [P, 1 if cross else 2, KD, 2, S], F32R)
        O_SLOTS = 1 if cross else 2
        neg_max = sb("neg_max", [P, 2, TT, HEADS_AT_ONCE])
        max_parts = sb("max_parts", [P, TT, 2 * HEADS_AT_ONCE], F32R)
        max_rows = sb("max_rows", [2 * HEADS_AT_ONCE, S], F32R)
        attn, flipped = sb("attn", [P, 2, S]), sb("flipped", [P, S])
        inverse = sb("inverse", [P, S // 32])
        attn_parts = sb("attn_parts", [P, 2, 2, S], F32R) if cross else None
        out_t = sb("out_t", [P, 2, D])
        if cross:
            bo_row = sb("bo_row", [P, D])

        cols = lambda m, n: m.rearrange("(k p) n -> p k n", p=P)[:, :, n * D : (n + 1) * D]
        split_weights(nc, s, [(cols(*a.wo), wo[0][:], wo[1][:])], raw)

        with nc.Block() as block:

            @block.sync
            def _(sp):
                if cross:
                    sp.dma_start(bo_row[:], a.bo.partition_broadcast(P)).then_inc(s.table_loaded, 16)
                    sp.wait_ge(s.table_loaded, 16)

            @block.vector
            def _(dve):
                for slot in range(STACK_SLOTS):
                    nc.vector.tensor_copy(
                        k_stack[MAX_ROW:STACK_ROWS, slot],
                        c.pick[MAX_ROW:STACK_ROWS, :].unsqueeze(2).to_broadcast([2 * HEADS_AT_ONCE, HEADS_AT_ONCE, S]),
                    ).then_inc(s.table_made, 1)

            @block.gpsimd
            def _(pool):
                if cross:
                    for r0 in (32, 64):
                        for stack in (q_stack, k_stack):
                            pool.memset(stack[r0 : r0 + 32].bitcast(F32), 0.0).then_inc(s.const_made, 1)

        s.clear()

        AHEAD = N16 + a.lead
        SPLIT_STEP = N16 - 1 - a.lead
        MAX_STEP = 9
        NORM_STEP = a.norm_step
        OUT_STEPS = (1, 4, 10, 13)
        THIRDS = 3

        width_q = lambda m: (m + 1) * P if causal else S
        start_k = lambda m: m * P if causal else 0
        bank_score, bank_scoreT = ((0, 1, 2), (3, 4, 5)) if cross else ((0, 1), (2, 3))
        bank_o, bank_sum = ((6,), 6) if cross else ((4, 5), 6)
        bank_out = bank_max = 7
        N_SCORE, N_SCORET, N_O = len(bank_score), len(bank_scoreT), len(bank_o)
        stack_loaded = (s.stack_loaded0, s.stack_loaded1, s.stack_loaded2, s.stack_loaded3)
        attn_packed = (s.attn_packed0, s.attn_packed1)
        v_loaded, out_stored = (s.v_loaded0, s.v_loaded1), (s.out_stored0, s.out_stored1)

        def tile_ahead(g, step):
            n = g * N16 + step + AHEAD
            return divmod(n, N16) if n < GROUPS * N16 else None

        def projected_at(g, step):
            if g >= G + 1 and (g - 1) % G == 0:
                for m, first in enumerate(OUT_STEPS):
                    if first <= step < first + THIRDS:
                        return (g - 1) // G - 1, m, step - first
            return None

        def outputs_before(g):
            return sum(1 for h in range(g) for step in range(N16)
                       if projected_at(h, step) and projected_at(h, step)[2] == THIRDS - 1 and (h, step) < (g - 1, MAX_STEP))

        def maxima_before(bi, m):
            h, step = (bi + 1) * G + 1, OUT_STEPS[m]
            return min(GROUPS, h + 1 + (step >= MAX_STEP))

        with nc.Fori(0, B // BODY) as loop:
            rows = lambda m, bi: m[bass.ds((loop * BODY + bi) * S, S), :].rearrange("(t p) d -> p t d", p=P)
            with nc.Block() as block:

                def load_stack(sp, g):
                    bi, h0 = g // G, (g % G) * HEADS_AT_ONCE * dh
                    if g >= STACK_SLOTS:
                        sp.wait_ge(s.scoresT_ready, N16 * (g - STACK_SLOTS + 1))
                    for stack, w, order in ((q_stack, 0, (0, 1, 0)), (k_stack, 1, (0, 0, 1))):
                        src = a.scratch[bass.ds(loop * BODY + bi, 1), w, h0 : h0 + HEADS_AT_ONCE * dh]
                        for i, part in enumerate(order):
                            sp.dma_start(stack[i * dh : (i + 1) * dh, g % STACK_SLOTS].bitcast(F32),
                                         src[:, :, part, :].rearrange("a (h p) n -> p (a h) n", p=dh)).then_inc(stack_loaded[g % STACK_SLOTS], 16)

                def load_values(sp, bi):
                    if bi >= 2:
                        sp.wait_ge(s.pv_done, TT * G * (bi - 1))
                    sp.dma_start(v[:, bi % 2], rows(a.v, bi)).then_inc(v_loaded[bi % 2], 16)

                def load_residual(sp, bi):
                    if bi:
                        sp.wait_ge(s.out_made, TT * bi)
                    sp.dma_start(xt[:], rows(a.residual, bi)).then_inc(s.x_loaded0, 16)

                def send_max(sp, g):
                    sp.wait_ge(s.max_rows, g + 1)
                    sp.dma_start(q_stack[MAX_ROW:STACK_ROWS, g % STACK_SLOTS].bitcast(F32),
                                 max_rows[:].bitcast(F32).unsqueeze(1).to_broadcast([2 * HEADS_AT_ONCE, HEADS_AT_ONCE, S])).then_inc(s.max_loaded, 16)

                def pack(sp, g):
                    sp.wait_ge(s.attn_hi, g + 1)
                    sp.wait_ge(s.attn_lo, g + 1)
                    if g % G == 0 and g >= G:
                        sp.wait_ge(s.out_proj, TT * (g // G))
                    for j in range(HEADS_AT_ONCE):
                        r = (g % 2) * 64 + dh * j
                        sp.dma_start(oT[r : r + dh, 0, g % G // 2].bitcast(F32),
                                     attn_parts[32 * j : 32 * j + dh, g % 2].bitcast(F32)).then_inc(attn_packed[g % 2], 16)

                def store(sp, n):
                    bi, m = divmod(n, TT)
                    sp.wait_ge(s.out_made, n + 1)
                    sp.dma_start(a.out[bass.ds((loop * BODY + bi) * S + m * P, P), :], out_t[:, n % 2]).then_inc(out_stored[n % 2], 16)

                @block.sync
                def _(sp):
                    load_stack(sp, 0)
                    load_stack(sp, 1)
                    load_values(sp, 0)
                    load_stack(sp, 2)
                    send_max(sp, 0)
                    load_residual(sp, 0)
                    for g in range(GROUPS):
                        if g + 3 < GROUPS:
                            load_stack(sp, g + 3)
                        if g % G == min(2, G - 1) and g // G + 1 < BODY:
                            load_values(sp, g // G + 1)
                        projected = projected_at(g, OUT_STEPS[0])
                        if projected:
                            for m in range(2):
                                store(sp, projected[0] * TT + m)
                        if g + 1 < GROUPS:
                            send_max(sp, g + 1)
                        if projected:
                            for m in range(2, TT):
                                store(sp, projected[0] * TT + m)
                            load_residual(sp, projected[0] + 1)
                        if cross and g:
                            pack(sp, g - 1)
                    if cross:
                        pack(sp, GROUPS - 1)
                    for m in range(TT):
                        store(sp, (BODY - 1) * TT + m)
                    for st in out_stored:
                        sp.wait_ge(st, 16 * (BODY * TT // 2))

                @block.tensor
                def _(pe):
                    def scores(g, i):
                        m, j = divmod(i, HEADS_AT_ONCE)
                        n, slot = g * N16 + i, g % STACK_SLOTS
                        bank = psum[bank_score[n % N_SCORE]]
                        if i == 0:
                            pe.wait_ge(stack_loaded[slot], 96 * (g // STACK_SLOTS + 1))
                        if n >= N_SCORE:
                            pe.wait_ge(s.max_done, n - N_SCORE + 1)
                        last = nc.tensor.matmul(bank[:, 0 : width_q(m)], q_stack[0:MAX_ROW, slot, j, m * P : (m + 1) * P],
                                                k_stack[0:MAX_ROW, slot, j, 0 : width_q(m)], start=True, stop=not causal)
                        if causal:
                            last = nc.tensor.matmul(bank[:, m * P : (m + 1) * P], c.identb[:], c.maskqb[:], start=False, stop=True)
                        last.then_inc(s.scores_ready, 1)

                    def max_transpose(g):
                        pe.wait_ge(s.max_split, 2 * (g + 1))
                        if outputs_before(g):
                            pe.wait_ge(s.out_made, outputs_before(g))
                        for m in range(TT):
                            last = nc.tensor.transpose(psum[bank_max][0 : 2 * HEADS_AT_ONCE, m * P : (m + 1) * P],
                                                       max_parts[:, m, :].bitcast(F32), c.ident[:])
                        last.then_inc(s.max_transposed, 1)

                    def scoresT(g, i):
                        m, j = divmod(i, HEADS_AT_ONCE)
                        n, slot = g * N16 + i, g % STACK_SLOTS
                        bank, q0 = psum[bank_scoreT[n % N_SCORET]], start_k(m)
                        if i == 0:
                            pe.wait_ge(s.max_loaded, 16 * (g + 1))
                        if n >= N_SCORET:
                            pe.wait_ge(s.exp_done, n - N_SCORET + 1)
                        last = nc.tensor.matmul(bank[:, 0 : S - q0], k_stack[0:STACK_ROWS, slot, j, m * P : (m + 1) * P],
                                                q_stack[0:STACK_ROWS, slot, j, q0:S], start=True, stop=not causal)
                        if causal:
                            last = nc.tensor.matmul(bank[:, 0:P], c.identb[:], c.maskkb[:], start=False, stop=True)
                        last.then_inc(s.scoresT_ready, 1)

                    def weighted(g, m):
                        q0, bi = start_k(m), g // G
                        if g % G == 0 and m == 0:
                            pe.wait_ge(v_loaded[bi % 2], 16 * (bi // 2 + 1))
                        pe.wait_ge(s.exp_done, g * N16 + (m + 1) * HEADS_AT_ONCE)
                        if m == 0 and g:
                            pe.wait_ge(s.flip, g)
                            if g >= N_O and not cross:
                                pe.wait_ge(s.attn_out, g - N_O + 1)
                        for bank in (bank_o[0],) if cross else (bank_o[g % N_O], bank_sum):
                            for j in range(HEADS_AT_ONCE):
                                pr = prob[:, (g * N16 + m * HEADS_AT_ONCE + j) % PROB_SLOTS, 0 : S - q0]
                                h = (g % G) * HEADS_AT_ONCE + j
                                val = c.ones[:] if bank == bank_sum and not cross else v[:, bi % 2, m, 32 * h : 32 * h + 32]
                                last = nc.tensor.matmul(psum[bank][32 * j : 32 * j + 32, q0:S], val, pr, start=m == 0, stop=m == TT - 1)
                        last.then_inc(s.pv_done, 1)

                    def project(bi, m, third):
                        n = bi * TT + m
                        if third == 0:
                            if m == 0 and cross:
                                for packed in attn_packed:
                                    pe.wait_ge(packed, 16 * HEADS_AT_ONCE * (G // 2) * (bi + 1))
                            elif m == 0:
                                pe.wait_ge(s.attn_hi, G * (bi + 1))
                                pe.wait_ge(s.attn_lo, G * (bi + 1))
                            if n:
                                pe.wait_ge(s.out_made, n)
                            pe.wait_ge(s.max_rows, maxima_before(bi, m))
                        steps = list(enumerate(hi_lo_passes(KD)))
                        for i, (k, pa, pb) in steps[third * len(steps) // THIRDS : (third + 1) * len(steps) // THIRDS]:
                            last = nc.tensor.matmul(psum[bank_out][:], oT[:, bi % O_SLOTS, k, pa, m * P : (m + 1) * P], wo[pb][:, k, :],
                                                    start=i == 0, stop=i == len(steps) - 1)
                        if third == THIRDS - 1:
                            last.then_inc(s.out_proj, 1)

                    for i in range(N16):
                        scores(0, i)
                    for i in range(a.lead):
                        scores(1, i)
                        if i == 2:
                            max_transpose(0)
                    for g in range(GROUPS):
                        for step in range(N16):
                            if tile_ahead(g, step):
                                scores(*tile_ahead(g, step))
                            scoresT(g, step)
                            if step == MAX_STEP and g + 1 < GROUPS:
                                max_transpose(g + 1)
                            if step % HEADS_AT_ONCE == HEADS_AT_ONCE - 1:
                                m = step // HEADS_AT_ONCE
                                if m:
                                    weighted(g, m - 1)
                                elif g:
                                    weighted(g - 1, TT - 1)
                            if projected_at(g, step):
                                project(*projected_at(g, step))
                    weighted(GROUPS - 1, TT - 1)
                    for m in range(TT):
                        for third in range(THIRDS):
                            project(BODY - 1, m, third)

                @block.scalar
                def _(act):
                    def take_max(g):
                        act.wait_ge(s.max_transposed, g + 1)
                        if g:
                            act.wait_ge(s.max_loaded, 16 * g)
                        nc.scalar.activation(max_rows[:], psum[bank_max][0 : 2 * HEADS_AT_ONCE, :], ACT.Copy).then_inc(s.max_rows, 1)

                    def attn_high(g):
                        act.wait_ge(s.attn_out, g + 1)
                        if cross:
                            if g >= 2:
                                act.wait_ge(attn_packed[g % 2], 16 * HEADS_AT_ONCE * (g // 2))
                            dst = attn_parts[:, g % 2, 0]
                        else:
                            if g >= O_SLOTS * G and g % G == 0:
                                act.wait_ge(s.out_proj, TT * (g // G - O_SLOTS + 1))
                            dst = oT[:, g // G % O_SLOTS, g % G, 0]
                        nc.scalar.activation(dst, attn[:, g % 2], ACT.Copy).then_inc(s.attn_hi, 1)

                    take_max(0)
                    for g in range(GROUPS):
                        for step in range(N16):
                            n = g * N16 + step
                            q0 = start_k(step // HEADS_AT_ONCE)
                            act.wait_ge(s.scoresT_ready, n + 1)
                            if n >= PROB_SLOTS:
                                act.wait_ge(s.pv_done, (n - PROB_SLOTS) // HEADS_AT_ONCE + 1)
                            nc.scalar.activation(prob[:, n % PROB_SLOTS, 0 : S - q0], psum[bank_scoreT[n % N_SCORET]][:, 0 : S - q0],
                                                 ACT.Exp).then_inc(s.exp_done, 1)
                            if step == MAX_STEP and g + 1 < GROUPS:
                                take_max(g + 1)
                            if step == NORM_STEP + 3 and g:
                                attn_high(g - 1)
                    attn_high(GROUPS - 1)

                @block.vector
                def _(dve):
                    def tile_max(g, i):
                        m, j = divmod(i, HEADS_AT_ONCE)
                        n = g * N16 + i
                        dve.wait_ge(s.scores_ready, n + 1)
                        nc.vector.tensor_reduce(neg_max[:, g % 2, m, j : j + 1], psum[bank_score[n % N_SCORE]][:, 0 : width_q(m)], AX_X, ALU.max,
                                                negate=True).then_inc(s.max_done, 1)

                    def split_max(g):
                        dve.wait_ge(s.max_done, N16 * (g + 1))
                        if g:
                            dve.wait_ge(s.max_transposed, g)
                        high, low = max_parts[:, :, 0:HEADS_AT_ONCE], max_parts[:, :, HEADS_AT_ONCE:]
                        nc.vector.tensor_copy(high, neg_max[:, g % 2]).then_inc(s.max_split, 1)
                        dve.wait_ge(s.max_split, 2 * g + 1)
                        nc.vector.tensor_tensor(low, neg_max[:, g % 2], high.bitcast(F32), ALU.subtract).then_inc(s.max_split, 1)

                    def normalise(g):
                        dve.wait_ge(s.pv_done, TT * (g + 1))
                        if g:
                            dve.wait_ge(s.attn_out, g)
                        blocks = flipped[:].rearrange("p (b c) -> p b c", c=32)
                        sums = psum[bank_sum]
                        of_block = inverse[:].unsqueeze(2)
                        nc.vector.transpose(flipped[:], sums[:]).then_inc(s.flip, 1)
                        dve.wait_ge(s.flip, g + 1)
                        nc.vector.reciprocal(inverse[:], blocks[:, :, dh if cross else 0]).then_inc(s.recip_made, 1)
                        dve.wait_ge(s.recip_made, g + 1)
                        if g >= 2:
                            dve.wait_ge(s.attn_hi, g - 1)
                            dve.wait_ge(s.attn_lo, g - 1)
                        if cross:
                            nc.vector.tensor_tensor(blocks[:, :, 0:dh], blocks[:, :, 0:dh], of_block.to_broadcast([P, S // 32, dh]),
                                                    ALU.mult).then_inc(s.scaled, 1)
                            dve.wait_ge(s.scaled, g + 1)
                            nc.vector.transpose(attn[:, g % 2], flipped[:]).then_inc(s.attn_out, 1)
                        else:
                            nc.vector.transpose(flipped[:], of_block.to_broadcast([P, S // 32, 32])).then_inc(s.scaled, 1)
                            dve.wait_ge(s.scaled, g + 1)
                            nc.vector.tensor_tensor(attn[:, g % 2], psum[bank_o[g % N_O]][:], flipped[:], ALU.mult).then_inc(s.attn_out, 1)

                    def add_residual(bi, m):
                        n = bi * TT + m
                        if m == 0:
                            dve.wait_ge(s.x_loaded0, 16 * (bi + 1))
                            if cross:
                                dve.wait_ge(s.residual_made, TT * (bi + 1))
                        dve.wait_ge(s.out_proj, n + 1)
                        if n >= 2:
                            dve.wait_ge(out_stored[n % 2], 16 * (n // 2))
                        nc.vector.tensor_tensor(out_t[:, n % 2], psum[bank_out][:], xt[:, m, :], ALU.add).then_inc(s.out_made, 1)

                    for i in range(N16):
                        tile_max(0, i)
                    for i in range(a.lead):
                        tile_max(1, i)
                        if i == 0:
                            split_max(0)
                    for g in range(GROUPS):
                        for step in range(N16):
                            if tile_ahead(g, step):
                                tile_max(*tile_ahead(g, step))
                            if step == NORM_STEP and g:
                                normalise(g - 1)
                            if step == SPLIT_STEP + 1 and g + 1 < GROUPS:
                                split_max(g + 1)
                            projected = projected_at(g, step)
                            if projected and projected[2] == THIRDS - 1:
                                add_residual(projected[0], projected[1])
                    normalise(GROUPS - 1)
                    for m in range(TT):
                        add_residual(BODY - 1, m)

                @block.gpsimd
                def _(pool):
                    def bias_residual(bi):
                        pool.wait_ge(s.x_loaded0, 16 * (bi + 1))
                        for m in range(TT):
                            nc.gpsimd.tensor_tensor(xt[:, m, :], xt[:, m, :], bo_row[:], ALU.add).then_inc(s.residual_made, 1)

                    def attn_low(g):
                        pool.wait_ge(s.attn_hi, g + 1)
                        if cross:
                            if g >= 2:
                                pool.wait_ge(attn_packed[g % 2], 16 * HEADS_AT_ONCE * (g // 2))
                            parts = attn_parts[:, g % 2]
                        else:
                            parts = oT[:, g // G % O_SLOTS, g % G]
                        nc.gpsimd.tensor_tensor(parts[:, 1], attn[:, g % 2], parts[:, 0].bitcast(F32), ALU.subtract).then_inc(s.attn_lo, 1)

                    for g in range(GROUPS):
                        attn_low(g)
                        if cross and g % G == 3:
                            bias_residual(g // G)

            s.clear()


EXPERTS, TOP, FE, FS = 8, 2, 352, 1408
N_TILES = B * TT
SLOT_TILES = (B * S * TOP + EXPERTS * (P - 1)) // P
SLOTS = SLOT_TILES * P
CHUNK = 2
KF = FS // P
FE_K = [(0, P), (P, P), (2 * P, FE - 2 * P)]

MOE_SIGNALS = [
    "m_loaded", "m_x2_loaded", "m_sq", "m_var", "m_std", "m_rstd", "m_norm", "m_t", "m_hi", "m_lo", "m_rt", "m_rt_sb",
    "m_logits", "m_step", "m_exp", "m_egexp", "m_gate_up", "m_silu", "m_act", "m_ahi", "m_alo", "m_down", "m_resid",
    "m_out", "m_stored", "m_rows", "m_tab", "m_ld0", "m_ld1", "g_got0", "g_got1", "g_row0", "g_row1", "g_row2", "g_row3", "g_sent0", "g_sent1", "g_sent2", "g_sent3", "m_wt", "m_zero",
    "e_ld0", "e_ld1", "e_t", "e_hT", "e_g", "e_s", "e_a", "e_at", "e_aT", "e_y", "e_ysb", "e_st0", "e_st1",
]


def shared_phase(nc, s, c, psum, a, keep):

    n_col = EXPERTS + 1
    W = CHUNK * P
    ctx = ExitStack()
    with ctx:
        sb = lambda name, shape, dt=F32: ctx.enter_context(nc.sbuf_tensor(f"shared_{name}", shape, dt))
        wg = [sb(f"wg{i}", [P, KD, FS], F32R) for i in range(2)]
        wu = [sb(f"wu{i}", [P, KD, FS], F32R) for i in range(2)]
        wd = [sb(f"wd{i}", [P, KF, D], F32R) for i in range(2)]
        wr = [sb(f"wr{i}", [P, KD, n_col], F32R) for i in range(2)]
        raw = sb("raw", [P, 2, 4 * D])
        xt, x2 = raw[:, 0, :].rearrange("p (t d) -> p t d", d=D), raw[:, 1, :].rearrange("p (t d) -> p t d", d=D)
        xt, hn = xt[:, 0:2], xt[:, 2:4]
        x2, out_t = x2[:, 0:2], x2[:, 2:4]
        hT = [sb(f"hT{i}", [P, KD, W], F32R) for i in range(2)]
        act_p = [sb(f"act{i}", [P, KF, W], F32R) for i in range(2)]
        silu, prod = sb("silu", [P, 2, W]), sb("prod", [P, 2, W])
        w_ln = sb("w_ln", [P, KD])
        rt = sb("rt", [n_col, W])
        ssq, std, rstd = sb("ssq", [P, CHUNK]), sb("std", [P, CHUNK]), sb("rstd", [P, CHUNK])
        logit, nmax, ex = sb("logit", [P, CHUNK, n_col]), sb("nmax", [P, CHUNK]), sb("ex", [P, CHUNK, EXPERTS])
        total, best = sb("total", [P, CHUNK]), sb("best", [P, CHUNK, 8])
        where = sb("where", [P, CHUNK, 8], U32)
        wheref = sb("wheref", [P, CHUNK, 8])
        gate = sb("gate", [P, CHUNK])
        rows8 = sb("rows8", [P, EXPERTS])

        jobs = []
        for src, dst in ((a.w_gate, wg), (a.w_up, wu)):
            for k in range(KD):
                jobs.append((src[k * P : (k + 1) * P, :].rearrange("(k p) n -> p k n", p=P), dst[0][:, k : k + 1], dst[1][:, k : k + 1]))
        for k0 in range(0, KF, 4):
            k1 = min(KF, k0 + 4)
            jobs.append((a.w_down[k0 * P : k1 * P, :].rearrange("(k p) n -> p k n", p=P), wd[0][:, k0:k1], wd[1][:, k0:k1]))
        jobs.append((a.w_router.rearrange("(k p) n -> p k n", p=P), wr[0][:, :, 0:EXPERTS], wr[1][:, :, 0:EXPERTS]))
        jobs.append((a.w_eg.rearrange("(k p) n -> p k n", p=P), wr[0][:, :, EXPERTS:n_col], wr[1][:, :, EXPERTS:n_col]))
        split_weights(nc, s, jobs, raw)

        with nc.Block() as block:

            @block.sync
            def _(sp):
                sp.dma_start(w_ln[:], a.w_ln.rearrange("(k p) -> p k", p=P), allow_slow_non_contiguous=True).then_inc(s.m_tab, 16)
                sp.dma_start(rows8[:], a.count8.partition_broadcast(P)).then_inc(s.m_tab, 16)
                sp.wait_ge(s.m_tab, 32)

        s.clear()

        with nc.Fori(0, N_TILES // CHUNK) as i:
            at = lambda t: t[bass.ds(i * W, W), :].rearrange("(t p) d -> p t d", p=P)
            with nc.Block() as block:

                @block.sync
                def _(sp):
                    sp.dma_start(xt, at(a.x3)).then_inc(s.m_loaded, 16)
                    sp.dma_start(x2, at(a.x2)).then_inc(s.m_x2_loaded, 16)
                    sp.wait_ge(s.m_norm, CHUNK)
                    sp.dma_start(at(a.rows), hn).then_inc(s.m_rows, 16)
                    sp.wait_ge(s.m_out, CHUNK)
                    sp.dma_start(at(a.base), out_t).then_inc(s.m_stored, 16)
                    sp.wait_ge(s.m_rows, 16)
                    sp.wait_ge(s.m_stored, 16)

                @block.tensor
                def _(pe):
                    for t in range(CHUNK):
                        pe.wait_ge(s.m_norm, t + 1)
                        for k in range(KD):
                            last = nc.tensor.transpose(psum[k][:, t * P : (t + 1) * P], hn[:, t, k * P : (k + 1) * P], c.ident[:])
                    last.then_inc(s.m_t, 1)
                    pe.wait_ge(s.m_hi, KD)
                    pe.wait_ge(s.m_lo, KD)
                    steps = hi_lo_passes(KD)
                    for n, (k, pa, pb) in enumerate(steps):
                        last = nc.tensor.matmul(psum[2][0:n_col, 0:W], wr[pa][:, k, :], hT[pb][:, k, :], start=n == 0, stop=n == len(steps) - 1)
                    last.then_inc(s.m_rt, 1)
                    for f in range(KF):
                        if f == 1:
                            pe.wait_ge(s.m_rt_sb, 1)
                            for t in range(CHUNK):
                                last = nc.tensor.transpose(psum[3][:, t * 16 : t * 16 + n_col], rt[:, t * P : (t + 1) * P], c.ident[0:n_col, 0:n_col])
                            last.then_inc(s.m_logits, 1)
                        if f >= 2:
                            pe.wait_ge(s.m_act, f - 1)
                        for half, w in enumerate((wg, wu)):
                            for n, (k, pa, pb) in enumerate(steps):
                                last = nc.tensor.matmul(psum[4 + f % 2][:, half * W : (half + 1) * W], w[pa][:, k, f * P : (f + 1) * P], hT[pb][:, k, :],
                                                        start=n == 0, stop=n == len(steps) - 1)
                        last.then_inc(s.m_gate_up, 1)
                    down = hi_lo_passes(KF)
                    for t in range(CHUNK):
                        for n, (k, pa, pb) in enumerate(down):
                            if t == 0 and (pa, pb) == (0, 0):
                                pe.wait_ge(s.m_ahi, k + 1)
                                pe.wait_ge(s.m_alo, k + 1)
                            last = nc.tensor.matmul(psum[6 + t][:], act_p[pa][:, k, t * P : (t + 1) * P], wd[pb][:, k, :], start=n == 0, stop=n == len(down) - 1)
                        last.then_inc(s.m_down, 1)

                @block.scalar
                def _(act):
                    act.wait_ge(s.m_var, 1)
                    nc.scalar.activation(std[:], ssq[:], ACT.Sqrt).then_inc(s.m_std, 1)
                    act.wait_ge(s.m_t, 1)
                    for k in range(KD):
                        nc.scalar.activation(hT[0][:, k, :], psum[k][:, 0:W], ACT.Copy, scale=w_ln[:, k : k + 1]).then_inc(s.m_hi, 1)
                    act.wait_ge(s.m_rt, 1)
                    nc.scalar.activation(rt[:], psum[2][0:n_col, 0:W], ACT.Copy).then_inc(s.m_rt_sb, 1)
                    act.wait_ge(s.m_step, 1 + CHUNK)
                    for t in range(CHUNK):
                        nc.scalar.activation(ex[:, t, :], logit[:, t, 0:EXPERTS], ACT.Exp, bias=nmax[:, t : t + 1], accum_out=total[:, t : t + 1]).then_inc(s.m_exp, 1)
                    nc.scalar.activation(gate[:], logit[:, :, EXPERTS], ACT.Exp, scale=-1.0).then_inc(s.m_exp, 1)

                    def high(f):
                        act.wait_ge(s.m_act, f + 1)
                        nc.scalar.activation(act_p[0][:, f, :], prod[:, f % 2, :], ACT.Copy).then_inc(s.m_ahi, 1)

                    for f in range(KF):
                        act.wait_ge(s.m_gate_up, f + 1)
                        if f >= 2:
                            act.wait_ge(s.m_act, f - 1)
                        nc.scalar.activation(silu[:, f % 2, :], psum[4 + f % 2][:, 0:W], ACT.Silu).then_inc(s.m_silu, 1)
                        if f:
                            high(f - 1)
                    high(KF - 1)

                @block.vector
                def _(dve):
                    dve.wait_ge(s.m_loaded, 16)
                    for t in range(CHUNK):
                        nc.vector.tensor_tensor_reduce(out=hn[:, t, :], in0=xt[:, t, :], in1=xt[:, t, :], scale=1.0, scalar=0.0,
                                                       op0=ALU.mult, op1=ALU.add, accum_out=ssq[:, t : t + 1]).then_inc(s.m_sq, 1)
                    dve.wait_ge(s.m_sq, CHUNK)
                    nc.vector.tensor_scalar(ssq[:], ssq[:], 1.0 / D, 1e-6, ALU.mult, ALU.add).then_inc(s.m_var, 1)
                    dve.wait_ge(s.m_std, 1)
                    nc.vector.reciprocal(rstd[:], std[:]).then_inc(s.m_rstd, 1)
                    dve.wait_ge(s.m_rstd, 1)
                    for t in range(CHUNK):
                        nc.vector.tensor_scalar(hn[:, t, :], xt[:, t, :], rstd[:, t : t + 1], None, ALU.mult).then_inc(s.m_norm, 1)
                    for k in range(KD):
                        dve.wait_ge(s.m_hi, k + 1)
                        nc.vector.scalar_tensor_tensor(hT[1][:, k, :], psum[k][:, 0:W], w_ln[:, k : k + 1],
                                                       hT[0][:, k, :].bitcast(F32), ALU.mult, ALU.subtract).then_inc(s.m_lo, 1)
                    dve.wait_ge(s.m_logits, 1)
                    nc.vector.tensor_copy(logit[:], psum[3][:, 0 : 16 * CHUNK].rearrange("p (t e) -> p t e", e=16)[:, :, 0:n_col]).then_inc(s.m_step, 1)
                    dve.wait_ge(s.m_step, 1)
                    for t in range(CHUNK):
                        nc.vector.tensor_reduce(nmax[:, t : t + 1], logit[:, t, 0:EXPERTS], AX_X, ALU.max, negate=True).then_inc(s.m_step, 1)
                    dve.wait_ge(s.m_exp, CHUNK + 1)
                    nc.vector.reciprocal(total[:], total[:]).then_inc(s.m_step, 1)
                    nc.vector.tensor_scalar(gate[:], gate[:], 1.0, None, ALU.add).then_inc(s.m_step, 1)
                    n = CHUNK + 3
                    dve.wait_ge(s.m_step, n)
                    nc.vector.reciprocal(gate[:], gate[:]).then_inc(s.m_step, 1)
                    for t in range(CHUNK):
                        nc.vector.tensor_scalar(ex[:, t, :], ex[:, t, :], total[:, t : t + 1], None, ALU.mult).then_inc(s.m_step, 1)
                    n += 1 + CHUNK
                    dve.wait_ge(s.m_step, n)
                    for t in range(CHUNK):
                        nc.vector.max(best[:, t, :], ex[:, t, :]).then_inc(s.m_step, 1)
                    n += CHUNK
                    dve.wait_ge(s.m_step, n)
                    for t in range(CHUNK):
                        nc.vector.max_index(where[:, t, :], best[:, t, :], ex[:, t, :]).then_inc(s.m_step, 1)
                    n += CHUNK
                    dve.wait_ge(s.m_step, n)
                    nc.vector.tensor_copy(wheref[:], where[:]).then_inc(s.m_step, 1)
                    nc.vector.tensor_copy(keep.weight[:, bass.ds(i * CHUNK, CHUNK), :], best[:, :, 0:TOP]).then_inc(s.m_step, 1)
                    n += 2
                    dve.wait_ge(s.m_step, n)
                    for t in range(CHUNK):
                        for j in range(TOP):
                            nc.vector.tensor_scalar(keep.hot[:, j, bass.ds(i * CHUNK + t, 1), :].rearrange("p a e -> p (a e)"), rows8[:],
                                                    wheref[:, t, j : j + 1], None, ALU.is_equal).then_inc(s.m_step, 1)

                    def low(f):
                        dve.wait_ge(s.m_ahi, f + 1)
                        nc.vector.tensor_tensor(act_p[1][:, f, :], prod[:, f % 2, :], act_p[0][:, f, :].bitcast(F32), ALU.subtract).then_inc(s.m_alo, 1)

                    for f in range(KF):
                        dve.wait_ge(s.m_silu, f + 1)
                        if f >= 2:
                            dve.wait_ge(s.m_alo, f - 1)
                        nc.vector.tensor_tensor(prod[:, f % 2, :], silu[:, f % 2, :], psum[4 + f % 2][:, W : 2 * W], ALU.mult).then_inc(s.m_act, 1)
                        if f:
                            low(f - 1)
                    low(KF - 1)
                    dve.wait_ge(s.m_resid, CHUNK)
                    for t in range(CHUNK):
                        dve.wait_ge(s.m_down, t + 1)
                        nc.vector.scalar_tensor_tensor(out_t[:, t, :], psum[6 + t][:], gate[:, t : t + 1], x2[:, t, :], ALU.mult, ALU.add).then_inc(s.m_out, 1)

                @block.gpsimd
                def _(pool):
                    pool.wait_ge(s.m_loaded, 16)
                    pool.wait_ge(s.m_x2_loaded, 16)
                    for t in range(CHUNK):
                        nc.gpsimd.tensor_tensor(x2[:, t, :], x2[:, t, :], xt[:, t, :], ALU.add).then_inc(s.m_resid, 1)

            s.clear()


def routed_phase(nc, s, c, psum, a, keep):

    NT, E = N_TILES, EXPERTS
    ctx = ExitStack()
    with ctx:
        sb = lambda name, shape, dt=F32: ctx.enter_context(nc.sbuf_tensor(f"routed_{name}", shape, dt))
        w_gu = sb("w_gu", [P, E, KD, 2 * FE])
        w_dn = sb("w_dn", [P, E, len(FE_K), D])
        w_ln = sb("w_ln", [P, KD])
        row = sb("row", [P, 4, D])
        below = sb("below", [P, P])
        allones = sb("allones", [P, P])
        hot = sb("hot", [P, NT, E])
        pre, tot, carry = sb("pre", [P, NT, E]), sb("tot", [P, NT, E]), sb("carry", [P, NT + 1, E])
        tiles_i, tiles_f = sb("tiles_i", [P, E], I32), sb("tiles_f", [P, E])
        begin = sb("begin", [P, E + 1])
        pick = sb("pick", [P, TOP, NT, E])
        slot_f, slot = sb("slot_f", [P, TOP, NT]), sb("slot", [P, TOP, NT], U32)
        count_t = sb("count_t", [P, SLOT_TILES])
        passed = sb("passed", [P, SLOT_TILES, E])
        owner_f, owner = sb("owner_f", [P, SLOT_TILES]), sb("owner", [P, SLOT_TILES], I32)
        hT = sb("hT", [P, 2, KD, P])
        silu, inner = sb("silu", [P, 2, FE]), sb("inner", [P, 2, FE])
        innerT = sb("innerT", [P, 2, len(FE_K), P])
        y = sb("y", [P, 2, D])

        row_here = (s.g_row0, s.g_row1, s.g_row2, s.g_row3)
        row_sent = (s.g_sent0, s.g_sent1, s.g_sent2, s.g_sent3)
        SLOT_STEPS = 4 + NT + 4 + E + 3 + 2 * TOP + 1

        def send(pool, i):
            pool.wait_ge(row_here[i % 4], 16 * (i // 4 + 1))
            if i == 0:
                pool.wait_ge(s.m_step, SLOT_STEPS)
            for j in range(TOP):
                pool.indirect_dma_start(a.slots, bass.IndirectOffsetOnAxis(ap=slot[:, j, i : i + 1], axis=0), row[:, i % 4, :], None
                                        ).then_inc(row_sent[i % 4], 16)

        with nc.Block() as block:

            @block.sync
            def _(sp):
                sp.dma_start(w_ln[:], a.w_ln.rearrange("(k p) -> p k", p=P), allow_slow_non_contiguous=True).then_inc(s.m_tab, 16)
                sp.dma_start(count_t[:], a.count_t.partition_broadcast(P)).then_inc(s.m_tab, 16)
                n = 0
                for e in range(E):
                    for dst, src in ((w_gu[:, e, :, 0:FE], a.w_gate[e]), (w_gu[:, e, :, FE : 2 * FE], a.w_up[e])):
                        sp.dma_start(dst, src.rearrange("(k p) n -> p k n", p=P)).then_inc(s.m_wt, 16)
                        n += 16
                    sp.dma_start(w_dn[:, e, 0:2, :], a.w_down[e][0 : 2 * P, :].rearrange("(k p) n -> p k n", p=P)).then_inc(s.m_wt, 16)
                    sp.dma_start(w_dn[0 : FE - 2 * P, e, 2, :], a.w_down[e][2 * P : FE, :]).then_inc(s.m_wt, 16)
                    n += 32
                sp.wait_ge(s.m_tab, 32)
                sp.wait_ge(s.m_wt, n)

            @block.gpsimd
            def _(pool):
                pool.memset(below[:], 1.0).then_inc(s.m_zero, 1)
                pool.memset(allones[:], 1.0).then_inc(s.m_zero, 1)
                pool.wait_ge(s.m_zero, 2)
                pool.affine_select(out=below[:], in_=below[:], compare_op=ALU.is_gt, fill=0.0, base=0,
                                   pattern=[[1, P]], channel_multiplier=-1).then_inc(s.m_zero, 1)
                for i in range(NT):
                    if i >= 4:
                        pool.wait_ge(row_sent[i % 4], 32 * (i // 4))
                    pool.dma_start(row[:, i % 4, :], a.rows[i * P : (i + 1) * P, :]).then_inc(row_here[i % 4], 16)
                    if i >= 2:
                        send(pool, i - 2)
                send(pool, NT - 2)
                send(pool, NT - 1)
                for m in range(4):
                    pool.wait_ge(row_sent[m], 32 * (NT // 4))

            @block.tensor
            def _(pe):
                pe.wait_ge(s.m_zero, 3)
                pe.wait_ge(s.m_step, 1)
                flat = hot[:].rearrange("p t e -> p (t e)")
                nc.tensor.matmul(psum[0][:, 0 : NT * E], below[:], flat, start=True, stop=True).then_inc(s.m_t, 1)
                nc.tensor.matmul(psum[1][:, 0 : NT * E], allones[:], flat, start=True, stop=True).then_inc(s.m_t, 1)

            @block.vector
            def _(dve):
                done = [0]

                def step(ins):
                    done[0] += 1
                    ins.then_inc(s.m_step, 1)
                    dve.wait_ge(s.m_step, done[0])

                step(nc.vector.tensor_tensor(hot[:], keep.hot[:, 0], keep.hot[:, 1], ALU.add))
                dve.wait_ge(s.m_t, 2)
                step(nc.vector.tensor_copy(pre[:].rearrange("p t e -> p (t e)"), psum[0][:, 0 : NT * E]))
                step(nc.vector.tensor_copy(tot[:].rearrange("p t e -> p (t e)"), psum[1][:, 0 : NT * E]))
                step(nc.vector.memset(carry[:, 0, :], 0.0))
                for t in range(NT):
                    step(nc.vector.tensor_tensor(carry[:, t + 1, :], carry[:, t, :], tot[:, t, :], ALU.add))
                step(nc.vector.tensor_scalar(tiles_i[:], carry[:, NT, :], float(P - 1), None, ALU.add))
                step(nc.vector.tensor_scalar(tiles_i[:], tiles_i[:], P.bit_length() - 1, None, ALU.arith_shift_right))
                step(nc.vector.tensor_copy(tiles_f[:], tiles_i[:]))
                step(nc.vector.memset(begin[:, 0:1], 0.0))
                for e in range(E):
                    step(nc.vector.tensor_tensor(begin[:, e + 1 : e + 2], begin[:, e : e + 1], tiles_f[:, e : e + 1], ALU.add))
                step(nc.vector.tensor_tensor(pre[:], pre[:], carry[:, 0:NT, :], ALU.add))
                step(nc.vector.tensor_scalar(tiles_f[:], begin[:, 0:E], float(P), None, ALU.mult))
                step(nc.vector.tensor_tensor(pre[:], pre[:], tiles_f[:].unsqueeze(1).to_broadcast([P, NT, E]), ALU.add))
                for j in range(TOP):
                    step(nc.vector.tensor_tensor(pick[:, j], keep.hot[:, j], pre[:], ALU.mult))
                    step(nc.vector.tensor_reduce(slot_f[:, j, :], pick[:, j], AX_X, ALU.add))
                done[0] += 1
                nc.vector.tensor_copy(slot[:], slot_f[:]).then_inc(s.m_step, 1)
                dve.wait_ge(s.m_step, done[0])
                assert done[0] == SLOT_STEPS
                dve.wait_ge(s.m_tab, 32)
                step(nc.vector.tensor_tensor(passed[:], count_t[:].unsqueeze(2).to_broadcast([P, SLOT_TILES, E]),
                                             begin[:, 1 : E + 1].unsqueeze(1).to_broadcast([P, SLOT_TILES, E]), ALU.is_ge))
                step(nc.vector.tensor_reduce(owner_f[:], passed[:], AX_X, ALU.add))
                step(nc.vector.tensor_scalar(owner[:], owner_f[:], float(E - 1), None, ALU.min))

        s.clear()

        def store(sp, t):
            sp.wait_ge(s.e_ysb, t + 1)
            sp.dma_start(a.results[bass.ds((i * PER + t) * P, P), :], y[:, t % 2, :]).then_inc((s.e_st0, s.e_st1)[t % 2], 16)

        def result(act, t):
            act.wait_ge(s.e_y, t + 1)
            if t >= 2:
                act.wait_ge((s.e_st0, s.e_st1)[t % 2], 16 * (t // 2))
            nc.scalar.activation(y[:, t % 2, :], psum[6 + t % 2][:], ACT.Copy).then_inc(s.e_ysb, 1)

        def put(sp, t):
            sp.wait_ge(s.m_out, t + 1)
            sp.dma_start(a.out[t * P : (t + 1) * P, :], y[:, t % 2, :]).then_inc((s.e_st0, s.e_st1)[t % 2], 16)

        PER = 13
        with nc.Fori(0, SLOT_TILES // PER) as i:
            with nc.Block() as block:

                @block.sync
                def _(sp):
                    for t in range(PER):
                        if t >= 4:
                            sp.wait_ge(s.e_t, t - 3)
                        sp.dma_start(row[:, t % 4, :], a.slots[bass.ds((i * PER + t) * P, P), :]).then_inc((s.e_ld0, s.e_ld1, s.m_ld0, s.m_ld1)[t % 4], 16)
                        if t >= 4:
                            store(sp, t - 4)
                    for t in range(PER - 4, PER):
                        store(sp, t)
                    for m, st in enumerate((s.e_st0, s.e_st1)):
                        sp.wait_ge(st, 16 * len(range(m, PER, 2)))

                @block.tensor
                def _(pe):
                    experts = {}

                    def front(t):
                        pe.wait_ge((s.e_ld0, s.e_ld1, s.m_ld0, s.m_ld1)[t % 4], 16 * (t // 4 + 1))
                        if t >= 1:
                            pe.wait_ge(s.e_hT, t)
                        for k in range(KD):
                            last = nc.tensor.transpose(psum[0][:, k * P : (k + 1) * P], row[:, t % 4, k * P : (k + 1) * P], c.ident[:])
                        last.then_inc(s.e_t, 1)

                    def gate_up(t):
                        e = pe.value_load(owner[0:1, bass.ds(i * PER + t, 1)], min_val=0, max_val=E - 1)
                        experts[t % 2] = e
                        pe.wait_ge(s.e_hT, t + 1)
                        if t >= 2:
                            pe.wait_ge(s.e_a, t - 1)
                        for half in range(2):
                            for k in range(KD):
                                rhs = w_gu[:, bass.ds(e, 1), k, half * FE : (half + 1) * FE].rearrange("p a n -> p (a n)")
                                last = nc.tensor.matmul(psum[1 + 2 * (t % 2) + half][:, 0:FE], hT[:, t % 2, k, :], rhs, start=k == 0, stop=k == KD - 1)
                        last.then_inc(s.e_g, 1)

                    def turn(t):
                        pe.wait_ge(s.e_a, t + 1)
                        if t >= 1:
                            pe.wait_ge(s.e_aT, t)
                        for n, (k0, kn) in enumerate(FE_K):
                            last = nc.tensor.transpose(psum[5][0:kn, n * P : (n + 1) * P], inner[:, t % 2, k0 : k0 + kn], c.ident[:])
                        last.then_inc(s.e_at, 1)

                    def down(t):
                        pe.wait_ge(s.e_aT, t + 1)
                        if t >= 2:
                            pe.wait_ge(s.e_ysb, t - 1)
                        for n, (k0, kn) in enumerate(FE_K):
                            rhs = w_dn[0:kn, bass.ds(experts[t % 2], 1), n, :].rearrange("p a n -> p (a n)")
                            last = nc.tensor.matmul(psum[6 + t % 2][:], innerT[0:kn, t % 2, n, :], rhs, start=n == 0, stop=n == len(FE_K) - 1)
                        last.then_inc(s.e_y, 1)

                    front(0)
                    for t in range(PER):
                        if t + 1 < PER:
                            front(t + 1)
                        if t:
                            turn(t - 1)
                            down_e = experts[(t - 1) % 2]
                        gate_up(t)
                        if t:
                            experts[(t - 1) % 2] = down_e
                            down(t - 1)
                    turn(PER - 1)
                    down(PER - 1)

                @block.scalar
                def _(act):
                    for t in range(PER):
                        act.wait_ge(s.e_g, t + 1)
                        if t >= 2:
                            act.wait_ge(s.e_a, t - 1)
                        nc.scalar.activation(silu[:, t % 2], psum[1 + 2 * (t % 2)][:, 0:FE], ACT.Silu).then_inc(s.e_s, 1)
                        if t:
                            result(act, t - 1)
                    result(act, PER - 1)

                @block.vector
                def _(dve):
                    def columns(t):
                        dve.wait_ge(s.e_t, t + 1)
                        if t >= 2:
                            dve.wait_ge(s.e_g, t - 1)
                        nc.vector.tensor_tensor(hT[:, t % 2], psum[0][:].rearrange("p (k n) -> p k n", k=KD),
                                                w_ln[:].unsqueeze(2).to_broadcast([P, KD, P]), ALU.mult).then_inc(s.e_hT, 1)

                    columns(0)
                    for t in range(PER):
                        if t + 1 < PER:
                            columns(t + 1)
                        dve.wait_ge(s.e_s, t + 1)
                        if t >= 2:
                            dve.wait_ge(s.e_at, t - 1)
                        nc.vector.tensor_tensor(inner[:, t % 2], silu[:, t % 2], psum[2 + 2 * (t % 2)][:, 0:FE], ALU.mult).then_inc(s.e_a, 1)
                        dve.wait_ge(s.e_at, t + 1)
                        if t >= 2:
                            dve.wait_ge(s.e_y, t - 1)
                        nc.vector.tensor_copy(innerT[:, t % 2, 0:2], psum[5][:, 0 : 2 * P].rearrange("p (k n) -> p k n", k=2)).then_inc(s.m_step, 1)
                        kn = FE_K[2][1]
                        nc.vector.tensor_copy(innerT[0:kn, t % 2, 2], psum[5][0:kn, 2 * P : 3 * P]).then_inc(s.e_aT, 1)

            s.clear()

        with nc.Block() as block:
            NB = 2
            got = row[:].rearrange("p (n j) d -> p n j d", n=NB)
            baset, res = y, innerT[:].rearrange("p a b n -> p (a b n)")[:, 0:D]

            @block.gpsimd
            def _(pool):
                for t in range(NT):
                    if t >= NB:
                        pool.wait_ge(s.m_out, t - NB + 1)
                    for j in range(TOP):
                        pool.indirect_dma_start(got[:, t % NB, j, :], None, a.results, bass.IndirectOffsetOnAxis(ap=slot[:, j, t : t + 1], axis=0)
                                                ).then_inc((s.g_got0, s.g_got1)[t % NB], 16)

            @block.sync
            def _(sp):
                for t in range(NT):
                    if t >= NB:
                        sp.wait_ge((s.e_st0, s.e_st1)[t % 2], 16 * (t // 2))
                    sp.dma_start(baset[:, t % 2, :], a.base[t * P : (t + 1) * P, :]).then_inc((s.m_ld0, s.m_ld1)[t % 2], 16)
                    if t >= 1:
                        put(sp, t - 1)
                put(sp, NT - 1)
                for st in (s.e_st0, s.e_st1):
                    sp.wait_ge(st, 16 * (NT // 2))

            @block.vector
            def _(dve):
                for t in range(NT):
                    dve.wait_ge((s.m_ld0, s.m_ld1)[t % 2], 16 * (t // 2 + 1))
                    dve.wait_ge((s.g_got0, s.g_got1)[t % NB], 32 * (t // NB + 1))
                    if t >= 1:
                        dve.wait_ge(s.m_out, t)
                    nc.vector.scalar_tensor_tensor(res, got[:, t % NB, 0, :], keep.weight[:, t, 0:1], baset[:, t % 2, :], ALU.mult, ALU.add).then_inc(s.m_act, 1)
                    dve.wait_ge(s.m_act, t + 1)
                    nc.vector.scalar_tensor_tensor(baset[:, t % 2, :], got[:, t % NB, 1, :], keep.weight[:, t, 1:2], res, ALU.mult, ALU.add).then_inc(s.m_out, 1)

        s.clear()


def zero_slots(nc, s, slots):
    with nc.sbuf_tensor("zeros", [P, D], F32) as zeros, nc.Block() as block:

        @block.vector
        def _(dve):
            nc.vector.memset(zeros[:], 0.0).then_inc(s.m_zero, 1)

        @block.sync
        def _(sp):
            sp.wait_ge(s.m_zero, 1)
            for t in range(SLOT_TILES):
                sp.dma_start(slots[t * P : (t + 1) * P, :], zeros[:]).then_inc(s.m_stored, 16)
            sp.wait_ge(s.m_stored, 16 * SLOT_TILES)

    s.clear()


ROPE_HEAD, ROPE_THETA = 32, 1.0e6
AXIAL_HEAD, AXIAL_BASE = 16, 10000.0


def shape_constants():
    inv = (np.float32(1.0) / np.float32(ROPE_THETA) ** (np.arange(0, ROPE_HEAD, 2, dtype=np.float32) / ROPE_HEAD)).astype(np.float32)
    angle = (inv[:, None] * np.arange(S, dtype=np.float32)[None, :]).astype(np.float32)
    cos, sin = np.cos(angle), np.sin(angle)
    half = AXIAL_HEAD // 4
    base = (np.float32(AXIAL_BASE) ** (-np.arange(half, dtype=np.float32) / half)).astype(np.float32)
    freq, sign = np.zeros((2, P), np.float32), np.zeros((P, 1), np.float32)
    for r in range(P):
        axis, rest = divmod(r % AXIAL_HEAD, AXIAL_HEAD // 2)
        freq[axis, r] = base[rest // 2]
        sign[r, 0] = -1.0 if r % 2 == 0 else 1.0
    return {
        "rope_cos": np.tile(cos, (2 * P // ROPE_HEAD, 1)),
        "rope_sin": np.tile(np.concatenate([-sin, sin]), (P // ROPE_HEAD, 1)),
        "axial_freq": freq,
        "axial_sign": sign,
        "expert_number": np.arange(EXPERTS, dtype=np.float32),
        "tile_number": np.arange(SLOT_TILES, dtype=np.float32),
    }


def build(nc, i, out):

    rows = lambda t: t.rearrange("b s d -> (b s) d")
    dram = lambda name, shape: nc.dram_tensor(name, shape, F32, kind="Internal").ap()
    x1, x2, x3, h1 = (dram(n, (B * S, D)) for n in ("x1", "x2", "x3", "h1"))
    scratch, values = dram("qk_parts", (B, 2, D, 2, S)), dram("values", (B * S, 2 * D))
    normed, base = dram("normed", (B * S, D)), dram("base", (B * S, D))
    slots, results = dram("slots", (SLOTS, D)), dram("results", (SLOTS, D))
    ctx = ExitStack()
    with ctx:
        sb = lambda name, shape, dt=F32: ctx.enter_context(nc.sbuf_tensor(name, shape, dt))
        c = Args(ident=sb("ident", [P, P]), pick=sb("pick", [P, HEADS_AT_ONCE]),
                 ones=sb("ones", [P, 32]), identb=sb("identb", [P, P], BF16), maskqb=sb("maskqb", [P, P], BF16), maskkb=sb("maskkb", [P, P], BF16))
        psum = [ctx.enter_context(nc.psum_tensor(f"bank{n}", [P, D], F32)) for n in range(8)]
        s = Signals(nc, SIGNALS + MOE_SIGNALS)
        make_constants(nc, s, c)
        zero_slots(nc, s, slots)
        qkv = i["L0_attn_w_qkv"]
        qk = dict(scratch=scratch, body=4, lead=10, norm_step=5)
        first = Args(kind="first", x=rows(i["x"]), wq=(qkv, 0), wk=(qkv, 1), wv=(qkv, 2), wo=(i["L0_attn_w_out"], 0),
                     v=values[:, 0:D], residual=rows(i["x"]), out=x1, **qk)
        projection_phase(nc, s, c, psum, first)
        core_phase(nc, s, c, psum, first)
        wkv = i["L0_xattn_Wkv"]
        cross = Args(kind="cross", x=x1, ctx=rows(i["ctx_1024"]), pos=rows(i["fside_BxSx2_0"]), wq=(i["L0_xattn_Wq"], 0),
                     wk=(wkv, 0), wv=(wkv, 1), wo=(i["L0_xattn_Wout"], 0), bo=i["L0_xattn_bout"], freq=i["axial_freq"],
                     sign=i["axial_sign"], v=values, residual=x1, out=x2, **qk)
        projection_phase(nc, s, c, psum, cross)
        core_phase(nc, s, c, psum, cross)
        rotary = Args(kind="rotary", x=x2, h1=h1, wq=(i["L0_ffn_wq"], 0), wk=(i["L0_ffn_wk"], 0), wv=(i["L0_ffn_wv"], 0),
                      wo=(i["L0_ffn_wo"], 0), bq=i["L0_ffn_bq"], bk=i["L0_ffn_bk"], bv=i["L0_ffn_bv"], w_ln=i["L0_ffn_w_ln1"],
                      cos=i["rope_cos"], sin=i["rope_sin"], v=values[:, 0:D], residual=h1, out=x3, **qk)
        projection_phase(nc, s, c, psum, rotary)
        core_phase(nc, s, c, psum, rotary)
        keep = Args(weight=sb("top_weight", [P, N_TILES, TOP]), hot=sb("top_hot", [P, TOP, N_TILES, EXPERTS]))
        shared_phase(nc, s, c, psum, Args(
            x3=x3, x2=x2, rows=normed, base=base, w_ln=i["L0_ffn_w_ln2"], w_gate=i["L0_ffn_w_sh_gate"], w_up=i["L0_ffn_w_sh_up"],
            w_down=i["L0_ffn_w_sh_down"], w_router=i["L0_ffn_w_router"], w_eg=i["L0_ffn_w_sh_eg"], count8=i["expert_number"]), keep)
        routed_phase(nc, s, c, psum, Args(
            rows=normed, base=base, slots=slots, results=results, w_ln=i["L0_ffn_w_ln2"], w_gate=i["L0_ffn_w_gate_e"],
            w_up=i["L0_ffn_w_up_e"], w_down=i["L0_ffn_w_down_e"], count_t=i["tile_number"], out=rows(out)), keep)


def kernel(**inputs):
    import concourse.bacc as bacc
    from concourse.bass_utils import run_bass_kernel_spmd

    nc = bacc.Bacc("TRN2", target_bir_lowering=False, num_devices=1)
    arrays, args = {}, {}
    for name, value in [*inputs.items(), *shape_constants().items()]:
        array = np.ascontiguousarray(value)
        arrays[f"in_{name}"] = array
        args[name] = nc.dram_tensor(f"in_{name}", array.shape, mybir.dt.from_np(array.dtype), kind="ExternalInput").ap()
    out = nc.dram_tensor("out_x", (B, S, D), F32, kind="ExternalOutput").ap()
    build(nc, args, out)
    result = run_bass_kernel_spmd(nc, [arrays], core_ids=[0])
    return result.results[0]["out_x"]
```

```python
from contextlib import ExitStack

import numpy as np

import concourse.bass as bass
import concourse.mybir as mybir

F32 = mybir.dt.float32
F32R = mybir.dt.float32r
BF16 = mybir.dt.bfloat16
I32 = mybir.dt.int32
U32 = mybir.dt.uint32
ACT = mybir.ActivationFunctionType
ALU = mybir.AluOpType
AX_X = mybir.AxisListType.X

P = 128
B, S, D = 4, 512, 512
TT = S // P
KD = D // P
CTX = 256
MASKED = -1.0e30
HEADS_AT_ONCE = 4
STACK_SLOTS = 4
PROB_SLOTS = 8
MAX_ROW = 96
STACK_ROWS = MAX_ROW + 2 * HEADS_AT_ONCE


def hi_lo_passes(n_k):
    return [(k, a, b) for k in range(n_k) for a, b in ((0, 0), (0, 1), (1, 0))]


class Args:

    def __init__(self, **items):
        self.items = items

    def __getattr__(self, name):
        return self.items[name]


class Signals:

    def __init__(self, nc, names):
        self.nc = nc
        self.of = {n: nc.alloc_semaphore(n) for n in names}
        nums = sorted(s.num for s in self.of.values())
        assert nums == list(range(nums[0], nums[-1] + 1))
        self.range = range(nums[0], nums[-1] + 1)

    def __getattr__(self, name):
        return self.of[name]

    def range_of(self, semaphores):
        return range(min(x.num for x in semaphores), max(x.num for x in semaphores) + 1)

    def clear(self):
        self.nc.all_engine_barrier(sems_to_clear=self.range)


SIGNALS = [
    "raw_loaded0", "raw_loaded1", "hi_made", "lo_made", "table_loaded", "table_made", "const_made",
    "x_loaded0", "x_loaded1", "ctx_loaded", "pos_loaded", "ln_step", "var_ready", "std_ready", "norm_ready", "rms_ready",
    "rms_std", "transposed", "hT_hi", "hT_lo", "proj_done", "v_made", "v_stored0", "v_stored1", "h1_stored",
    "straight_made", "swap_made", "cos_made", "sin_made", "rotated", "parts_hi", "parts_lo", "qk_stored0", "qk_stored1",
    "pos_t", "pos_sb", "angles", "ang_step", "trig_made",
    "q_zeroed", "k_zeroed", "picks_made",
    "stack_loaded0", "stack_loaded1", "stack_loaded2", "stack_loaded3", "v_loaded0", "v_loaded1", "scores_ready", "max_done",
    "max_split", "max_transposed", "max_rows", "max_loaded", "scoresT_ready", "exp_done", "pv_done", "flip",
    "recip_made", "scaled", "attn_out", "attn_hi", "attn_lo", "attn_packed0", "attn_packed1", "out_proj", "out_made",
    "out_stored0", "out_stored1", "residual_made",
]


def make_constants(nc, s, c):
    with (
        nc.sbuf_tensor("maskq", [P, P], F32) as maskq,
        nc.sbuf_tensor("maskk", [P, P], F32) as maskk,
        nc.Block() as block,
    ):

        @block.gpsimd
        def _(pool):
            pool.memset(c.ident[:], 0.0).then_inc(s.const_made, 1)
            pool.memset(maskq[:], 0.0).then_inc(s.const_made, 1)
            pool.memset(maskk[:], 0.0).then_inc(s.const_made, 1)
            pool.memset(c.pick[:], 0.0).then_inc(s.const_made, 1)
            pool.wait_ge(s.const_made, 4)
            diag = dict(base=0, pattern=[[-1, P]], channel_multiplier=1)
            pool.affine_select(out=c.ident[:], in_=c.ident[:], compare_op=ALU.not_equal, fill=1.0,
                               **diag).then_inc(s.const_made, 1)
            pool.affine_select(out=maskq[:], in_=maskq[:], compare_op=ALU.is_ge, fill=MASKED,
                               **diag).then_inc(s.const_made, 1)
            pool.affine_select(out=maskk[:], in_=maskk[:], compare_op=ALU.is_ge, fill=MASKED,
                               base=0, pattern=[[1, P]], channel_multiplier=-1).then_inc(s.const_made, 1)
            for n, base in enumerate((0, -HEADS_AT_ONCE)):
                pool.wait_ge(s.const_made, 7 + n)
                pool.affine_select(out=c.pick[MAX_ROW:STACK_ROWS, :], in_=c.pick[MAX_ROW:STACK_ROWS, :],
                                   compare_op=ALU.not_equal, fill=1.0, base=base,
                                   pattern=[[-1, HEADS_AT_ONCE]], channel_multiplier=1).then_inc(s.const_made, 1)

        @block.vector
        def _(dve):
            nc.vector.memset(c.ones[:], 1.0).then_inc(s.table_made, 1)
            dve.wait_ge(s.const_made, 9)
            nc.vector.tensor_copy(c.identb[:], c.ident[:]).then_inc(s.table_made, 1)
            nc.vector.tensor_copy(c.maskqb[:], maskq[:]).then_inc(s.table_made, 1)
            nc.vector.tensor_copy(c.maskkb[:], maskk[:]).then_inc(s.table_made, 1)

    s.clear()


def split_weights(nc, s, jobs, raw):

    def staged(n, j):
        k, m = j[0].shape[1], j[0].shape[2]
        return raw[:, n % 2, 0 : k * m].rearrange("p (k n) -> p k n", k=k)

    with nc.Block() as block:

        @block.sync
        def _(sp):
            for n, j in enumerate(jobs):
                if n >= 2:
                    sp.wait_ge(s.hi_made, n - 1)
                    sp.wait_ge(s.lo_made, n - 1)
                sp.dma_start(staged(n, j), j[0], allow_slow_non_contiguous=True).then_inc((s.raw_loaded0, s.raw_loaded1)[n % 2], 16)

        @block.scalar
        def _(act):
            for n, j in enumerate(jobs):
                act.wait_ge((s.raw_loaded0, s.raw_loaded1)[n % 2], 16 * (n // 2 + 1))
                nc.scalar.activation(j[1], staged(n, j), ACT.Copy).then_inc(s.hi_made, 1)

        @block.vector
        def _(dve):
            for n, j in enumerate(jobs):
                dve.wait_ge(s.hi_made, n + 1)
                nc.vector.tensor_tensor(j[2], staged(n, j), j[1].bitcast(F32), ALU.subtract).then_inc(s.lo_made, 1)

    s.clear()


class Attention:

    def __init__(self, kind):
        self.kind = kind
        self.cross, self.rotary = kind == "cross", kind == "rotary"
        self.causal, self.rope = not self.cross, kind != "first"
        self.dh = 16 if self.cross else 32
        self.heads = D // self.dh
        self.groups = self.heads // HEADS_AT_ONCE
        self.scale = float(self.dh) ** -0.5
        self.n_kv = (CTX if self.cross else D) // P
        self.v_width = 2 * D if self.cross else D
        self.n_in = KD + (self.n_kv if self.cross else 0)


def projection_phase(nc, s, c, psum, a):
    t = Attention(a.kind)
    cross, rotary, rope = t.cross, t.rotary, t.rope
    BODY = a.body
    ctx = ExitStack()
    with ctx:
        sb = lambda name, shape, dt=F32: ctx.enter_context(nc.sbuf_tensor(f"{a.kind}_p_{name}", shape, dt))
        n_w = KD + 2 * t.n_kv
        w = [sb("w_hi", [P, n_w, D], F32R), sb("w_lo", [P, n_w, D], F32R)]
        at_w = {"q": 0, "k": KD, "v": KD + t.n_kv}
        raw = sb("raw", [P, 2, KD * D])
        xt = sb("xt", [P, 2, TT, D])
        h1 = sb("h1", [P, TT, D]) if rotary else None
        hn = sb("hn", [P, TT, D])
        IN_SLOTS = 2
        hT = [sb("hT_hi", [P, IN_SLOTS, t.n_in, S], F32R), sb("hT_lo", [P, IN_SLOTS, t.n_in, S], F32R)]
        v = sb("v", [P, 2, t.v_width])
        parts = sb("parts", [P, 2, 2, S], F32R)
        if rope:
            straight, swapped, turned = sb("straight", [P, 2, S]), sb("swapped", [P, 2, S]), sb("turned", [P, 2, S])
            TRIG_SLOTS = 2 if cross else 1
            cos_t, sin_t = sb("cos_t", [P, TRIG_SLOTS, S]), sb("sin_t", [P, TRIG_SLOTS, S])
        stats, mv = sb("stats", [P, TT, 6]), sb("mv", [P, TT, 2])
        std, rstd = sb("std", [P, TT]), sb("rstd", [P, TT])
        ssq, rms = sb("ssq", [P, TT]), sb("rms", [P, TT])
        if rotary:
            w_ln, bias_raw, bias_q = sb("w_ln", [P, KD]), sb("bias_raw", [P, 2, KD]), sb("bias_q", [P, KD])
            bv_row = sb("bv_row", [P, D])
        if cross:
            freq, sign = sb("freq", [2, P]), sb("sign", [P, 1])
            ctx_t, pos = sb("ctx_t", [P, TT, CTX]), sb("pos", [P, TT, 2])
            posT, turns = sb("posT", [2, S]), sb("turns", [P, S])
            ang = [sb("ang0", [P, S]), sb("ang1", [P, S])]

        cols = lambda m, n: m.rearrange("(k p) n -> p k n", p=P)[:, :, n * D : (n + 1) * D]
        jobs = []
        for what, src in (("q", a.wq), ("k", a.wk), ("v", a.wv)):
            n_k = KD if what == "q" else t.n_kv
            jobs.append((cols(*src), *(x[:, at_w[what] : at_w[what] + n_k, :] for x in w)))
        tables = []
        if rotary:
            tables = [(cos_t[:, 0], a.cos), (sin_t[:, 0], a.sin), (w_ln[:], a.w_ln.rearrange("(k p) -> p k", p=P)),
                      (bias_raw[:, 0, :], a.bq.rearrange("(k p) -> p k", p=P)),
                      (bias_raw[:, 1, :], a.bk.rearrange("(k p) -> p k", p=P)), (bv_row[:], a.bv.partition_broadcast(P))]
        if cross:
            tables = [(freq[:], a.freq), (sign[:], a.sign)]
        staged = lambda n: raw[:, n % 2, 0 : jobs[n][0].shape[1] * D].rearrange("p (k n) -> p k n", n=D)
        raw_loaded = (s.raw_loaded0, s.raw_loaded1)

        NORM_AT, ROOT_AT, TURN_AT = (0, 2, 4), (2, 4), 6
        ring = [(0, "pos", 0), (0, "angle", 0)] if cross else []
        for bi in range(BODY):
            for m in range(TT):
                if cross and m == TT - 1 and bi + 1 < BODY:
                    ring += [(bi + 1, "pos", 0), (bi + 1, "angle", 0)]
                ring += [(bi, "q", m), (bi, "k", m), (bi, "v", m)]
        n_v, n_qk = TT, 2 * KD
        ring_banks = (6, 7) if cross else (4, 5, 6, 7)
        N_RING = len(ring_banks)
        freed, count = [], {}
        for bi, what, m in ring:
            name = {"pos": "pos_sb", "angle": "ang_step", "v": "v_made"}.get(what, "straight_made" if rope else "parts_lo")
            count[name] = count.get(name, 0) + 1
            freed.append(("ang_step", 12 * bi + 1) if what == "angle" else (name, count[name]))
        qk_stored, v_stored = (s.qk_stored0, s.qk_stored1), (s.v_stored0, s.v_stored1)
        x_loaded = (s.x_loaded0, s.x_loaded1)

        with nc.Fori(0, B // BODY) as loop:
            rows = lambda m, bi: m[bass.ds((loop * BODY + bi) * S, S), :].rearrange("(t p) d -> p t d", p=P)
            with nc.Block() as block:

                @block.sync
                def _(sp):
                    def load(bi):
                        if bi >= 2:
                            sp.wait_ge(s.norm_ready, TT * (bi - 1))
                        sp.dma_start(xt[:, bi % 2], rows(a.x, bi)).then_inc(x_loaded[bi % 2], 16)
                        if cross:
                            if bi >= 1:
                                sp.wait_ge(s.transposed, 2 * bi)
                                sp.wait_ge(s.pos_t, bi)
                            sp.dma_start(ctx_t[:], rows(a.ctx, bi)).then_inc(s.ctx_loaded, 16)
                            sp.dma_start(pos[:], rows(a.pos, bi)).then_inc(s.pos_loaded, 16)

                    def load_weights(n):
                        if n >= 2:
                            sp.wait_ge(s.lo_made, n - 1)
                        sp.dma_start(staged(n), jobs[n][0]).then_inc(raw_loaded[n % 2], 16)

                    load(0)
                    load_weights(0)
                    for dst, src in tables:
                        sp.dma_start(dst, src, allow_slow_non_contiguous=True).then_inc(s.table_loaded, 16)
                    load_weights(1)
                    load_weights(2)
                    if cross:
                        sp.wait_ge(s.const_made, 2)
                    for bi in range(BODY):
                        if bi == 0:
                            load(1)
                        if rotary:
                            sp.wait_ge(s.norm_ready, TT * (bi + 1))
                            sp.dma_start(rows(a.h1, bi), h1[:]).then_inc(s.h1_stored, 16)
                        for m in range(TT):
                            if m == TT - 1 and bi + 2 < BODY:
                                load(bi + 2)
                            for i in (2 * m, 2 * m + 1):
                                n = bi * n_qk + i
                                sp.wait_ge(s.parts_hi, n + 1)
                                sp.wait_ge(s.parts_lo, n + 1)
                                dst = a.scratch[bass.ds(loop * BODY + bi, 1), i % 2, m * P : (m + 1) * P]
                                sp.dma_start(dst.rearrange("a p x n -> p (a x) n"), parts[:, n % 2].bitcast(F32)).then_inc(qk_stored[n % 2], 16)
                            n = bi * TT + m
                            sp.wait_ge(s.v_made, n + 1)
                            sp.dma_start(a.v[bass.ds((loop * BODY + bi) * S + m * P, P), :], v[:, n % 2]).then_inc(v_stored[n % 2], 16)
                    for st in v_stored:
                        sp.wait_ge(st, 16 * (BODY * TT // 2))
                    for st in qk_stored:
                        sp.wait_ge(st, 16 * (BODY * n_qk // 2))
                    if rotary:
                        sp.wait_ge(s.h1_stored, 16 * BODY)

                @block.tensor
                def _(pe):
                    def turn_in(bi):
                        if bi:
                            pe.wait_ge(s.hT_lo, t.n_in * bi)
                        for m in range(TT):
                            pe.wait_ge(s.norm_ready, bi * TT + m + 1)
                            for k in range(KD):
                                last = nc.tensor.transpose(psum[k][:, m * P : (m + 1) * P], hn[:, m, k * P : (k + 1) * P], c.ident[:])
                        last.then_inc(s.transposed, 1)
                        if cross:
                            pe.wait_ge(s.ctx_loaded, 16 * (bi + 1))
                            for k in range(t.n_kv):
                                for m in range(TT):
                                    last = nc.tensor.transpose(psum[KD + k][:, m * P : (m + 1) * P], ctx_t[:, m, k * P : (k + 1) * P], c.ident[:])
                            last.then_inc(s.transposed, 1)

                    turn_in(0)
                    for n, (bi, what, m) in enumerate(ring):
                        bank = psum[ring_banks[n % N_RING]]
                        if n >= N_RING:
                            name, value = freed[n - N_RING]
                            pe.wait_ge(s.of[name], value)
                        slot = bi % IN_SLOTS
                        if what == "pos":
                            pe.wait_ge(s.pos_loaded, 16 * (bi + 1))
                            for m_ in range(TT):
                                last = nc.tensor.transpose(bank[0:2, m_ * P : (m_ + 1) * P], pos[:, m_, :], c.ident[:])
                            last.then_inc(s.pos_t, 1)
                            continue
                        if what == "angle":
                            if bi == 0:
                                pe.wait_ge(s.table_loaded, 16 * len(tables))
                            pe.wait_ge(s.pos_sb, bi + 1)
                            nc.tensor.matmul(bank[:], freq[:], posT[:], start=True, stop=True).then_inc(s.angles, 1)
                            continue
                        if bi == 0 and (what, m) in (("v", 0), ("q", 0), ("k", 0)):
                            pe.wait_ge(s.lo_made, "qkv".index(what) + 1)
                        if (what, m) == ("q", 0):
                            pe.wait_ge(s.hT_hi, t.n_in * (bi + 1))
                            pe.wait_ge(s.hT_lo, t.n_in * (bi + 1))
                        nk, first = (t.n_kv if what in "kv" else KD), (KD if cross and what in "kv" else 0)
                        steps = hi_lo_passes(nk)
                        for i, (k, pa, pb) in enumerate(steps):
                            if what == "v":
                                lhs, rhs = hT[pa][:, slot, first + k, m * P : (m + 1) * P], w[pb][:, at_w[what] + k, :]
                            else:
                                lhs, rhs = w[pa][:, at_w[what] + k, m * P : (m + 1) * P], hT[pb][:, slot, first + k, :]
                            last = nc.tensor.matmul(bank[:], lhs, rhs, start=i == 0, stop=i == len(steps) - 1)
                        last.then_inc(s.proj_done, 1)
                        if what in "qk" and 2 * m + (what == "k") == TURN_AT and bi + 1 < BODY:
                            turn_in(bi + 1)

                def hT_high(act, bi):
                    if bi >= IN_SLOTS:
                        act.wait_ge(s.proj_done, (n_v + n_qk) * (bi - IN_SLOTS + 1))
                    for k in range(t.n_in):
                        act.wait_ge(s.transposed, (2 * bi + (1 if k < KD else 2)) if cross else bi + 1)
                        dst, src = hT[0][:, bi % IN_SLOTS, k, :], psum[k][:]
                        if rotary:
                            nc.scalar.activation(dst, src, ACT.Copy, scale=w_ln[:, k : k + 1]).then_inc(s.hT_hi, 1)
                        else:
                            nc.scalar.activation(dst, src, ACT.Copy).then_inc(s.hT_hi, 1)

                def hT_low(dve, bi):
                    for k in range(t.n_in):
                        dve.wait_ge(s.hT_hi, t.n_in * bi + k + 1)
                        dst, src, high = hT[1][:, bi % IN_SLOTS, k, :], psum[k][:], hT[0][:, bi % IN_SLOTS, k, :].bitcast(F32)
                        if rotary:
                            nc.vector.scalar_tensor_tensor(dst, src, w_ln[:, k : k + 1], high, ALU.mult, ALU.subtract).then_inc(s.hT_lo, 1)
                        else:
                            nc.vector.tensor_tensor(dst, src, high, ALU.subtract).then_inc(s.hT_lo, 1)

                @block.scalar
                def _(act):
                    def root(bi):
                        act.wait_ge(s.var_ready, bi + 1)
                        nc.scalar.activation(std[:], mv[:, :, 1], ACT.Sqrt).then_inc(s.std_ready, 1)

                    def root_of_squares(bi):
                        if rotary:
                            act.wait_ge(s.rms_ready, bi + 1)
                            nc.scalar.activation(rms[:], ssq[:], ACT.Sqrt).then_inc(s.rms_std, 1)

                    def high(n):
                        act.wait_ge(s.rotated, n + 1)
                        if n >= 2:
                            act.wait_ge(qk_stored[n % 2], 16 * (n // 2))
                        nc.scalar.activation(parts[:, n % 2, 0], turned[:, n % 2], ACT.Copy).then_inc(s.parts_hi, 1)

                    def trig(bi):
                        act.wait_ge(s.ang_step, 12 * (bi + 1))
                        if bi >= 2:
                            act.wait_ge(s.rotated, n_qk * (bi - 1))
                        nc.scalar.activation(sin_t[:, bi % 2], ang[0][:], ACT.Sin, scale=sign[:, 0:1]).then_inc(s.trig_made, 1)
                        nc.scalar.activation(cos_t[:, bi % 2], ang[1][:], ACT.Sin).then_inc(s.trig_made, 1)

                    def weights_high(n):
                        act.wait_ge(raw_loaded[n % 2], 16 * (n // 2 + 1))
                        nc.scalar.activation(jobs[n][1], staged(n), ACT.Copy).then_inc(s.hi_made, 1)

                    weights_high(0)
                    root(0)
                    root_of_squares(0)
                    weights_high(1)
                    if tables:
                        act.wait_ge(s.table_loaded, 16 * len(tables))
                    hT_high(act, 0)
                    weights_high(2)
                    done = 0
                    for n, (bi, what, m) in enumerate(ring):
                        bank = psum[ring_banks[n % N_RING]]
                        if what == "pos":
                            act.wait_ge(s.pos_t, bi + 1)
                            if bi:
                                act.wait_ge(s.angles, bi)
                            nc.scalar.activation(posT[:], bank[0:2, :], ACT.Copy).then_inc(s.pos_sb, 1)
                            continue
                        if what == "angle":
                            if bi == 0:
                                trig(0)
                            continue
                        done += 1
                        if what == "v":
                            i = bi * TT + m
                            if not rotary:
                                act.wait_ge(s.proj_done, done)
                                if i >= 2:
                                    act.wait_ge(v_stored[i % 2], 16 * (i // 2))
                                dst, src = v[:, i % 2], bank[:]
                                if cross:
                                    dst = dst.rearrange("p (h two d) -> p h two d", two=2, d=t.dh)[:, :, 0, :]
                                    src = src.rearrange("p (h d) -> p h d", d=t.dh)
                                nc.scalar.activation(dst, src, ACT.Copy).then_inc(s.v_made, 1)
                            if m == TT - 1 and cross and bi + 1 < BODY:
                                trig(bi + 1)
                            continue
                        if rotary and (bi, what, m) == (0, "q", 0):
                            act.wait_ge(s.table_made, 1)
                        i = bi * n_qk + 2 * m + (what == "k")
                        scale = t.scale if what == "q" else 1.0
                        act.wait_ge(s.proj_done, done)
                        if rope:
                            if i >= 2:
                                act.wait_ge(s.swap_made, i - 1)
                                act.wait_ge(s.cos_made, i - 1)
                            if rotary:
                                bias = bias_q[:, m : m + 1] if what == "q" else bias_raw[:, 1, m : m + 1]
                                nc.scalar.activation(straight[:, i % 2], bank[:], ACT.Identity, bias=bias, scale=scale).then_inc(s.straight_made, 1)
                            else:
                                nc.scalar.activation(straight[:, i % 2], bank[:], ACT.Copy, scale=scale).then_inc(s.straight_made, 1)
                            if i >= 2:
                                high(i - 2)
                            if i == BODY * n_qk - 1:
                                high(i - 1)
                                high(i)
                        else:
                            if i >= 2:
                                act.wait_ge(qk_stored[i % 2], 16 * (i // 2))
                            nc.scalar.activation(parts[:, i % 2, 0], bank[:], ACT.Copy, scale=scale).then_inc(s.parts_hi, 1)
                        if bi + 1 < BODY:
                            if i % n_qk == ROOT_AT[0]:
                                root(bi + 1)
                            if i % n_qk == ROOT_AT[1]:
                                root_of_squares(bi + 1)
                            if i % n_qk == TURN_AT:
                                hT_high(act, bi + 1)

                @block.vector
                def _(dve):
                    count = [0]

                    def small(ins):
                        count[0] += 1
                        ins.then_inc(s.ln_step, 1)
                        dve.wait_ge(s.ln_step, count[0])

                    def norm(bi, part):
                        x = xt[:, bi % 2]
                        if part == 0:
                            dve.wait_ge(x_loaded[bi % 2], 16 * (bi // 2 + 1))
                            for m in range(TT):
                                count[0] += 1
                                nc.vector.bn_stats(stats[:, m, :], x[:, m, :]).then_inc(s.ln_step, 1)
                            dve.wait_ge(s.ln_step, count[0])
                            for m in range(TT):
                                count[0] += 1
                                nc.vector.bn_aggr(mv[:, m, :], stats[:, m, :]).then_inc(s.ln_step, 1)
                            dve.wait_ge(s.ln_step, count[0])
                            nc.vector.tensor_scalar(mv[:, :, 1], mv[:, :, 1], 1e-5, None, ALU.add).then_inc(s.var_ready, 1)
                        if part == 1:
                            if bi:
                                dve.wait_ge(s.transposed, 2 * bi - 1 if cross else bi)
                            dve.wait_ge(s.std_ready, bi + 1)
                            small(nc.vector.reciprocal(rstd[:], std[:]))
                            if rotary and bi:
                                dve.wait_ge(s.h1_stored, 16 * bi)
                            for m in range(TT):
                                centred = nc.vector.tensor_scalar((h1 if rotary else hn)[:, m, :], x[:, m, :], mv[:, m, 0:1],
                                                                  rstd[:, m : m + 1], ALU.subtract, ALU.mult)
                                if rotary:
                                    count[0] += 1
                                    centred.then_inc(s.ln_step, 1)
                                else:
                                    centred.then_inc(s.norm_ready, 1)
                            if rotary:
                                dve.wait_ge(s.ln_step, count[0])
                                for m in range(TT):
                                    count[0] += 1
                                    nc.vector.tensor_tensor_reduce(out=hn[:, m, :], in0=h1[:, m, :], in1=h1[:, m, :], scale=1.0, scalar=0.0,
                                                                   op0=ALU.mult, op1=ALU.add, accum_out=ssq[:, m : m + 1]).then_inc(s.ln_step, 1)
                                dve.wait_ge(s.ln_step, count[0])
                                nc.vector.tensor_scalar(ssq[:], ssq[:], 1.0 / D, 1e-6, ALU.mult, ALU.add).then_inc(s.rms_ready, 1)
                        if part == 2 and rotary:
                            dve.wait_ge(s.rms_std, bi + 1)
                            small(nc.vector.reciprocal(rstd[:], rms[:]))
                            for m in range(TT):
                                nc.vector.tensor_scalar(hn[:, m, :], h1[:, m, :], rstd[:, m : m + 1], None, ALU.mult).then_inc(s.norm_ready, 1)

                    def angle_steps(bi, bank):
                        two_pi = 2.0 * np.pi
                        big = 6.28125
                        small_part = float(np.float32(two_pi - big))
                        n = 12 * bi
                        dve.wait_ge(s.angles, bi + 1)
                        if bi:
                            dve.wait_ge(s.trig_made, 2 * bi)
                        nc.vector.tensor_copy(ang[0][:], bank[:]).then_inc(s.ang_step, 1)
                        dve.wait_ge(s.ang_step, n + 1)
                        nc.vector.tensor_scalar(ang[1][:], ang[0][:], float(np.pi / 2), None, ALU.add).then_inc(s.ang_step, 1)
                        n += 2
                        for x in ang:
                            dve.wait_ge(s.ang_step, n)
                            nc.vector.tensor_scalar(turns[:], x[:], 1.0 / two_pi, 12582912.0, ALU.mult, ALU.add).then_inc(s.ang_step, 1)
                            dve.wait_ge(s.ang_step, n + 1)
                            nc.vector.tensor_scalar(turns[:], turns[:], 12582912.0, None, ALU.subtract).then_inc(s.ang_step, 1)
                            dve.wait_ge(s.ang_step, n + 2)
                            nc.vector.scalar_tensor_tensor(x[:], turns[:], -big, x[:], ALU.mult, ALU.add).then_inc(s.ang_step, 1)
                            dve.wait_ge(s.ang_step, n + 3)
                            nc.vector.scalar_tensor_tensor(x[:], turns[:], -small_part, x[:], ALU.mult, ALU.add).then_inc(s.ang_step, 1)
                            dve.wait_ge(s.ang_step, n + 4)
                            nc.vector.tensor_scalar(x[:], x[:], 3.1415925, -3.1415925, ALU.min, ALU.max).then_inc(s.ang_step, 1)
                            n += 5

                    def rotate(i):
                        dve.wait_ge(s.cos_made, i + 1)
                        dve.wait_ge(s.sin_made, i + 1)
                        nc.vector.tensor_tensor(turned[:, i % 2], turned[:, i % 2], swapped[:, i % 2], ALU.add).then_inc(s.rotated, 1)

                    def low(i):
                        dve.wait_ge(s.parts_hi, i + 1)
                        nc.vector.tensor_tensor(parts[:, i % 2, 1], turned[:, i % 2], parts[:, i % 2, 0].bitcast(F32), ALU.subtract).then_inc(s.parts_lo, 1)

                    def weights_low(n):
                        dve.wait_ge(s.hi_made, n + 1)
                        nc.vector.tensor_tensor(jobs[n][2], staged(n), jobs[n][1].bitcast(F32), ALU.subtract).then_inc(s.lo_made, 1)

                    for part in range(3):
                        norm(0, part)
                    weights_low(0)
                    if tables:
                        dve.wait_ge(s.table_loaded, 16 * len(tables))
                    if rotary:
                        nc.vector.tensor_scalar(bias_q[:], bias_raw[:, 0, :], t.scale, None, ALU.mult).then_inc(s.table_made, 1)
                    weights_low(1)
                    hT_low(dve, 0)
                    weights_low(2)
                    done = 0
                    for n, (bi, what, m) in enumerate(ring):
                        bank = psum[ring_banks[n % N_RING]]
                        if what == "pos":
                            continue
                        if what == "angle":
                            angle_steps(bi, bank)
                            continue
                        done += 1
                        if what == "v":
                            i = bi * TT + m
                            if rotary:
                                dve.wait_ge(s.proj_done, done)
                                if i >= 2:
                                    dve.wait_ge(v_stored[i % 2], 16 * (i // 2))
                                nc.vector.tensor_tensor(v[:, i % 2], bank[:], bv_row[:], ALU.add).then_inc(s.v_made, 1)
                            continue
                        i = bi * n_qk + 2 * m + (what == "k")
                        if rope:
                            dve.wait_ge(s.straight_made, i + 1)
                            if i % n_qk == 0 and cross:
                                dve.wait_ge(s.trig_made, 2 * (bi + 1))
                            if i >= 2:
                                dve.wait_ge(s.rotated, i - 1)
                            swap = [r ^ 1 for r in range(32)] if cross else [(r + 16) % 32 for r in range(32)]
                            nc.vector.stream_shuffle(swapped[:, i % 2], straight[:, i % 2], swap).then_inc(s.swap_made, 1)
                            if i >= 2:
                                low(i - 2)
                            if i >= 1:
                                rotate(i - 1)
                            if i == BODY * n_qk - 1:
                                rotate(i)
                                low(i - 1)
                                low(i)
                        else:
                            dve.wait_ge(s.parts_hi, i + 1)
                            nc.vector.scalar_tensor_tensor(parts[:, i % 2, 1], bank[:], t.scale if what == "q" else 1.0,
                                                           parts[:, i % 2, 0].bitcast(F32), ALU.mult, ALU.subtract).then_inc(s.parts_lo, 1)
                        if bi + 1 < BODY:
                            if i % n_qk in NORM_AT:
                                norm(bi + 1, NORM_AT.index(i % n_qk))
                            if i % n_qk == TURN_AT:
                                hT_low(dve, bi + 1)

                @block.gpsimd
                def _(pool):
                    if cross:
                        for slot in range(2):
                            pool.memset(v[:, slot].rearrange("p (h two d) -> p h two d", two=2, d=t.dh)[:, :, 1, :], 1.0).then_inc(s.const_made, 1)
                    if rotary:
                        pool.wait_ge(s.table_loaded, 16 * len(tables))
                    if rope:
                        for i in range(BODY * n_qk):
                            pool.wait_ge(s.straight_made, i + 1)
                            if i % n_qk == 0 and cross:
                                pool.wait_ge(s.trig_made, 2 * (i // n_qk + 1))
                            if i >= 2:
                                pool.wait_ge(s.parts_lo, i - 1)
                            nc.gpsimd.tensor_tensor(turned[:, i % 2], straight[:, i % 2], cos_t[:, i // n_qk % TRIG_SLOTS], ALU.mult).then_inc(s.cos_made, 1)
                            pool.wait_ge(s.swap_made, i + 1)
                            nc.gpsimd.tensor_tensor(swapped[:, i % 2], swapped[:, i % 2], sin_t[:, i // n_qk % TRIG_SLOTS], ALU.mult).then_inc(s.sin_made, 1)

            s.clear()


def core_phase(nc, s, c, psum, a):
    t = Attention(a.kind)
    cross, causal, dh, G = t.cross, t.causal, t.dh, t.groups
    BODY = a.body
    GROUPS = G * BODY
    N16 = TT * HEADS_AT_ONCE
    ctx = ExitStack()
    with ctx:
        sb = lambda name, shape, dt=F32: ctx.enter_context(nc.sbuf_tensor(f"{a.kind}_c_{name}", shape, dt))
        wo = [sb("wo_hi", [P, KD, D], F32R), sb("wo_lo", [P, KD, D], F32R)]
        v = sb("v", [P, 2, TT, t.v_width])
        xt = sb("xt", [P, TT, D])
        prob = sb("prob", [P, PROB_SLOTS, S])
        q_stack = sb("q_stack", [P, STACK_SLOTS, HEADS_AT_ONCE, S], F32R)
        k_stack = sb("k_stack", [P, STACK_SLOTS, HEADS_AT_ONCE, S], F32R)
        oT = sb("oT", [P, 1 if cross else 2, KD, 2, S], F32R)
        O_SLOTS = 1 if cross else 2
        neg_max = sb("neg_max", [P, 2, TT, HEADS_AT_ONCE])
        max_parts = sb("max_parts", [P, TT, 2 * HEADS_AT_ONCE], F32R)
        max_rows = sb("max_rows", [2 * HEADS_AT_ONCE, S], F32R)
        attn, flipped = sb("attn", [P, 2, S]), sb("flipped", [P, S])
        inverse = sb("inverse", [P, S // 32])
        attn_parts = sb("attn_parts", [P, 2, 2, S], F32R) if cross else None
        out_t = sb("out_t", [P, 2, D])
        if cross:
            bo_row = sb("bo_row", [P, D])

        cols = lambda m, n: m.rearrange("(k p) n -> p k n", p=P)[:, :, n * D : (n + 1) * D]

        AHEAD = N16 + a.lead
        SPLIT_STEP = N16 - 1 - a.lead
        MAX_STEP = 9
        NORM_STEP = a.norm_step
        OUT_STEPS = (1, 4, 10, 13)
        THIRDS = 3
        WEIGHTS_GROUP, WEIGHTS_STEPS = 1, (0, 3, 11, 14)

        width_q = lambda m: (m + 1) * P if causal else S
        start_k = lambda m: m * P if causal else 0
        bank_score, bank_scoreT = ((0, 1, 2), (3, 4, 5)) if cross else ((0, 1), (2, 3))
        bank_o, bank_sum = ((6,), 6) if cross else ((4, 5), 6)
        bank_out = bank_max = 7
        N_SCORE, N_SCORET, N_O = len(bank_score), len(bank_scoreT), len(bank_o)
        stack_loaded = (s.stack_loaded0, s.stack_loaded1, s.stack_loaded2, s.stack_loaded3)
        attn_packed = (s.attn_packed0, s.attn_packed1)
        v_loaded, out_stored = (s.v_loaded0, s.v_loaded1), (s.out_stored0, s.out_stored1)

        def tile_ahead(g, step):
            n = g * N16 + step + AHEAD
            return divmod(n, N16) if n < GROUPS * N16 else None

        def projected_at(g, step):
            if g >= G + 1 and (g - 1) % G == 0:
                for m, first in enumerate(OUT_STEPS):
                    if first <= step < first + THIRDS:
                        return (g - 1) // G - 1, m, step - first
            return None

        def outputs_before(g):
            return sum(1 for h in range(g) for step in range(N16)
                       if projected_at(h, step) and projected_at(h, step)[2] == THIRDS - 1 and (h, step) < (g - 1, MAX_STEP))

        def maxima_before(bi, m):
            h, step = (bi + 1) * G + 1, OUT_STEPS[m]
            return min(GROUPS, h + 1 + (step >= MAX_STEP))

        with nc.Fori(0, B // BODY) as loop:
            rows = lambda m, bi: m[bass.ds((loop * BODY + bi) * S, S), :].rearrange("(t p) d -> p t d", p=P)
            with nc.Block() as block:

                def load_stack(sp, g):
                    bi, h0 = g // G, (g % G) * HEADS_AT_ONCE * dh
                    if cross and g < STACK_SLOTS:
                        sp.wait_ge(s.q_zeroed, 2 * (g + 1))
                        sp.wait_ge(s.k_zeroed, 2 * (g + 1))
                    if g >= STACK_SLOTS:
                        sp.wait_ge(s.scoresT_ready, N16 * (g - STACK_SLOTS + 1))
                    for stack, w, order in ((q_stack, 0, (0, 1, 0)), (k_stack, 1, (0, 0, 1))):
                        src = a.scratch[bass.ds(loop * BODY + bi, 1), w, h0 : h0 + HEADS_AT_ONCE * dh]
                        for i, part in enumerate(order):
                            sp.dma_start(stack[i * dh : (i + 1) * dh, g % STACK_SLOTS].bitcast(F32),
                                         src[:, :, part, :].rearrange("a (h p) n -> p (a h) n", p=dh)).then_inc(stack_loaded[g % STACK_SLOTS], 16)

                def load_values(sp, bi):
                    if bi >= 2:
                        sp.wait_ge(s.pv_done, TT * G * (bi - 1))
                    sp.dma_start(v[:, bi % 2], rows(a.v, bi)).then_inc(v_loaded[bi % 2], 16)

                def load_residual(sp, bi):
                    if bi:
                        sp.wait_ge(s.out_made, TT * bi)
                    sp.dma_start(xt[:], rows(a.residual, bi)).then_inc(s.x_loaded0, 16)

                def send_max(sp, g):
                    sp.wait_ge(s.max_rows, g + 1)
                    sp.dma_start(q_stack[MAX_ROW:STACK_ROWS, g % STACK_SLOTS].bitcast(F32),
                                 max_rows[:].bitcast(F32).unsqueeze(1).to_broadcast([2 * HEADS_AT_ONCE, HEADS_AT_ONCE, S])).then_inc(s.max_loaded, 16)

                def pack(sp, g):
                    sp.wait_ge(s.attn_hi, g + 1)
                    sp.wait_ge(s.attn_lo, g + 1)
                    if g % G == 0 and g >= G:
                        sp.wait_ge(s.out_proj, TT * (g // G))
                    for j in range(HEADS_AT_ONCE):
                        r = (g % 2) * 64 + dh * j
                        sp.dma_start(oT[r : r + dh, 0, g % G // 2].bitcast(F32),
                                     attn_parts[32 * j : 32 * j + dh, g % 2].bitcast(F32)).then_inc(attn_packed[g % 2], 16)

                def store(sp, n):
                    bi, m = divmod(n, TT)
                    sp.wait_ge(s.out_made, n + 1)
                    sp.dma_start(a.out[bass.ds((loop * BODY + bi) * S + m * P, P), :], out_t[:, n % 2]).then_inc(out_stored[n % 2], 16)

                @block.sync
                def _(sp):
                    load_stack(sp, 0)
                    load_stack(sp, 1)
                    load_values(sp, 0)
                    if not cross:
                        load_stack(sp, 2)
                    sp.dma_start(xt[:], cols(*a.wo)).then_inc(s.raw_loaded0, 16)
                    if cross:
                        sp.dma_start(bo_row[:], a.bo.partition_broadcast(P)).then_inc(s.table_loaded, 16)
                    send_max(sp, 0)
                    if cross:
                        load_stack(sp, 2)
                    for g in range(GROUPS):
                        if g + 3 < GROUPS:
                            load_stack(sp, g + 3)
                        if g % G == min(2, G - 1) and g // G + 1 < BODY:
                            load_values(sp, g // G + 1)
                        projected = projected_at(g, OUT_STEPS[0])
                        if projected:
                            for m in range(2):
                                store(sp, projected[0] * TT + m)
                        if g + 1 < GROUPS:
                            send_max(sp, g + 1)
                        if g == WEIGHTS_GROUP:
                            sp.wait_ge(s.lo_made, KD)
                            load_residual(sp, 0)
                        if projected:
                            for m in range(2, TT):
                                store(sp, projected[0] * TT + m)
                            load_residual(sp, projected[0] + 1)
                        if cross and g:
                            pack(sp, g - 1)
                    if cross:
                        pack(sp, GROUPS - 1)
                    for m in range(TT):
                        store(sp, (BODY - 1) * TT + m)
                    for st in out_stored:
                        sp.wait_ge(st, 16 * (BODY * TT // 2))

                @block.tensor
                def _(pe):
                    def scores(g, i):
                        m, j = divmod(i, HEADS_AT_ONCE)
                        n, slot = g * N16 + i, g % STACK_SLOTS
                        bank = psum[bank_score[n % N_SCORE]]
                        if i == 0:
                            pe.wait_ge(stack_loaded[slot], 96 * (g // STACK_SLOTS + 1))
                        if n >= N_SCORE:
                            pe.wait_ge(s.max_done, n - N_SCORE + 1)
                        last = nc.tensor.matmul(bank[:, 0 : width_q(m)], q_stack[0:MAX_ROW, slot, j, m * P : (m + 1) * P],
                                                k_stack[0:MAX_ROW, slot, j, 0 : width_q(m)], start=True, stop=not causal)
                        if causal:
                            last = nc.tensor.matmul(bank[:, m * P : (m + 1) * P], c.identb[:], c.maskqb[:], start=False, stop=True)
                        last.then_inc(s.scores_ready, 1)

                    def max_transpose(g):
                        pe.wait_ge(s.max_split, 2 * (g + 1))
                        if outputs_before(g):
                            pe.wait_ge(s.out_made, outputs_before(g))
                        for m in range(TT):
                            last = nc.tensor.transpose(psum[bank_max][0 : 2 * HEADS_AT_ONCE, m * P : (m + 1) * P],
                                                       max_parts[:, m, :].bitcast(F32), c.ident[:])
                        last.then_inc(s.max_transposed, 1)

                    def scoresT(g, i):
                        m, j = divmod(i, HEADS_AT_ONCE)
                        n, slot = g * N16 + i, g % STACK_SLOTS
                        bank, q0 = psum[bank_scoreT[n % N_SCORET]], start_k(m)
                        if i == 0:
                            if g < STACK_SLOTS:
                                pe.wait_ge(s.picks_made, g + 1)
                            pe.wait_ge(s.max_loaded, 16 * (g + 1))
                        if n >= N_SCORET:
                            pe.wait_ge(s.exp_done, n - N_SCORET + 1)
                        last = nc.tensor.matmul(bank[:, 0 : S - q0], k_stack[0:STACK_ROWS, slot, j, m * P : (m + 1) * P],
                                                q_stack[0:STACK_ROWS, slot, j, q0:S], start=True, stop=not causal)
                        if causal:
                            last = nc.tensor.matmul(bank[:, 0:P], c.identb[:], c.maskkb[:], start=False, stop=True)
                        last.then_inc(s.scoresT_ready, 1)

                    def weighted(g, m):
                        q0, bi = start_k(m), g // G
                        if g % G == 0 and m == 0:
                            pe.wait_ge(v_loaded[bi % 2], 16 * (bi // 2 + 1))
                        pe.wait_ge(s.exp_done, g * N16 + (m + 1) * HEADS_AT_ONCE)
                        if m == 0 and g:
                            pe.wait_ge(s.flip, g)
                            if g >= N_O and not cross:
                                pe.wait_ge(s.attn_out, g - N_O + 1)
                        for bank in (bank_o[0],) if cross else (bank_o[g % N_O], bank_sum):
                            for j in range(HEADS_AT_ONCE):
                                pr = prob[:, (g * N16 + m * HEADS_AT_ONCE + j) % PROB_SLOTS, 0 : S - q0]
                                h = (g % G) * HEADS_AT_ONCE + j
                                val = c.ones[:] if bank == bank_sum and not cross else v[:, bi % 2, m, 32 * h : 32 * h + 32]
                                last = nc.tensor.matmul(psum[bank][32 * j : 32 * j + 32, q0:S], val, pr, start=m == 0, stop=m == TT - 1)
                        last.then_inc(s.pv_done, 1)

                    def project(bi, m, third):
                        n = bi * TT + m
                        if third == 0:
                            if m == 0 and cross:
                                for packed in attn_packed:
                                    pe.wait_ge(packed, 16 * HEADS_AT_ONCE * (G // 2) * (bi + 1))
                            elif m == 0:
                                pe.wait_ge(s.attn_hi, G * (bi + 1))
                                pe.wait_ge(s.attn_lo, G * (bi + 1))
                            if n == 0:
                                pe.wait_ge(s.lo_made, KD)
                            if n:
                                pe.wait_ge(s.out_made, n)
                            pe.wait_ge(s.max_rows, maxima_before(bi, m))
                        steps = list(enumerate(hi_lo_passes(KD)))
                        for i, (k, pa, pb) in steps[third * len(steps) // THIRDS : (third + 1) * len(steps) // THIRDS]:
                            last = nc.tensor.matmul(psum[bank_out][:], oT[:, bi % O_SLOTS, k, pa, m * P : (m + 1) * P], wo[pb][:, k, :],
                                                    start=i == 0, stop=i == len(steps) - 1)
                        if third == THIRDS - 1:
                            last.then_inc(s.out_proj, 1)

                    for i in range(N16):
                        scores(0, i)
                    for i in range(a.lead):
                        scores(1, i)
                        if i == 2:
                            max_transpose(0)
                    for g in range(GROUPS):
                        for step in range(N16):
                            if tile_ahead(g, step):
                                scores(*tile_ahead(g, step))
                            scoresT(g, step)
                            if step == MAX_STEP and g + 1 < GROUPS:
                                max_transpose(g + 1)
                            if step % HEADS_AT_ONCE == HEADS_AT_ONCE - 1:
                                m = step // HEADS_AT_ONCE
                                if m:
                                    weighted(g, m - 1)
                                elif g:
                                    weighted(g - 1, TT - 1)
                            if projected_at(g, step):
                                project(*projected_at(g, step))
                    weighted(GROUPS - 1, TT - 1)
                    for m in range(TT):
                        for third in range(THIRDS):
                            project(BODY - 1, m, third)

                @block.scalar
                def _(act):
                    def take_max(g):
                        act.wait_ge(s.max_transposed, g + 1)
                        if g:
                            act.wait_ge(s.max_loaded, 16 * g)
                        nc.scalar.activation(max_rows[:], psum[bank_max][0 : 2 * HEADS_AT_ONCE, :], ACT.Copy).then_inc(s.max_rows, 1)

                    def attn_high(g):
                        act.wait_ge(s.attn_out, g + 1)
                        if cross:
                            if g >= 2:
                                act.wait_ge(attn_packed[g % 2], 16 * HEADS_AT_ONCE * (g // 2))
                            dst = attn_parts[:, g % 2, 0]
                        else:
                            if g >= O_SLOTS * G and g % G == 0:
                                act.wait_ge(s.out_proj, TT * (g // G - O_SLOTS + 1))
                            dst = oT[:, g // G % O_SLOTS, g % G, 0]
                        nc.scalar.activation(dst, attn[:, g % 2], ACT.Copy).then_inc(s.attn_hi, 1)

                    for slot in range(STACK_SLOTS):
                        nc.scalar.activation(
                            k_stack[MAX_ROW:STACK_ROWS, slot],
                            c.pick[MAX_ROW:STACK_ROWS, :].unsqueeze(2).to_broadcast([2 * HEADS_AT_ONCE, HEADS_AT_ONCE, S]),
                            ACT.Copy).then_inc(s.picks_made, 1)
                    take_max(0)
                    for g in range(GROUPS):
                        for step in range(N16):
                            n = g * N16 + step
                            q0 = start_k(step // HEADS_AT_ONCE)
                            act.wait_ge(s.scoresT_ready, n + 1)
                            if n >= PROB_SLOTS:
                                act.wait_ge(s.pv_done, (n - PROB_SLOTS) // HEADS_AT_ONCE + 1)
                            nc.scalar.activation(prob[:, n % PROB_SLOTS, 0 : S - q0], psum[bank_scoreT[n % N_SCORET]][:, 0 : S - q0],
                                                 ACT.Exp).then_inc(s.exp_done, 1)
                            if step == MAX_STEP and g + 1 < GROUPS:
                                take_max(g + 1)
                            if step == NORM_STEP + 3 and g:
                                attn_high(g - 1)
                            if g == WEIGHTS_GROUP and step in WEIGHTS_STEPS:
                                k = WEIGHTS_STEPS.index(step)
                                act.wait_ge(s.raw_loaded0, 16)
                                nc.scalar.activation(wo[0][:, k, :], xt[:, k, :], ACT.Copy).then_inc(s.hi_made, 1)
                    attn_high(GROUPS - 1)

                @block.vector
                def _(dve):
                    def tile_max(g, i):
                        m, j = divmod(i, HEADS_AT_ONCE)
                        n = g * N16 + i
                        dve.wait_ge(s.scores_ready, n + 1)
                        nc.vector.tensor_reduce(neg_max[:, g % 2, m, j : j + 1], psum[bank_score[n % N_SCORE]][:, 0 : width_q(m)], AX_X, ALU.max,
                                                negate=True).then_inc(s.max_done, 1)

                    def split_max(g):
                        dve.wait_ge(s.max_done, N16 * (g + 1))
                        if g:
                            dve.wait_ge(s.max_transposed, g)
                        high, low = max_parts[:, :, 0:HEADS_AT_ONCE], max_parts[:, :, HEADS_AT_ONCE:]
                        nc.vector.tensor_copy(high, neg_max[:, g % 2]).then_inc(s.max_split, 1)
                        dve.wait_ge(s.max_split, 2 * g + 1)
                        nc.vector.tensor_tensor(low, neg_max[:, g % 2], high.bitcast(F32), ALU.subtract).then_inc(s.max_split, 1)

                    def normalise(g):
                        dve.wait_ge(s.pv_done, TT * (g + 1))
                        if g:
                            dve.wait_ge(s.attn_out, g)
                        blocks = flipped[:].rearrange("p (b c) -> p b c", c=32)
                        sums = psum[bank_sum]
                        of_block = inverse[:].unsqueeze(2)
                        nc.vector.transpose(flipped[:], sums[:]).then_inc(s.flip, 1)
                        dve.wait_ge(s.flip, g + 1)
                        nc.vector.reciprocal(inverse[:], blocks[:, :, dh if cross else 0]).then_inc(s.recip_made, 1)
                        dve.wait_ge(s.recip_made, g + 1)
                        if g >= 2:
                            dve.wait_ge(s.attn_hi, g - 1)
                            dve.wait_ge(s.attn_lo, g - 1)
                        if cross:
                            nc.vector.tensor_tensor(blocks[:, :, 0:dh], blocks[:, :, 0:dh], of_block.to_broadcast([P, S // 32, dh]),
                                                    ALU.mult).then_inc(s.scaled, 1)
                            dve.wait_ge(s.scaled, g + 1)
                            nc.vector.transpose(attn[:, g % 2], flipped[:]).then_inc(s.attn_out, 1)
                        else:
                            nc.vector.transpose(flipped[:], of_block.to_broadcast([P, S // 32, 32])).then_inc(s.scaled, 1)
                            dve.wait_ge(s.scaled, g + 1)
                            nc.vector.tensor_tensor(attn[:, g % 2], psum[bank_o[g % N_O]][:], flipped[:], ALU.mult).then_inc(s.attn_out, 1)

                    def add_residual(bi, m):
                        n = bi * TT + m
                        if m == 0:
                            dve.wait_ge(s.x_loaded0, 16 * (bi + 1))
                            if cross:
                                dve.wait_ge(s.residual_made, TT * (bi + 1))
                        dve.wait_ge(s.out_proj, n + 1)
                        if n >= 2:
                            dve.wait_ge(out_stored[n % 2], 16 * (n // 2))
                        nc.vector.tensor_tensor(out_t[:, n % 2], psum[bank_out][:], xt[:, m, :], ALU.add).then_inc(s.out_made, 1)

                    def zero_rows(slot):
                        if cross:
                            for r0 in (32, 64):
                                nc.vector.memset(k_stack[r0 : r0 + 32, slot].bitcast(F32), 0.0).then_inc(s.k_zeroed, 1)

                    zero_rows(0)
                    zero_rows(1)
                    for i in range(N16):
                        tile_max(0, i)
                    for i in range(a.lead):
                        tile_max(1, i)
                        if i == 0:
                            split_max(0)
                        if i == 2:
                            zero_rows(2)
                    zero_rows(3)
                    for g in range(GROUPS):
                        for step in range(N16):
                            if tile_ahead(g, step):
                                tile_max(*tile_ahead(g, step))
                            if step == NORM_STEP and g:
                                normalise(g - 1)
                            if step == SPLIT_STEP + 1 and g + 1 < GROUPS:
                                split_max(g + 1)
                            if g == WEIGHTS_GROUP and step in WEIGHTS_STEPS:
                                k = WEIGHTS_STEPS.index(step)
                                dve.wait_ge(s.hi_made, k + 1)
                                nc.vector.tensor_tensor(wo[1][:, k, :], xt[:, k, :], wo[0][:, k, :].bitcast(F32), ALU.subtract).then_inc(s.lo_made, 1)
                            projected = projected_at(g, step)
                            if projected and projected[2] == THIRDS - 1:
                                add_residual(projected[0], projected[1])
                    normalise(GROUPS - 1)
                    for m in range(TT):
                        add_residual(BODY - 1, m)

                @block.gpsimd
                def _(pool):
                    def bias_residual(bi):
                        pool.wait_ge(s.x_loaded0, 16 * (bi + 1))
                        for m in range(TT):
                            nc.gpsimd.tensor_tensor(xt[:, m, :], xt[:, m, :], bo_row[:], ALU.add).then_inc(s.residual_made, 1)

                    def attn_low(g):
                        pool.wait_ge(s.attn_hi, g + 1)
                        if cross:
                            if g >= 2:
                                pool.wait_ge(attn_packed[g % 2], 16 * HEADS_AT_ONCE * (g // 2))
                            parts = attn_parts[:, g % 2]
                        else:
                            parts = oT[:, g // G % O_SLOTS, g % G]
                        nc.gpsimd.tensor_tensor(parts[:, 1], attn[:, g % 2], parts[:, 0].bitcast(F32), ALU.subtract).then_inc(s.attn_lo, 1)

                    if cross:
                        for slot in range(STACK_SLOTS):
                            for r0 in (32, 64):
                                pool.memset(q_stack[r0 : r0 + 32, slot].bitcast(F32), 0.0).then_inc(s.q_zeroed, 1)
                        pool.wait_ge(s.table_loaded, 16)
                    for g in range(GROUPS):
                        attn_low(g)
                        if cross and g % G == 3:
                            bias_residual(g // G)

            s.clear()


EXPERTS, TOP, FE, FS = 8, 2, 352, 1408
N_TILES = B * TT
SLOT_TILES = (B * S * TOP + EXPERTS * (P - 1)) // P
SLOTS = SLOT_TILES * P
KF = FS // P
FE_K = [(0, P), (P, P), (2 * P, FE - 2 * P)]

MOE_SIGNALS = [
    "m_table", "m_const", "m_x_loaded0", "m_x_loaded1", "m_squares", "m_var", "m_std", "m_rstd", "m_normed",
    "m_rows_stored0", "m_rows_stored1", "m_weights", "m_turned", "m_hi", "m_lo", "m_router", "m_logits_sb", "m_logits",
    "m_step", "m_shifted", "m_exp", "m_chosen", "m_counted", "m_hot_made", "m_hot_used", "m_owners",
    "e_index", "e_row0", "e_row1", "e_row2", "e_row3", "e_turned", "e_hT", "e_gate_up", "e_silu", "e_inner", "e_inner_turned",
    "e_innerT01", "e_innerT", "e_down", "e_result", "e_stored0", "e_stored1",
    "s_rows", "s_x2", "s_x3", "s_turned", "s_hi", "s_lo", "s_gate_up", "s_silu", "s_inner", "s_inner_hi", "s_inner_lo", "s_down",
    "s_residual", "s_got", "s_added", "s_out", "s_stored",
]


def router_phase(nc, s, c, psum, a, keep, w_gu, w_dn):
    NT, E = N_TILES, EXPERTS
    n_col = E + 1
    GROUP = 8
    ctx = ExitStack()
    with ctx:
        sb = lambda name, shape, dt=F32: ctx.enter_context(nc.sbuf_tensor(f"router_{name}", shape, dt))
        wr, wr_raw = [sb(f"wr{i}", [P, KD, n_col], F32R) for i in range(2)], sb("wr_raw", [P, KD, n_col])
        TABLES = 7
        xt, squares = sb("xt", [P, 2, TT, D]), sb("squares", [P, TT, D])
        hT = [sb(f"hT{i}", [P, KD, S], F32R) for i in range(2)]
        w_ln, rows8, count_t, ids = sb("w_ln", [P, KD]), sb("rows8", [P, E]), sb("count_t", [P, SLOT_TILES]), sb("ids", [P, NT])
        counts = sb("counts", [P, P])
        rt = sb("rt", [n_col, S])
        ssq, std, rstd = sb("ssq", [P, TT]), sb("std", [P, TT]), sb("rstd", [P, TT])
        logit, nmax, ex = sb("logit", [P, NT, n_col]), sb("nmax", [P, NT]), sb("ex", [P, NT, E])
        total, best = sb("total", [P, NT]), sb("best", [P, NT, 8])
        where, wheref = sb("where", [P, NT, 8], U32), sb("wheref", [P, NT, 8])
        below, allones = sb("below", [P, P]), sb("allones", [P, P])
        hot, both = sb("hot", [P, TOP, NT, E]), sb("both", [P, NT, E])
        pre, tot, carry = sb("pre", [P, NT, E]), sb("tot", [P, NT, E]), sb("carry", [P, NT + 1, E])
        tiles_i, tiles_f, begin = sb("tiles_i", [P, E], I32), sb("tiles_f", [P, E]), sb("begin", [P, E + 1])
        pick, slot_f = sb("pick", [P, TOP, NT, E]), sb("slot_f", [P, TOP, NT])
        tile_i, tile_f, place = sb("tile_i", [P, TOP, NT], I32), sb("tile_f", [P, TOP, NT]), sb("place", [P, TOP, NT])
        hot_tile = sb("hot_tile", [P, 2, GROUP, SLOT_TILES])
        passed, owner_f = sb("passed", [P, SLOT_TILES, E]), sb("owner_f", [P, SLOT_TILES])
        x_loaded, rows_stored = (s.m_x_loaded0, s.m_x_loaded1), (s.m_rows_stored0, s.m_rows_stored1)
        rows = lambda m, b: m[b * S : (b + 1) * S, :].rearrange("(t p) d -> p t d", p=P)

        def hot_place(g):
            return squares[:, (g % 2) * 2 : (g % 2) * 2 + 2, :].rearrange("p a (b n) -> p (a b) n", n=P)

        with nc.Block() as block:

            @block.sync
            def _(sp):
                def weights(e):
                    for dst, src in ((w_gu[:, e, :, 0:FE], a.w_gate[e]), (w_gu[:, e, :, FE : 2 * FE], a.w_up[e])):
                        sp.dma_start(dst, src.rearrange("(k p) n -> p k n", p=P)).then_inc(s.m_weights, 16)
                    sp.dma_start(w_dn[:, e, 0:2, :], a.w_down[e][0 : 2 * P, :].rearrange("(k p) n -> p k n", p=P)).then_inc(s.m_weights, 16)
                    sp.dma_start(w_dn[0 : FE - 2 * P, e, 2, :], a.w_down[e][2 * P : FE, :]).then_inc(s.m_weights, 16)

                sp.dma_start(xt[:, 0], rows(a.x3, 0)).then_inc(x_loaded[0], 16)
                sp.dma_start(w_ln[:], a.w_ln.rearrange("(k p) -> p k", p=P), allow_slow_non_contiguous=True).then_inc(s.m_table, 16)
                for dst, src in ((rows8, a.count8), (count_t, a.count_t), (counts, a.count_p)):
                    sp.dma_start(dst[:], src.partition_broadcast(P)).then_inc(s.m_table, 16)
                sp.dma_start(ids[:], a.token_ids).then_inc(s.m_table, 16)
                for src, cols in ((a.w_router, slice(0, E)), (a.w_eg, slice(E, n_col))):
                    sp.dma_start(wr_raw[:, :, cols], src.rearrange("(k p) n -> p k n", p=P), allow_slow_non_contiguous=True).then_inc(s.m_table, 16)
                sp.dma_start(xt[:, 1], rows(a.x3, 1)).then_inc(x_loaded[1], 16)
                weights(0)
                for b in range(B):
                    sp.wait_ge(s.m_normed, TT * (b + 1))
                    sp.dma_start(rows(a.rows, b), xt[:, b % 2]).then_inc(rows_stored[b % 2], 16)
                    if b + 2 < B:
                        sp.wait_ge(rows_stored[b % 2], 16 * (b // 2 + 1))
                        sp.wait_ge(s.m_turned, b + 1)
                        sp.dma_start(xt[:, b % 2], rows(a.x3, b + 2)).then_inc(x_loaded[b % 2], 16)
                for e in range(1, E):
                    weights(e)
                for m in range(2):
                    sp.wait_ge(rows_stored[m], 16 * (B // 2))
                sp.wait_ge(s.m_weights, 16 * 4 * E)

            @block.gpsimd
            def _(pool):
                pool.memset(below[:], 1.0).then_inc(s.m_const, 1)
                pool.memset(allones[:], 1.0).then_inc(s.m_const, 1)
                pool.wait_ge(s.m_const, 2)
                pool.affine_select(out=below[:], in_=below[:], compare_op=ALU.is_gt, fill=0.0, base=0,
                                   pattern=[[1, P]], channel_multiplier=-1).then_inc(s.m_const, 1)

            @block.tensor
            def _(pe):
                def logits(b):
                    pe.wait_ge(s.m_logits_sb, b + 1)
                    for t in range(TT):
                        at = (b * TT + t) * 16
                        last = nc.tensor.transpose(psum[6][:, at : at + n_col], rt[:, t * P : (t + 1) * P], c.ident[0:n_col, 0:n_col])
                    last.then_inc(s.m_logits, 1)

                for b in range(B):
                    if b:
                        pe.wait_ge(s.m_lo, KD * b)
                    for t in range(TT):
                        pe.wait_ge(s.m_normed, b * TT + t + 1)
                        for k in range(KD):
                            last = nc.tensor.transpose(psum[k][:, t * P : (t + 1) * P], xt[:, b % 2, t, k * P : (k + 1) * P], c.ident[:])
                    last.then_inc(s.m_turned, 1)
                    if b:
                        logits(b - 1)
                    if b == 0:
                        pe.wait_ge(s.lo_made, 1)
                    pe.wait_ge(s.m_hi, KD * (b + 1))
                    pe.wait_ge(s.m_lo, KD * (b + 1))
                    steps = hi_lo_passes(KD)
                    for n, (k, pa, pb) in enumerate(steps):
                        last = nc.tensor.matmul(psum[4][0:n_col, :], wr[pa][:, k, :], hT[pb][:, k, :], start=n == 0, stop=n == len(steps) - 1)
                    last.then_inc(s.m_router, 1)
                logits(B - 1)
                pe.wait_ge(s.m_const, 3)
                pe.wait_ge(s.m_chosen, 1)
                flat = both[:].rearrange("p t e -> p (t e)")
                nc.tensor.matmul(psum[0][:, 0 : NT * E], below[:], flat, start=True, stop=True).then_inc(s.m_counted, 1)
                nc.tensor.matmul(psum[1][:, 0 : NT * E], allones[:], flat, start=True, stop=True).then_inc(s.m_counted, 1)
                n_groups = TOP * NT // GROUP
                for g in range(n_groups):
                    pe.wait_ge(s.m_hot_made, 3 * (g + 1))
                    for n in range(GROUP):
                        last = nc.tensor.matmul(psum[2][:, 0:SLOT_TILES], hot_place(g)[:, n, :], hot_tile[:, g % 2, n, :],
                                                start=g == 0 and n == 0, stop=g == n_groups - 1 and n == GROUP - 1)
                    last.then_inc(s.m_hot_used, 1)

            @block.scalar
            def _(act):
                for b in range(B):
                    act.wait_ge(s.m_var, b + 1)
                    nc.scalar.activation(std[:], ssq[:], ACT.Sqrt).then_inc(s.m_std, 1)
                    if b == 0:
                        act.wait_ge(s.m_table, 16 * TABLES)
                        nc.scalar.activation(wr[0][:], wr_raw[:], ACT.Copy).then_inc(s.hi_made, 1)
                    act.wait_ge(s.m_turned, b + 1)
                    if b:
                        act.wait_ge(s.m_router, b)
                    for k in range(KD):
                        nc.scalar.activation(hT[0][:, k, :], psum[k][:], ACT.Copy, scale=w_ln[:, k : k + 1]).then_inc(s.m_hi, 1)
                    act.wait_ge(s.m_router, b + 1)
                    if b:
                        act.wait_ge(s.m_logits, b)
                    nc.scalar.activation(rt[:], psum[4][0:n_col, :], ACT.Copy).then_inc(s.m_logits_sb, 1)
                act.wait_ge(s.m_shifted, 1)
                nc.scalar.activation(ex[:], ex[:], ACT.Exp).then_inc(s.m_exp, 1)
                nc.scalar.activation(keep.gate[:], logit[:, :, E], ACT.Exp, scale=-1.0).then_inc(s.m_exp, 1)

            @block.vector
            def _(dve):
                done = [0]

                def step(ins):
                    done[0] += 1
                    ins.then_inc(s.m_step, 1)
                    dve.wait_ge(s.m_step, done[0])

                dve.wait_ge(s.m_table, 16 * TABLES)
                for b in range(B):
                    x = xt[:, b % 2]
                    dve.wait_ge(x_loaded[b % 2], 16 * (b // 2 + 1))
                    if b:
                        dve.wait_ge(s.m_normed, TT * b)
                    for t in range(TT):
                        nc.vector.tensor_tensor_reduce(out=squares[:, t, :], in0=x[:, t, :], in1=x[:, t, :], scale=1.0, scalar=0.0,
                                                       op0=ALU.mult, op1=ALU.add, accum_out=ssq[:, t : t + 1]).then_inc(s.m_squares, 1)
                    dve.wait_ge(s.m_squares, TT * (b + 1))
                    nc.vector.tensor_scalar(ssq[:], ssq[:], 1.0 / D, 1e-6, ALU.mult, ALU.add).then_inc(s.m_var, 1)
                    dve.wait_ge(s.m_std, b + 1)
                    nc.vector.reciprocal(rstd[:], std[:]).then_inc(s.m_rstd, 1)
                    dve.wait_ge(s.m_rstd, b + 1)
                    for t in range(TT):
                        nc.vector.tensor_scalar(x[:, t, :], x[:, t, :], rstd[:, t : t + 1], None, ALU.mult).then_inc(s.m_normed, 1)
                    if b == 0:
                        dve.wait_ge(s.hi_made, 1)
                        nc.vector.tensor_tensor(wr[1][:], wr_raw[:], wr[0][:].bitcast(F32), ALU.subtract).then_inc(s.lo_made, 1)
                    for k in range(KD):
                        dve.wait_ge(s.m_hi, KD * b + k + 1)
                        nc.vector.scalar_tensor_tensor(hT[1][:, k, :], psum[k][:], w_ln[:, k : k + 1],
                                                       hT[0][:, k, :].bitcast(F32), ALU.mult, ALU.subtract).then_inc(s.m_lo, 1)
                dve.wait_ge(s.m_logits, B)
                step(nc.vector.tensor_copy(logit[:], psum[6][:, 0 : 16 * NT].rearrange("p (t e) -> p t e", e=16)[:, :, 0:n_col]))
                step(nc.vector.tensor_reduce(nmax[:], logit[:, :, 0:E], AX_X, ALU.max, negate=True))
                nc.vector.tensor_tensor(ex[:], logit[:, :, 0:E], nmax[:].unsqueeze(2).to_broadcast([P, NT, E]), ALU.add).then_inc(s.m_shifted, 1)
                dve.wait_ge(s.m_exp, 2)
                step(nc.vector.tensor_reduce(total[:], ex[:], AX_X, ALU.add))
                step(nc.vector.reciprocal(total[:], total[:]))
                step(nc.vector.tensor_scalar(keep.gate[:], keep.gate[:], 1.0, None, ALU.add))
                step(nc.vector.reciprocal(keep.gate[:], keep.gate[:]))
                step(nc.vector.tensor_tensor(ex[:], ex[:], total[:].unsqueeze(2).to_broadcast([P, NT, E]), ALU.mult))
                for t in range(NT):
                    done[0] += 1
                    nc.vector.max(best[:, t, :], ex[:, t, :]).then_inc(s.m_step, 1)
                dve.wait_ge(s.m_step, done[0])
                for t in range(NT):
                    done[0] += 1
                    nc.vector.max_index(where[:, t, :], best[:, t, :], ex[:, t, :]).then_inc(s.m_step, 1)
                dve.wait_ge(s.m_step, done[0])
                step(nc.vector.tensor_copy(wheref[:], where[:]))
                step(nc.vector.tensor_copy(keep.weight[:], best[:, :, 0:TOP]))
                for j in range(TOP):
                    step(nc.vector.tensor_tensor(hot[:, j], rows8[:].unsqueeze(1).to_broadcast([P, NT, E]),
                                                 wheref[:, :, j : j + 1].to_broadcast([P, NT, E]), ALU.is_equal))
                nc.vector.tensor_tensor(both[:], hot[:, 0], hot[:, 1], ALU.add).then_inc(s.m_chosen, 1)
                dve.wait_ge(s.m_counted, 2)
                step(nc.vector.tensor_copy(pre[:].rearrange("p t e -> p (t e)"), psum[0][:, 0 : NT * E]))
                step(nc.vector.tensor_copy(tot[:].rearrange("p t e -> p (t e)"), psum[1][:, 0 : NT * E]))
                step(nc.vector.memset(carry[:, 0, :], 0.0))
                for t in range(NT):
                    step(nc.vector.tensor_tensor(carry[:, t + 1, :], carry[:, t, :], tot[:, t, :], ALU.add))
                step(nc.vector.tensor_scalar(tiles_i[:], carry[:, NT, :], float(P - 1), None, ALU.add))
                step(nc.vector.tensor_scalar(tiles_i[:], tiles_i[:], P.bit_length() - 1, None, ALU.arith_shift_right))
                step(nc.vector.tensor_copy(tiles_f[:], tiles_i[:]))
                step(nc.vector.memset(begin[:, 0:1], 0.0))
                for e in range(E):
                    step(nc.vector.tensor_tensor(begin[:, e + 1 : e + 2], begin[:, e : e + 1], tiles_f[:, e : e + 1], ALU.add))
                step(nc.vector.tensor_tensor(pre[:], pre[:], carry[:, 0:NT, :], ALU.add))
                step(nc.vector.tensor_scalar(tiles_f[:], begin[:, 0:E], float(P), None, ALU.mult))
                step(nc.vector.tensor_tensor(pre[:], pre[:], tiles_f[:].unsqueeze(1).to_broadcast([P, NT, E]), ALU.add))
                for j in range(TOP):
                    step(nc.vector.tensor_tensor(pick[:, j], hot[:, j], pre[:], ALU.mult))
                    step(nc.vector.tensor_reduce(slot_f[:, j, :], pick[:, j], AX_X, ALU.add))
                step(nc.vector.tensor_copy(keep.slot[:], slot_f[:]))
                step(nc.vector.tensor_copy(tile_i[:], slot_f[:]))
                step(nc.vector.tensor_scalar(tile_i[:], tile_i[:], P.bit_length() - 1, None, ALU.arith_shift_right))
                step(nc.vector.tensor_copy(tile_f[:], tile_i[:]))
                step(nc.vector.scalar_tensor_tensor(place[:], tile_f[:], -float(P), slot_f[:], ALU.mult, ALU.add))
                for g in range(TOP * NT // GROUP):
                    j, t0 = divmod(g * GROUP, NT)
                    if g >= 2:
                        dve.wait_ge(s.m_hot_used, g - 1)
                    of = lambda m: m[:, j, t0 : t0 + GROUP].unsqueeze(2)
                    tiles = hot_tile[:, g % 2]
                    nc.vector.tensor_tensor(hot_place(g), counts[:].unsqueeze(1).to_broadcast([P, GROUP, P]),
                                            of(place).to_broadcast([P, GROUP, P]), ALU.is_equal).then_inc(s.m_hot_made, 1)
                    nc.vector.tensor_tensor(tiles, count_t[:].unsqueeze(1).to_broadcast([P, GROUP, SLOT_TILES]),
                                            of(tile_f).to_broadcast([P, GROUP, SLOT_TILES]), ALU.is_equal).then_inc(s.m_hot_made, 1)
                    dve.wait_ge(s.m_hot_made, 3 * g + 2)
                    nc.vector.tensor_tensor(tiles, tiles, ids[:, t0 : t0 + GROUP].unsqueeze(2).to_broadcast([P, GROUP, SLOT_TILES]),
                                            ALU.mult).then_inc(s.m_hot_made, 1)
                step(nc.vector.tensor_tensor(passed[:], count_t[:].unsqueeze(2).to_broadcast([P, SLOT_TILES, E]),
                                             begin[:, 1 : E + 1].unsqueeze(1).to_broadcast([P, SLOT_TILES, E]), ALU.is_ge))
                step(nc.vector.tensor_reduce(owner_f[:], passed[:], AX_X, ALU.add))
                nc.vector.tensor_scalar(keep.owner[:], owner_f[:], float(E - 1), None, ALU.min).then_inc(s.m_owners, 1)
                dve.wait_ge(s.m_hot_used, TOP * NT // GROUP)
                nc.vector.tensor_copy(keep.token[:], psum[2][:, 0:SLOT_TILES]).then_inc(s.m_owners, 1)

        s.clear()


def experts_phase(nc, s, c, psum, a, keep, w_gu, w_dn):
    E = EXPERTS
    PER = SLOT_TILES
    ctx = ExitStack()
    with ctx:
        sb = lambda name, shape, dt=F32: ctx.enter_context(nc.sbuf_tensor(f"experts_{name}", shape, dt))
        w_ln, token = sb("w_ln", [P, KD]), sb("token", [P, PER], U32)
        row = sb("row", [P, 4, D])
        hT = sb("hT", [P, 2, KD, P])
        silu, inner = sb("silu", [P, 2, FE]), sb("inner", [P, 2, FE])
        innerT = sb("innerT", [P, 2, len(FE_K), P])
        y = sb("y", [P, 2, D])
        row_here, stored = (s.e_row0, s.e_row1, s.e_row2, s.e_row3), (s.e_stored0, s.e_stored1)

        with nc.Fori(0, SLOT_TILES // PER) as i:
            with nc.Block() as block:

                @block.gpsimd
                def _(pool):
                    pool.wait_ge(s.e_index, 1)
                    for t in range(PER):
                        if t >= 4:
                            pool.wait_ge(s.e_turned, t - 3)
                        pool.indirect_dma_start(row[:, t % 4, :], None, a.rows, bass.IndirectOffsetOnAxis(ap=token[:, t : t + 1], axis=0)
                                                ).then_inc(row_here[t % 4], 16)
                    for m, here in enumerate(row_here):
                        pool.wait_ge(here, 16 * len(range(m, PER, 4)))
                    pool.dma_reset(s.range_of(row_here))

                @block.sync
                def _(sp):
                    sp.dma_start(w_ln[:], a.w_ln.rearrange("(k p) -> p k", p=P), allow_slow_non_contiguous=True).then_inc(s.m_table, 16)
                    for t in range(PER):
                        sp.wait_ge(s.e_result, t + 1)
                        sp.dma_start(a.results[bass.ds((i * PER + t) * P, P), :], y[:, t % 2, :]).then_inc(stored[t % 2], 16)
                    for m, st in enumerate(stored):
                        sp.wait_ge(st, 16 * len(range(m, PER, 2)))

                @block.tensor
                def _(pe):
                    experts = {}

                    def front(t):
                        pe.wait_ge(row_here[t % 4], 16 * (t // 4 + 1))
                        if t >= 1:
                            pe.wait_ge(s.e_hT, t)
                        for k in range(KD):
                            last = nc.tensor.transpose(psum[0][:, k * P : (k + 1) * P], row[:, t % 4, k * P : (k + 1) * P], c.ident[:])
                        last.then_inc(s.e_turned, 1)

                    def gate_up(t):
                        e = pe.value_load(keep.owner[0:1, bass.ds(i * PER + t, 1)], min_val=0, max_val=E - 1)
                        experts[t] = e
                        pe.wait_ge(s.e_hT, t + 1)
                        if t >= 2:
                            pe.wait_ge(s.e_inner, t - 1)
                        for half in range(2):
                            for k in range(KD):
                                rhs = w_gu[:, bass.ds(e, 1), k, half * FE : (half + 1) * FE].rearrange("p a n -> p (a n)")
                                last = nc.tensor.matmul(psum[1 + 2 * (t % 2) + half][:, 0:FE], hT[:, t % 2, k, :], rhs, start=k == 0, stop=k == KD - 1)
                        last.then_inc(s.e_gate_up, 1)

                    def turn(t):
                        pe.wait_ge(s.e_inner, t + 1)
                        if t >= 1:
                            pe.wait_ge(s.e_innerT, t)
                            pe.wait_ge(s.e_innerT01, t)
                        for n, (k0, kn) in enumerate(FE_K):
                            last = nc.tensor.transpose(psum[5][0:kn, n * P : (n + 1) * P], inner[:, t % 2, k0 : k0 + kn], c.ident[:])
                        last.then_inc(s.e_inner_turned, 1)

                    def down(t):
                        pe.wait_ge(s.e_innerT, t + 1)
                        pe.wait_ge(s.e_innerT01, t + 1)
                        if t >= 2:
                            pe.wait_ge(s.e_result, t - 1)
                        for n, (k0, kn) in enumerate(FE_K):
                            rhs = w_dn[0:kn, bass.ds(experts[t], 1), n, :].rearrange("p a n -> p (a n)")
                            last = nc.tensor.matmul(psum[6 + t % 2][:], innerT[0:kn, t % 2, n, :], rhs, start=n == 0, stop=n == len(FE_K) - 1)
                        last.then_inc(s.e_down, 1)

                    front(0)
                    for t in range(PER):
                        if t + 1 < PER:
                            front(t + 1)
                        if t:
                            turn(t - 1)
                        gate_up(t)
                        if t:
                            down(t - 1)
                    turn(PER - 1)
                    down(PER - 1)

                @block.scalar
                def _(act):
                    def result(t):
                        act.wait_ge(s.e_down, t + 1)
                        if t >= 2:
                            act.wait_ge(stored[t % 2], 16 * (t // 2))
                        nc.scalar.activation(y[:, t % 2, :], psum[6 + t % 2][:], ACT.Copy).then_inc(s.e_result, 1)

                    for t in range(PER):
                        act.wait_ge(s.e_gate_up, t + 1)
                        if t >= 2:
                            act.wait_ge(s.e_inner, t - 1)
                        nc.scalar.activation(silu[:, t % 2], psum[1 + 2 * (t % 2)][:, 0:FE], ACT.Silu).then_inc(s.e_silu, 1)
                        if t:
                            result(t - 1)
                    result(PER - 1)

                @block.vector
                def _(dve):
                    def columns(t):
                        dve.wait_ge(s.e_turned, t + 1)
                        if t >= 2:
                            dve.wait_ge(s.e_gate_up, t - 1)
                        nc.vector.tensor_tensor(hT[:, t % 2], psum[0][:].rearrange("p (k n) -> p k n", k=KD),
                                                w_ln[:].unsqueeze(2).to_broadcast([P, KD, P]), ALU.mult).then_inc(s.e_hT, 1)

                    nc.vector.tensor_copy(token[:], keep.token[:, bass.ds(i * PER, PER)]).then_inc(s.e_index, 1)
                    dve.wait_ge(s.m_table, 16)
                    columns(0)
                    for t in range(PER):
                        if t + 1 < PER:
                            columns(t + 1)
                        dve.wait_ge(s.e_silu, t + 1)
                        if t >= 2:
                            dve.wait_ge(s.e_inner_turned, t - 1)
                        nc.vector.tensor_tensor(inner[:, t % 2], silu[:, t % 2], psum[2 + 2 * (t % 2)][:, 0:FE], ALU.mult).then_inc(s.e_inner, 1)
                        dve.wait_ge(s.e_inner_turned, t + 1)
                        if t >= 2:
                            dve.wait_ge(s.e_down, t - 1)
                        nc.vector.tensor_copy(innerT[:, t % 2, 0:2], psum[5][:, 0 : 2 * P].rearrange("p (k n) -> p k n", k=2)).then_inc(s.e_innerT01, 1)
                        kn = FE_K[2][1]
                        nc.vector.tensor_copy(innerT[0:kn, t % 2, 2], psum[5][0:kn, 2 * P : 3 * P]).then_inc(s.e_innerT, 1)

            s.clear()


def shared_phase(nc, s, c, psum, a, keep):
    CHUNK = 2
    BODY = 8
    W = CHUNK * P
    TURN_AT, HALVES_AT, ADD_AT = 8, 9, 8
    ctx = ExitStack()
    with ctx:
        sb = lambda name, shape, dt=F32: ctx.enter_context(nc.sbuf_tensor(f"shared_{name}", shape, dt))
        wg = [sb(f"wg{i}", [P, KD, FS], F32R) for i in range(2)]
        wu = [sb(f"wu{i}", [P, KD, FS], F32R) for i in range(2)]
        wd = [sb(f"wd{i}", [P, KF, D], F32R) for i in range(2)]
        hT = sb("hT", [P, 2, 2, KD, W], F32R)
        inner_p = [sb(f"inner{i}", [P, KF, W], F32R) for i in range(2)]
        silu, prod = sb("silu", [P, 2, W]), sb("prod", [P, 2, W])
        w_ln = sb("w_ln", [P, KD])
        token_rows = sb("token_rows", [P, 3, CHUNK, D])
        row, total, got = (token_rows[:, n] for n in range(3))
        N_NOW = BODY * CHUNK
        slot_now, weight_now, gate_now = sb("slot_now", [P, TOP, N_NOW], U32), sb("weight_now", [P, N_NOW, TOP]), sb("gate_now", [P, N_NOW])

        jobs = []
        for src, dst in ((a.w_gate, wg), (a.w_up, wu)):
            for k in range(KD):
                jobs.append((src[k * P : (k + 1) * P, :].rearrange("(k p) n -> p k n", p=P), dst[0][:, k : k + 1], dst[1][:, k : k + 1]))
        raw = token_rows[:].rearrange("p a t d -> p (a t d)").rearrange("p (two n) -> p two n", two=2)
        split_weights(nc, s, jobs, raw)
        down_cuts = [(k0, min(KF, k0 + CHUNK)) for k0 in range(0, KF, CHUNK)]
        staged = lambda n: (total, got)[n % 2][:, 0 : down_cuts[n][1] - down_cuts[n][0], :]
        raw_loaded = (s.raw_loaded0, s.raw_loaded1)

        with nc.Fori(0, N_TILES // CHUNK // BODY) as loop:
            at = lambda m, ch: m[bass.ds((loop * BODY + ch) * W, W), :].rearrange("(t p) d -> p t d", p=P)
            with nc.Block() as block:

                @block.sync
                def _(sp):
                    sp.dma_start(w_ln[:], a.w_ln.rearrange("(k p) -> p k", p=P), allow_slow_non_contiguous=True).then_inc(s.m_table, 16)
                    for ch in range(BODY + 1):
                        if ch < BODY:
                            if ch:
                                sp.wait_ge(s.s_turned, ch)
                            sp.dma_start(row, at(a.rows, ch)).then_inc(s.s_rows, 16)
                        if ch == 0:
                            for n, (k0, k1) in enumerate(down_cuts):
                                if n >= 2:
                                    sp.wait_ge(s.lo_made, n - 1)
                                sp.dma_start(staged(n), a.w_down[k0 * P : k1 * P, :].rearrange("(k p) n -> p k n", p=P)).then_inc(raw_loaded[n % 2], 16)
                            sp.wait_ge(s.lo_made, len(down_cuts))
                        if ch:
                            sp.wait_ge(s.s_out, CHUNK * ch)
                            sp.dma_start(at(a.out, ch - 1), total).then_inc(s.s_stored, 16)
                            sp.wait_ge(s.s_stored, 16 * ch)
                        if ch < BODY:
                            sp.dma_start(total, at(a.x2, ch)).then_inc(s.s_x2, 16)
                            sp.dma_start(got, at(a.x3, ch)).then_inc(s.s_x3, 16)

                @block.gpsimd
                def _(pool):
                    pool.wait_ge(s.e_index, 3)
                    for ch in range(BODY):
                        pool.wait_ge(s.s_x2, 16 * (ch + 1))
                        pool.wait_ge(s.s_x3, 16 * (ch + 1))
                        for t in range(CHUNK):
                            nc.gpsimd.tensor_tensor(total[:, t, :], total[:, t, :], got[:, t, :], ALU.add).then_inc(s.s_residual, 1)
                        pool.wait_ge(s.s_residual, CHUNK * (ch + 1))
                        for t in range(CHUNK):
                            n = CHUNK * ch + t
                            if t:
                                pool.wait_ge(s.s_added, TOP * n)
                            for j in range(TOP):
                                pool.indirect_dma_start(got[:, j, :], None, a.results,
                                                        bass.IndirectOffsetOnAxis(ap=slot_now[:, j, n : n + 1], axis=0)).then_inc(s.s_got, 16)
                    pool.wait_ge(s.s_got, 16 * TOP * BODY * CHUNK)
                    pool.dma_reset(s.range_of([s.s_got]))

                @block.tensor
                def _(pe):
                    def front(ch):
                        pe.wait_ge(s.s_rows, 16 * (ch + 1))
                        if ch:
                            pe.wait_ge(s.s_lo, KD * ch)
                        for k in range(KD):
                            for t in range(CHUNK):
                                last = nc.tensor.transpose(psum[k][:, t * P : (t + 1) * P], row[:, t, k * P : (k + 1) * P], c.ident[:])
                        last.then_inc(s.s_turned, 1)

                    front(0)
                    up, down = hi_lo_passes(KD), hi_lo_passes(KF)
                    for ch in range(BODY):
                        for f in range(KF):
                            n = ch * KF + f
                            if f == TURN_AT and ch + 1 < BODY:
                                front(ch + 1)
                            if f == 0:
                                pe.wait_ge(s.s_hi, KD * (ch + 1))
                                pe.wait_ge(s.s_lo, KD * (ch + 1))
                            if n >= 2:
                                pe.wait_ge(s.s_inner, n - 1)
                            for half, w in enumerate((wg, wu)):
                                for m, (k, pa, pb) in enumerate(up):
                                    last = nc.tensor.matmul(psum[4 + n % 2][:, half * W : (half + 1) * W], w[pa][:, k, f * P : (f + 1) * P],
                                                            hT[:, ch % 2, pb, k, :], start=m == 0, stop=m == len(up) - 1)
                            last.then_inc(s.s_gate_up, 1)
                        if ch == 0:
                            pe.wait_ge(s.lo_made, len(down_cuts))
                        for t in range(CHUNK):
                            if ch:
                                pe.wait_ge(s.s_out, CHUNK * (ch - 1) + t + 1)
                            for m, (k, pa, pb) in enumerate(down):
                                if t == 0 and (pa, pb) == (0, 0):
                                    pe.wait_ge(s.s_inner_hi, ch * KF + k + 1)
                                    pe.wait_ge(s.s_inner_lo, ch * KF + k + 1)
                                last = nc.tensor.matmul(psum[6 + t][:], inner_p[pa][:, k, t * P : (t + 1) * P], wd[pb][:, k, :],
                                                        start=m == 0, stop=m == len(down) - 1)
                            last.then_inc(s.s_down, 1)

                @block.scalar
                def _(act):
                    def rows_high(ch):
                        act.wait_ge(s.s_turned, ch + 1)
                        if ch >= 2:
                            act.wait_ge(s.s_gate_up, KF * (ch - 1))
                        for k in range(KD):
                            nc.scalar.activation(hT[:, ch % 2, 0, k, :], psum[k][:, 0:W], ACT.Copy, scale=w_ln[:, k : k + 1]).then_inc(s.s_hi, 1)

                    def high(n):
                        act.wait_ge(s.s_inner, n + 1)
                        if n >= KF:
                            act.wait_ge(s.s_down, CHUNK * (n // KF))
                        nc.scalar.activation(inner_p[0][:, n % KF, :], prod[:, n % 2, :], ACT.Copy).then_inc(s.s_inner_hi, 1)

                    act.wait_ge(s.m_table, 16)
                    rows_high(0)
                    for ch in range(BODY):
                        for f in range(KF):
                            n = ch * KF + f
                            act.wait_ge(s.s_gate_up, n + 1)
                            if n >= 2:
                                act.wait_ge(s.s_inner, n - 1)
                            nc.scalar.activation(silu[:, n % 2, :], psum[4 + n % 2][:, 0:W], ACT.Silu).then_inc(s.s_silu, 1)
                            if f:
                                high(n - 1)
                            if ch == 0 and 1 <= f <= len(down_cuts):
                                k0, k1 = down_cuts[f - 1]
                                act.wait_ge(raw_loaded[(f - 1) % 2], 16 * ((f - 1) // 2 + 1))
                                nc.scalar.activation(wd[0][:, k0:k1], staged(f - 1), ACT.Copy).then_inc(s.hi_made, 1)
                            if f == HALVES_AT and ch + 1 < BODY:
                                rows_high(ch + 1)
                        high(ch * KF + KF - 1)

                @block.vector
                def _(dve):
                    def rows_low(ch):
                        for k in range(KD):
                            dve.wait_ge(s.s_hi, KD * ch + k + 1)
                            nc.vector.scalar_tensor_tensor(hT[:, ch % 2, 1, k, :], psum[k][:, 0:W], w_ln[:, k : k + 1],
                                                           hT[:, ch % 2, 0, k, :].bitcast(F32), ALU.mult, ALU.subtract).then_inc(s.s_lo, 1)

                    def low(n):
                        dve.wait_ge(s.s_inner_hi, n + 1)
                        nc.vector.tensor_tensor(inner_p[1][:, n % KF, :], prod[:, n % 2, :], inner_p[0][:, n % KF, :].bitcast(F32),
                                                ALU.subtract).then_inc(s.s_inner_lo, 1)

                    def add_results(ch, t):
                        n = CHUNK * ch + t
                        dve.wait_ge(s.s_residual, CHUNK * (ch + 1))
                        dve.wait_ge(s.s_got, 16 * TOP * (n + 1))
                        for j in range(TOP):
                            nc.vector.scalar_tensor_tensor(total[:, t, :], got[:, j, :], weight_now[:, n, j : j + 1], total[:, t, :],
                                                           ALU.mult, ALU.add).then_inc(s.s_added, 1)
                            dve.wait_ge(s.s_added, TOP * n + j + 1)

                    tiles = bass.ds(loop * BODY * CHUNK, BODY * CHUNK)
                    nc.vector.tensor_copy(slot_now[:], keep.slot[:, :, tiles]).then_inc(s.e_index, 1)
                    nc.vector.tensor_copy(weight_now[:], keep.weight[:, tiles, :]).then_inc(s.e_index, 1)
                    nc.vector.tensor_copy(gate_now[:], keep.gate[:, tiles]).then_inc(s.e_index, 1)
                    dve.wait_ge(s.e_index, 3)
                    dve.wait_ge(s.m_table, 16)
                    rows_low(0)
                    for ch in range(BODY):
                        for f in range(KF):
                            n = ch * KF + f
                            dve.wait_ge(s.s_silu, n + 1)
                            if n >= 2:
                                dve.wait_ge(s.s_inner_hi, n - 1)
                                dve.wait_ge(s.s_inner_lo, n - 1)
                            nc.vector.tensor_tensor(prod[:, n % 2, :], silu[:, n % 2, :], psum[4 + n % 2][:, W : 2 * W], ALU.mult).then_inc(s.s_inner, 1)
                            if f:
                                low(n - 1)
                            if ch == 0 and 1 <= f <= len(down_cuts):
                                k0, k1 = down_cuts[f - 1]
                                dve.wait_ge(s.hi_made, f)
                                nc.vector.tensor_tensor(wd[1][:, k0:k1], staged(f - 1), wd[0][:, k0:k1].bitcast(F32), ALU.subtract).then_inc(s.lo_made, 1)
                            if f == HALVES_AT and ch + 1 < BODY:
                                rows_low(ch + 1)
                            if ADD_AT <= f < ADD_AT + CHUNK:
                                add_results(ch, f - ADD_AT)
                        low(ch * KF + KF - 1)
                        for t in range(CHUNK):
                            n = CHUNK * ch + t
                            dve.wait_ge(s.s_down, n + 1)
                            nc.vector.scalar_tensor_tensor(total[:, t, :], psum[6 + t][:], gate_now[:, n : n + 1], total[:, t, :],
                                                           ALU.mult, ALU.add).then_inc(s.s_out, 1)

            s.clear()


ROPE_HEAD, ROPE_THETA = 32, 1.0e6
AXIAL_HEAD, AXIAL_BASE = 16, 10000.0


def shape_constants():
    inv = (np.float32(1.0) / np.float32(ROPE_THETA) ** (np.arange(0, ROPE_HEAD, 2, dtype=np.float32) / ROPE_HEAD)).astype(np.float32)
    angle = (inv[:, None] * np.arange(S, dtype=np.float32)[None, :]).astype(np.float32)
    cos, sin = np.cos(angle), np.sin(angle)
    half = AXIAL_HEAD // 4
    base = (np.float32(AXIAL_BASE) ** (-np.arange(half, dtype=np.float32) / half)).astype(np.float32)
    freq, sign = np.zeros((2, P), np.float32), np.zeros((P, 1), np.float32)
    for r in range(P):
        axis, rest = divmod(r % AXIAL_HEAD, AXIAL_HEAD // 2)
        freq[axis, r] = base[rest // 2]
        sign[r, 0] = -1.0 if r % 2 == 0 else 1.0
    return {
        "rope_cos": np.tile(cos, (2 * P // ROPE_HEAD, 1)),
        "rope_sin": np.tile(np.concatenate([-sin, sin]), (P // ROPE_HEAD, 1)),
        "axial_freq": freq,
        "axial_sign": sign,
        "expert_number": np.arange(EXPERTS, dtype=np.float32),
        "tile_number": np.arange(SLOT_TILES, dtype=np.float32),
        "place_number": np.arange(P, dtype=np.float32),
        "token_number": np.arange(B * S, dtype=np.float32).reshape(N_TILES, P).T,
    }


def build(nc, i, out):

    rows = lambda t: t.rearrange("b s d -> (b s) d")
    dram = lambda name, shape: nc.dram_tensor(name, shape, F32, kind="Internal").ap()
    x1, x2, x3, h1 = (dram(n, (B * S, D)) for n in ("x1", "x2", "x3", "h1"))
    scratch, values = dram("qk_parts", (B, 2, D, 2, S)), dram("values", (B * S, 2 * D))
    normed, results = dram("normed", (B * S, D)), dram("results", (SLOTS, D))
    ctx = ExitStack()
    with ctx:
        sb = lambda name, shape, dt=F32: ctx.enter_context(nc.sbuf_tensor(name, shape, dt))
        c = Args(ident=sb("ident", [P, P]), pick=sb("pick", [P, HEADS_AT_ONCE]),
                 ones=sb("ones", [P, 32]), identb=sb("identb", [P, P], BF16), maskqb=sb("maskqb", [P, P], BF16), maskkb=sb("maskkb", [P, P], BF16))
        psum = [ctx.enter_context(nc.psum_tensor(f"bank{n}", [P, D], F32)) for n in range(8)]
        s = Signals(nc, SIGNALS + MOE_SIGNALS)
        make_constants(nc, s, c)
        qkv = i["L0_attn_w_qkv"]
        qk = dict(scratch=scratch, body=4, lead=10, norm_step=5)
        first = Args(kind="first", x=rows(i["x"]), wq=(qkv, 0), wk=(qkv, 1), wv=(qkv, 2), wo=(i["L0_attn_w_out"], 0),
                     v=values[:, 0:D], residual=rows(i["x"]), out=x1, **qk)
        projection_phase(nc, s, c, psum, first)
        core_phase(nc, s, c, psum, first)
        wkv = i["L0_xattn_Wkv"]
        cross = Args(kind="cross", x=x1, ctx=rows(i["ctx_1024"]), pos=rows(i["fside_BxSx2_0"]), wq=(i["L0_xattn_Wq"], 0),
                     wk=(wkv, 0), wv=(wkv, 1), wo=(i["L0_xattn_Wout"], 0), bo=i["L0_xattn_bout"], freq=i["axial_freq"],
                     sign=i["axial_sign"], v=values, residual=x1, out=x2, **qk)
        projection_phase(nc, s, c, psum, cross)
        core_phase(nc, s, c, psum, cross)
        rotary = Args(kind="rotary", x=x2, h1=h1, wq=(i["L0_ffn_wq"], 0), wk=(i["L0_ffn_wk"], 0), wv=(i["L0_ffn_wv"], 0),
                      wo=(i["L0_ffn_wo"], 0), bq=i["L0_ffn_bq"], bk=i["L0_ffn_bk"], bv=i["L0_ffn_bv"], w_ln=i["L0_ffn_w_ln1"],
                      cos=i["rope_cos"], sin=i["rope_sin"], v=values[:, 0:D], residual=h1, out=x3, **qk)
        projection_phase(nc, s, c, psum, rotary)
        core_phase(nc, s, c, psum, rotary)
        keep = Args(weight=sb("top_weight", [P, N_TILES, TOP]), slot=sb("slot", [P, TOP, N_TILES], U32), gate=sb("gate", [P, N_TILES]),
                    token=sb("slot_token", [P, SLOT_TILES], U32), owner=sb("tile_owner", [P, SLOT_TILES], I32))
        with (
            nc.sbuf_tensor("experts_gate_up", [P, EXPERTS, KD, 2 * FE], F32) as w_gu,
            nc.sbuf_tensor("experts_down", [P, EXPERTS, len(FE_K), D], F32) as w_dn,
        ):
            router_phase(nc, s, c, psum, Args(
                x3=x3, rows=normed, w_ln=i["L0_ffn_w_ln2"], w_gate=i["L0_ffn_w_gate_e"], w_up=i["L0_ffn_w_up_e"], w_down=i["L0_ffn_w_down_e"],
                w_router=i["L0_ffn_w_router"], w_eg=i["L0_ffn_w_sh_eg"], count8=i["expert_number"], count_t=i["tile_number"],
                count_p=i["place_number"], token_ids=i["token_number"]), keep, w_gu, w_dn)
            experts_phase(nc, s, c, psum, Args(rows=normed, results=results, w_ln=i["L0_ffn_w_ln2"]), keep, w_gu, w_dn)
        shared_phase(nc, s, c, psum, Args(
            x3=x3, x2=x2, rows=normed, results=results, w_ln=i["L0_ffn_w_ln2"], w_gate=i["L0_ffn_w_sh_gate"], w_up=i["L0_ffn_w_sh_up"],
            w_down=i["L0_ffn_w_sh_down"], out=rows(out)), keep)


def kernel(**inputs):
    import concourse.bacc as bacc
    from concourse.bass_utils import run_bass_kernel_spmd

    nc = bacc.Bacc("TRN2", target_bir_lowering=False, num_devices=1)
    arrays, args = {}, {}
    for name, value in [*inputs.items(), *shape_constants().items()]:
        array = np.ascontiguousarray(value)
        arrays[f"in_{name}"] = array
        args[name] = nc.dram_tensor(f"in_{name}", array.shape, mybir.dt.from_np(array.dtype), kind="ExternalInput").ap()
    out = nc.dram_tensor("out_x", (B, S, D), F32, kind="ExternalOutput").ap()
    build(nc, args, out)
    result = run_bass_kernel_spmd(nc, [arrays], core_ids=[0])
    return result.results[0]["out_x"]
```
